# Optimizing a Trainium2 kernel written in Bass

```python
import numpy as np
import jax
import jax.numpy as jnp

def _softmax(x, axis=-1):
    return jax.nn.softmax(x, axis=axis)

def _gelu(x):
    return jax.nn.gelu(x, approximate=True)

def _silu(x):
    return jax.nn.silu(x)

def _sigmoid(x):
    return jax.nn.sigmoid(x)

def _layernorm(x, axis=-1, eps=1e-05):
    m = jnp.mean(x, axis=axis, keepdims=True)
    v = jnp.var(x, axis=axis, keepdims=True)
    return (x - m) / jnp.sqrt(v + eps)

def _scatter_add(tgt, idx, src, axis=0):
    return tgt.at[idx].add(src)

def _segment_sum(src, seg, n):
    return jax.ops.segment_sum(src, seg, n)
kernel_name = 'mk_gnn_preln_d2_gnn_r64_351d27'

def setup_inputs(seed: int=0):
    np.random.seed(seed)
    _w = jnp.asarray

    def _rec_inputs():
        import jax
        import jax.numpy as jnp
        _gk = jax.random.key(seed)
        x = -0.0001006 + 1 * jax.random.normal(jax.random.fold_in(_gk, 1), (50000, 96), jnp.float32)
        src = jax.random.randint(jax.random.fold_in(_gk, 2), (25000,), 0, 50000, jnp.int32)
        dst = jax.random.randint(jax.random.fold_in(_gk, 3), (25000,), 0, 50000, jnp.int32)
        _o = jnp.argsort(dst, stable=True)
        src = src[_o]
        dst = dst[_o]
        edge_attr_96 = -4.21973e-05 + 0.999841 * jax.random.normal(jax.random.fold_in(_gk, 12), (25000, 96), jnp.float32)
        return (x, src, dst, edge_attr_96)
    x, src, dst, edge_attr_96 = _rec_inputs()

    def _L0_gnn_setup():
        import jax, jax.numpy as jnp
        import numpy as np
        N = 50000
        E = 12500
        D = 96
        H = 4
        L = 2
        NEG_SLOPE = 0.2
        EPS_BN = 1e-05

        def _gat_layer(x, src, dst, W, a_src, a_dst, b):
            h = (x @ W).reshape(N, H, D)
            alpha_src = jnp.einsum('nhd,hd->nh', h, a_src)
            alpha_dst = jnp.einsum('nhd,hd->nh', h, a_dst)
            e = jax.nn.leaky_relu(alpha_src[src] + alpha_dst[dst], NEG_SLOPE)
            m = jax.ops.segment_max(e, dst, num_segments=N)
            p = jnp.exp(e - m[dst])
            denom = jax.ops.segment_sum(p, dst, num_segments=N)
            alpha = p / (denom[dst] + 1e-16)
            msg = h[src] * alpha[:, :, None]
            out = jax.ops.segment_sum(msg, dst, num_segments=N)
            return out.mean(axis=1) + b
        key = jax.random.key(seed)
        ks = jax.random.split(key, 8)
        x = jax.random.normal(ks[0], (N, D), dtype=jnp.float32)
        edge_index = jax.random.randint(ks[1], (2, E), 0, N, dtype=jnp.int64)
        W = jax.random.normal(ks[2], (L, D, H * D), dtype=jnp.float32) / np.sqrt(D).astype(np.float32)
        att_src = jax.random.normal(ks[3], (L, H, D), dtype=jnp.float32) * 0.1
        att_dst = jax.random.normal(ks[4], (L, H, D), dtype=jnp.float32) * 0.1
        bias = jnp.zeros((L, D), dtype=jnp.float32)
        gamma = jnp.ones((L, D), dtype=jnp.float32)
        beta = jnp.zeros((L, D), dtype=jnp.float32)
        return dict(x=x, edge_index=edge_index, W=W, att_src=att_src, att_dst=att_dst, bias=bias, gamma=gamma, beta=beta)
    _L0_gnn_all = _L0_gnn_setup()
    _L0_gnn_in = {k: v for k, v in _L0_gnn_all.items() if k in ('W', 'att_src', 'att_dst', 'bias', 'gamma', 'beta')}
    del _L0_gnn_all

    def _L1_gnn_setup():
        import jax, jax.numpy as jnp
        import numpy as np
        N_NODES = 50000
        N_EDGES = 12500
        EMB = 96
        HID = 2 * EMB
        key = jax.random.key(seed)
        ks = jax.random.split(key, 8)
        h = jax.random.normal(ks[0], (N_NODES, EMB), dtype=jnp.float32)
        edge_attr = jax.random.normal(ks[1], (N_EDGES, EMB), dtype=jnp.float32)
        src = jax.random.randint(ks[2], (N_EDGES,), 0, N_NODES, dtype=jnp.int32)
        dst = jax.random.randint(ks[3], (N_EDGES,), 0, N_NODES, dtype=jnp.int32)
        W1 = jax.random.normal(ks[4], (EMB, HID), dtype=jnp.float32) * (1.0 / np.sqrt(EMB))
        b1 = jnp.zeros((HID,), dtype=jnp.float32)
        W2 = jax.random.normal(ks[5], (HID, EMB), dtype=jnp.float32) * (1.0 / np.sqrt(HID))
        b2 = jnp.zeros((EMB,), dtype=jnp.float32)
        eps = jnp.zeros((1,), dtype=jnp.float32)
        return {'h': h, 'edge_attr': edge_attr, 'src': src, 'dst': dst, 'W1': W1, 'b1': b1, 'W2': W2, 'b2': b2, 'eps': eps}
    _L1_gnn_all = _L1_gnn_setup()
    _L1_gnn_in = {k: v for k, v in _L1_gnn_all.items() if k in ('W1', 'b1', 'W2', 'b2', 'eps')}
    del _L1_gnn_all
    return {'x': x, 'src': src, 'dst': dst, 'edge_attr_96': edge_attr_96, 'L0_gnn_W': _L0_gnn_in['W'], 'L0_gnn_att_src': _L0_gnn_in['att_src'], 'L0_gnn_att_dst': _L0_gnn_in['att_dst'], 'L0_gnn_bias': _L0_gnn_in['bias'], 'L0_gnn_gamma': _L0_gnn_in['gamma'], 'L0_gnn_beta': _L0_gnn_in['beta'], 'L1_gnn_W1': _L1_gnn_in['W1'], 'L1_gnn_b1': _L1_gnn_in['b1'], 'L1_gnn_W2': _L1_gnn_in['W2'], 'L1_gnn_b2': _L1_gnn_in['b2'], 'L1_gnn_eps': _L1_gnn_in['eps']}

def reference(x, src, dst, edge_attr_96, L0_gnn_W, L0_gnn_att_src, L0_gnn_att_dst, L0_gnn_bias, L0_gnn_gamma, L0_gnn_beta, L1_gnn_W1, L1_gnn_b1, L1_gnn_W2, L1_gnn_b2, L1_gnn_eps):
    import jax
    import jax.numpy as jnp

    def _L0_gnn_ref(x, edge_index, W, att_src, att_dst, bias, gamma, beta):
        import jax, jax.numpy as jnp
        import numpy as np
        N = 50000
        E = 12500
        D = 96
        H = 4
        L = 2
        NEG_SLOPE = 0.2
        EPS_BN = 1e-05

        def _gat_layer(x, src, dst, W, a_src, a_dst, b):
            h = (x @ W).reshape(N, H, D)
            alpha_src = jnp.einsum('nhd,hd->nh', h, a_src)
            alpha_dst = jnp.einsum('nhd,hd->nh', h, a_dst)
            e = jax.nn.leaky_relu(alpha_src[src] + alpha_dst[dst], NEG_SLOPE)
            m = jax.ops.segment_max(e, dst, num_segments=N)
            p = jnp.exp(e - m[dst])
            denom = jax.ops.segment_sum(p, dst, num_segments=N)
            alpha = p / (denom[dst] + 1e-16)
            msg = h[src] * alpha[:, :, None]
            out = jax.ops.segment_sum(msg, dst, num_segments=N)
            return out.mean(axis=1) + b
        loops = jnp.arange(N, dtype=edge_index.dtype)
        ei = jnp.concatenate([edge_index, jnp.stack([loops, loops])], axis=1)
        src, dst = (ei[0], ei[1])
        for l in range(L):
            x_res = x
            out = _gat_layer(x, src, dst, W[l], att_src[l], att_dst[l], bias[l])
            mu = out.mean(axis=0)
            var = out.var(axis=0)
            out = (out - mu) / jnp.sqrt(var + EPS_BN) * gamma[l] + beta[l]
            x = jax.nn.relu(out) + x_res
        return x

    def _L1_gnn_ref(h, edge_attr, src, dst, W1, b1, W2, b2, eps):
        import jax, jax.numpy as jnp
        import numpy as np
        N_NODES = 50000
        N_EDGES = 12500
        EMB = 96
        HID = 2 * EMB
        m = h[src] + edge_attr
        aggr = jax.ops.segment_sum(m, dst, num_segments=N_NODES)
        hidden = jax.nn.relu(aggr @ W1 + b1)
        mlp_out = hidden @ W2 + b2
        out = (1.0 + eps[0]) * h + mlp_out
        return out
    edge_index = jnp.stack([src, dst])
    h = jnp.maximum(_layernorm(x, axis=-1), 0.0)
    x = x + _L0_gnn_ref(h, edge_index, L0_gnn_W, L0_gnn_att_src, L0_gnn_att_dst, L0_gnn_bias, L0_gnn_gamma, L0_gnn_beta)
    h = jnp.maximum(_layernorm(x, axis=-1), 0.0)
    x = x + _L1_gnn_ref(h, edge_attr_96, src, dst, L1_gnn_W1, L1_gnn_b1, L1_gnn_W2, L1_gnn_b2, L1_gnn_eps)
    return x

_drawn_inputs = setup_inputs


def setup_inputs(seed=0):
    import zlib

    import numpy as np

    out = dict(_drawn_inputs(seed))
    spreads = {'L0_gnn_bias': (0.0, 0.8),
     'L0_gnn_gamma': (1.0, 0.2),
     'L0_gnn_beta': (0.0, 0.1),
     'L1_gnn_b1': (0.0, 0.338),
     'L1_gnn_b2': (0.0, 0.1)}
    factors = {}
    for name, (base, spread) in spreads.items():
        noise = np.random.default_rng([zlib.crc32(name.encode()), seed]).standard_normal(out[name].shape)
        drawn = base * np.exp(spread * noise) if base else spread * noise
        out[name] = jnp.asarray(drawn.astype(out[name].dtype))
    for name, factor in factors.items():
        out[name] = (out[name] * factor).astype(out[name].dtype)
    return out
```

```python
import concourse.bass as bass
import concourse.mybir as mybir
from contextlib import ExitStack

fp32 = mybir.dt.float32
i32 = mybir.dt.int32
ALU = mybir.AluOpType
ACT = mybir.ActivationFunctionType
AX = mybir.AxisListType

N, E, D, H = 50000, 25000, 96, 4
LAYERS = 2
P = 125
CHUNKS = 20
TILES = 20
ET = TILES // 2
NODES_C = N // CHUNKS
EDGES_C = E // CHUNKS
EDGE_TILES = E // P
COLS = TILES * P
TG = 4
GROUPS = TILES // TG
RG = 5
RGROUPS = TILES // RG
LANES = H * CHUNKS
HD = H * D
SLOPE, EPS, TINY = 0.2, 1e-05, 1e-16
BIG = 1.0e30
assert N == CHUNKS * TILES * P and E == CHUNKS * ET * P


def wait(eng, sem, count):
    if isinstance(count, int) and count <= 0:
        return
    eng.wait_ge(sem, count)


def over_chunks(eng, body):
    for c in range(4):
        body(c, c % 2, c // 2)
    with eng.Fori(2, CHUNKS // 2) as i:
        body(i * 2, 0, i)
        body(i * 2 + 1, 1, i)


class Order:

    def __init__(self, eng, sem, per_chunk):
        self.eng, self.sem, self.per_chunk, self.n, self.base = eng, sem, per_chunk, 0, 0

    def chunk(self, c):
        assert self.n in (0, self.per_chunk), self.n
        self.base, self.n = c * self.per_chunk, 0

    def done(self, ins):
        ins.then_inc(self.sem, 1)
        self.n += 1

    def settle(self, back=0):
        wait(self.eng, self.sem, self.base + (self.n - back))


class Line:

    def __init__(self, eng, sem):
        self.eng, self.sem, self.n = eng, sem, 0

    def step(self, ins):
        ins.then_inc(self.sem, 1)
        self.n += 1
        self.eng.wait_ge(self.sem, self.n)


class Stage(ExitStack):

    def __init__(self, nc, tag):
        super().__init__()
        self.nc, self.tag, self.used = nc, tag, []

    def sb(self, name, shape, dt=fp32):
        return self.enter_context(self.nc.sbuf_tensor(f"{self.tag}_{name}", list(shape), dt))

    def pair(self, name, shape, dt=fp32):
        return [self.sb(f"{name}{b}", shape, dt) for b in range(2)]

    def bank(self, name):
        return self.enter_context(self.nc.psum_tensor(f"{self.tag}_{name}", [P, 512], fp32))

    def sem(self, name):
        self.used.append(self.nc.alloc_semaphore(f"{self.tag}_{name}"))
        return self.used[-1]

    def sems(self, name):
        return [self.sem(f"{name}{b}") for b in range(2)]

    def __exit__(self, *what):
        done = super().__exit__(*what)
        if what[0] is None and self.used:
            self.nc.clear_and_free_semaphores(self.used)
            self.nc.all_engine_barrier()
        return done


class Core:
    pass


def bc(ap, shape):
    return ap.broadcast_to(shape)



def prepare(nc, K, A):
    with Stage(nc, "prep") as st:
        sb, pair, bank, sem, sems = st.sb, st.pair, st.bank, st.sem, st.sems
        att = [[sb(f"att_{s}{l}", [D, HD]) for s in ("src", "dst")] for l in range(LAYERS)]
        prod = sb("prod", [D, HD])
        raw = [sb(f"raw_{n}", [100, 2, P], i32) for n in ("src", "dst", "next")]
        rawf = [sb(f"rawf_{n}", [100, 2, P]) for n in ("src", "dst", "next")]
        nextc = sb("nextc", [P, EDGE_TILES])
        gap = sb("gap", [P, EDGE_TILES])
        lane_d = sb("lane_d", [LANES, EDGES_C], i32)
        lane_n = sb("lane_n", [LANES, EDGES_C], i32)
        lane_p = sb("lane_p", [LANES, EDGES_C], i32)
        allf = sb("allf", [LANES, 1])
        allb = sb("allb", [LANES, 1])
        b1p = sb("b1p", [D, 2])
        b1r = sb("b1r", [D, 2, P])
        b2b = sb("b2b", [P, D])
        pick = sb("pick", [P, D])
        cols = bank("cols")
        rows = bank("rows")
        mlp0 = bank("mlp0")
        loads, blanks, made, dve_s, colsem, pe_s, eye_s = (
            sem(n) for n in ("loads", "blanks", "made", "dve_steps", "cols_ready", "pe_rows", "eye_s"))
        flags_ready, sel_ready, b1_ready, w_ready = (sem(n) for n in ("flags_ready", "sel_ready", "b1_ready", "w_ready"))
        cols_used, pool_mask = sem("cols_used"), sem("pool_mask")
        dst1 = K.dst.rearrange("(a n) -> a n", a=1)
        sp_go = sem("sp_go")
        block = st.enter_context(nc.Block())
        n_loads = [0]

        @block.sync
        def _(sp):
            def load(out, in_):
                sp.dma_start(out, in_).then_inc(loads, 16)
                n_loads[0] += 16

            sp.wait_ge(blanks, 3)
            for n, lst in ((0, K.src), (1, K.dst)):
                load(raw[n][:, :, :], lst.rearrange("(a q p) -> q a p", a=2, q=100))
            load(raw[2][:, 0, :], K.dst[1:100 * P + 1].rearrange("(q p) -> q p", q=100))
            load(raw[2][0:99, 1, :], K.dst[100 * P + 1:199 * P + 1].rearrange("(q p) -> q p", q=99))
            load(raw[2][99:100, 1, 0:P - 1], dst1[:, 199 * P + 1:E])
            last = CHUNKS - 1
            for h in range(H):
                o = h * CHUNKS
                load(lane_d[o:o + CHUNKS, :], K.dst.rearrange("(b e) -> b e", b=CHUNKS))
                load(lane_n[o:o + last, :], K.dst[1:1 + last * EDGES_C].rearrange("(b e) -> b e", b=last))
                load(lane_n[o + last:o + CHUNKS, 0:EDGES_C - 1], dst1[:, last * EDGES_C + 1:E])
                load(lane_p[o:o + 1, 1:EDGES_C], dst1[:, 0:EDGES_C - 1])
                load(lane_p[o + 1:o + CHUNKS, :],
                     K.dst[EDGES_C - 1:E - 1].rearrange("(b e) -> b e", b=last))
            for l in range(LAYERS):
                load(K.w[l][:, :], A["L0_gnn_W"][l, :, :])
                for s, name in enumerate(("L0_gnn_att_src", "L0_gnn_att_dst")):
                    load(att[l][s][:, :], bc(A[name][l:l + 1, :, :].rearrange("l h d -> l (h d)"), [D, HD]))
                load(K.bias[l][:, :], A["L0_gnn_bias"][l:l + 1, :].rearrange("l d -> d l"))
                load(K.gamma[l][:, :], A["L0_gnn_gamma"][l:l + 1, :].rearrange("l d -> d l"))
                load(K.beta[l][:, :], A["L0_gnn_beta"][l:l + 1, :].rearrange("l d -> d l"))
            load(K.w1[:, :], A["L1_gnn_W1"])
            load(K.w2[:, :, :], A["L1_gnn_W2"].rearrange("(k p) n -> p k n", k=2))
            for k in range(2):
                load(K.b1[:, k:k + 1], A["L1_gnn_b1"][k * D:(k + 1) * D].rearrange("(p a) -> p a", a=1))
            load(b2b[:, :], bc(A["L1_gnn_b2"].rearrange("(a n) -> a n", a=1), [P, D]))
            load(K.eps1[:, :], bc(A["L1_gnn_eps"].rearrange("(a n) -> a n", a=1), [P, 1]))
            sp.wait_ge(loads, n_loads[0])

        @block.gpsimd
        def _(pool):
            pool.memset(K.eye[:, :], 0.0).then_inc(eye_s, 1)
            pool.memset(pick[:, :], 1.0).then_inc(eye_s, 1)
            pool.wait_ge(eye_s, 2)
            pool.affine_select(out=K.eye[:, :], in_=K.eye[:, :], compare_op=ALU.not_equal, fill=1.0, base=0,
                               pattern=[[-1, P]], channel_multiplier=1).then_inc(sel_ready, 1)
            pool.affine_select(out=pick[:, :], in_=pick[:, :], compare_op=ALU.is_equal, fill=0.0, base=1 - P,
                               pattern=[[0, D]], channel_multiplier=1).then_inc(sel_ready, 1)
            pool.wait_ge(pool_mask, 1)
            pool.affine_select(out=K.prev_last[:, :], in_=K.prev_last[:, :], compare_op=ALU.is_equal,
                               fill=-1.0, base=1 - P, pattern=[[0, EDGE_TILES]],
                               channel_multiplier=1).then_inc(sel_ready, 1)
            pool.wait_ge(sel_ready, 3)

        @block.vector
        def _(dve):
            go = Line(dve, dve_s)
            nc.vector.memset(raw[2][:, :, :], -1).then_inc(blanks, 1)
            nc.vector.memset(lane_n[:, :], -1).then_inc(blanks, 1)
            nc.vector.memset(lane_p[:, :], -1).then_inc(blanks, 1)
            nc.vector.memset(K.eps[:, :], EPS).then_inc(made, 1)
            nc.vector.memset(K.ones[:, :], 1.0).then_inc(made, 1)
            nc.vector.memset(K.prev_last[:, :], -1.0).then_inc(made, 1)
            nc.vector.memset(K.ones1[:, :], 1.0).then_inc(made, 1)
            dve.wait_ge(made, 4)
            dve.wait_ge(loads, n_loads[0])
            for n in range(3):
                nc.vector.tensor_copy(rawf[n][:, :, :], raw[n][:, :, :]).then_inc(flags_ready, 1)
            go.step(nc.vector.tensor_tensor(K.cont_f[:, :], lane_d[:, :], lane_p[:, :], ALU.is_equal))
            go.step(nc.vector.tensor_tensor(K.cont_b[:, :], lane_d[:, :], lane_n[:, :], ALU.is_equal))
            go.step(nc.vector.tensor_scalar(K.tail[:, :], K.cont_b[:, :], -1.0, 1.0, ALU.mult, ALU.add))
            go.step(nc.vector.tensor_scalar(K.pen_f[:, :], K.cont_f[:, :], BIG, -BIG, ALU.mult, ALU.add))
            go.step(nc.vector.tensor_reduce(allf[:, :], K.cont_f[:, :], AX.X, ALU.min))
            nc.vector.tensor_reduce(allb[:, :], K.cont_b[:, :], AX.X, ALU.min).then_inc(flags_ready, 1)
            dve.wait_ge(pe_s, 1)
            go.step(nc.vector.tensor_copy(K.all_f[:, :], rows[0:1, 0:LANES]))
            go.step(nc.vector.tensor_copy(K.all_b[:, :], rows[0:1, LANES:2 * LANES]))
            go.step(nc.vector.tensor_scalar(K.all_pen[:, :], K.all_f[:, :], BIG, -BIG, ALU.mult, ALU.add))
            dve.wait_ge(colsem, 1)
            go.step(nc.vector.tensor_copy(K.src_i[:, :], cols[:, 0:200]))
            go.step(nc.vector.tensor_copy(K.dst_f[:, :], cols[:, 200:400]))
            nc.vector.tensor_copy(nextc[:, :], rows[:, 200:400]).then_inc(cols_used, 1)
            dve.wait_ge(cols_used, 1)
            go.step(nc.vector.tensor_copy(K.dst_i[:, :], K.dst_f[:, :]))
            go.step(nc.vector.tensor_tensor(K.tail_c[:, :], K.dst_f[:, :], nextc[:, :], ALU.not_equal))
            go.step(nc.vector.tensor_scalar(K.ntail_c[:, :], K.tail_c[:, :], -1.0, None, ALU.mult))
            go.step(nc.vector.tensor_scalar(gap[:, :], K.dst_f[:, :], -float(N), None, ALU.add))
            go.step(nc.vector.tensor_tensor(gap[:, :], gap[:, :], K.tail_c[:, :], ALU.mult))
            go.step(nc.vector.tensor_scalar(K.tail_i[:, :], gap[:, :], float(N), None, ALU.add))
            nc.vector.tensor_copy(K.prev_last[:, 1:EDGE_TILES], K.dst_f[:, 0:EDGE_TILES - 1]).then_inc(pool_mask, 1)
            dve.wait_ge(pe_s, 2)
            go.step(nc.vector.memset(K.prev_b[:, :], -1.0))
            go.step(nc.vector.tensor_copy(K.prev_b[:, 1:EDGE_TILES], mlp0[0:D, 200:399]))
            for l in range(LAYERS):
                for k, s in ((0, 0), (1, 1), (2, 0)):
                    go.step(nc.vector.tensor_tensor(prod[:, :], K.w[l][:, :], att[l][s][:, :], ALU.mult))
                    go.step(nc.vector.tensor_reduce(K.w_att[l][:, k * H:(k + 1) * H],
                                                    prod[:, :].rearrange("p (h d) -> p h d", h=H), AX.X, ALU.add))
                go.step(nc.vector.tensor_scalar(K.w[l][:, :], K.w[l][:, :], 1.0 / H, None, ALU.mult))
                go.step(nc.vector.tensor_reduce(K.w_bar[l][:, :], K.w[l][:, :].rearrange("p (h d) -> p d h", h=H),
                                                AX.X, ALU.add))
            go.step(nc.vector.tensor_scalar(K.eps1[:, :], K.eps1[:, :], 1.0, None, ALU.add))
            go.step(nc.vector.tensor_scalar(b1p[:, :], K.b1[:, :], 0.0, None, ALU.max))
            nc.vector.tensor_copy(b1r[:, :, :], bc(b1p[:, :].unsqueeze(2), [D, 2, P])).then_inc(b1_ready, 1)
            dve.wait_ge(w_ready, 1)
            go.step(nc.vector.tensor_tensor(K.mlp_empty[:, :], mlp0[:, 0:D], b2b[:, :], ALU.add))
            for r in range(RG):
                go.step(nc.vector.tensor_copy(K.b2_row[:, r * D:(r + 1) * D], b2b[0:1, :]))

        @block.tensor
        def _(pe):
            pe.wait_ge(sel_ready, 2)
            pe.wait_ge(flags_ready, 4)
            nc.tensor.transpose(rows[0:1, 0:LANES], allf[:, :], K.eye[0:LANES, 0:LANES])
            for a in range(2):
                nc.tensor.transpose(rows[:, 200 + 100 * a:300 + 100 * a], rawf[2][:, a, :], K.eye[0:100, 0:100])
            nc.tensor.transpose(rows[0:1, LANES:2 * LANES], allb[:, :], K.eye[0:LANES, 0:LANES]).then_inc(pe_s, 1)
            for n in range(2):
                for a in range(2):
                    o = 200 * n + 100 * a
                    last = nc.tensor.transpose(cols[:, o:o + 100], rawf[n][:, a, :], K.eye[0:100, 0:100])
            last.then_inc(colsem, 1)
            pe.wait_ge(pool_mask, 1)
            nc.tensor.matmul(mlp0[0:D, 200:400], lhsT=pick[:, :], rhs=K.dst_f[:, :], start=True, stop=True).then_inc(pe_s, 1)
            pe.wait_ge(b1_ready, 1)
            for k in range(2):
                last = nc.tensor.matmul(mlp0[:, 0:D], lhsT=b1r[:, k, :], rhs=K.w2[:, k, :],
                                        start=(k == 0), stop=(k == 1))
            last.then_inc(w_ready, 1)


def dma_rows(eng, out, in_, sem):
    eng.dma_start(out[0:112], in_[0:112]).then_inc(sem, 16)
    eng.dma_start(out[112:P], in_[112:P]).then_inc(sem, 16)



def first_layer(nc, K, A):
    x_nodes = A["x"].rearrange("(c p j) f -> c p (j f)", c=CHUNKS, p=P)
    out0_nodes = K.out[0].rearrange("(c p j) f -> c p (j f)", c=CHUNKS, p=P)
    with Stage(nc, "first") as st:
        sb, pair, bank, sem, sems = st.sb, st.pair, st.bank, st.sem, st.sems
        NODE, EDGE = 0, 1
        x_in = pair("x_in", [P, TILES, D])
        pairs = pair("pairs", [P, TILES, D])
        src_of = [x_in, pairs]
        norm = [pair("norm_node", [P, TILES, D]), pair("norm_edge", [P, TILES, D])]
        normT = [pair("normT_node", [D, COLS]), pair("normT_edge", [D, COLS])]
        square = [sb(f"square{k}", [P, TILES, D]) for k in range(2)]
        total = [sb(f"total{k}", [P, TILES]) for k in range(2)]
        sqsum = [sb(f"sqsum{k}", [P, TILES]) for k in range(2)]
        dev = [sb(f"dev{k}", [P, TILES]) for k in range(2)]
        rdev = [sb(f"rdev{k}", [P, TILES]) for k in range(2)]
        out_row = pair("out_row", [P, TILES * D])
        index = pair("index", [P, TILES], i32)
        turned = [bank("turned0"), bank("turned1")]
        rows = [bank("rows0"), bank("rows1")]
        outT = [bank("outT0"), bank("outT1")]
        logit = [bank("logit0"), bank("logit1")]

        x_loaded, gathered = sems("x_loaded"), sems("gathered")
        raw_stored, hT_stored, rows_stored, gT_stored = (sems(n) for n in ("raw_stored", "hT_stored", "rows_stored", "gT_stored"))
        centred, squared, summed, rooted, normed = (
            [sem(f"{n}{k}") for k in range(2)] for n in ("centred", "squared", "summed", "rooted", "normed"))
        steps, pool_go, index_ready = sem("dve_steps"), sem("pool_go"), sem("index_ready")
        t_done, t_evac, rows_done, rows_evac = (sem(n) for n in ("t_done", "t_evac", "rows_done", "rows_evac"))
        outT_done, outT_used, logit_done, logit_evac = (sem(n) for n in ("outT_done", "outT_used", "logit_done", "logit_evac"))
        sp_go = sem("sp_go")
        block = st.enter_context(nc.Block())

        def bank_no(c, kind, g):
            return c * (2 * GROUPS) + (kind * GROUPS + g)

        @block.sync
        def _(sp):
            def store(c, b, i):
                wait(sp, gathered[b], i * (16 * TILES) + 16 * TILES)
                sp.sem_inc(sp_go, 1)
                dma_rows(sp, K.raw_pairs[c], pairs[b][:, :, :].rearrange("p j f -> p (j f)"), raw_stored[b])
                wait(sp, t_evac, bank_no(c, NODE, GROUPS))
                sp.sem_inc(sp_go, 1)
                sp.dma_start(K.h0T[c], normT[NODE][b][:, :]).then_inc(hT_stored[b], 16)
                wait(sp, rows_evac, c * RGROUPS + RGROUPS)
                sp.sem_inc(sp_go, 1)
                dma_rows(sp, out0_nodes[c], out_row[b][:, :], rows_stored[b])
                wait(sp, t_evac, bank_no(c, EDGE, GROUPS))
                sp.sem_inc(sp_go, 1)
                sp.dma_start(K.pairT[0][c], normT[EDGE][b][:, :]).then_inc(gT_stored[b], 16)

            def body(c, b, i):
                wait(sp, centred[NODE], c - 1)
                sp.sem_inc(sp_go, 1)
                dma_rows(sp, x_in[b][:, :, :].rearrange("p j f -> p (j f)"), x_nodes[c], x_loaded[b])
                if not (isinstance(c, int) and c == 0):
                    store(c - 1, 1 - b, i if b else i - 1)

            over_chunks(sp, body)
            store(CHUNKS - 1, 1, CHUNKS // 2 - 1)
            for b in range(2):
                for s, per in ((raw_stored, 32), (hT_stored, 16), (rows_stored, 32), (gT_stored, 16)):
                    sp.wait_ge(s[b], per * CHUNKS // 2)

        @block.gpsimd
        def _(pool):
            def body(c, b, i):
                wait(pool, centred[EDGE], c - 1)
                wait(pool, raw_stored[b], i * 32)
                wait(pool, gathered[b], i * (16 * TILES))
                pool.sem_inc(pool_go, 1)
                pool.tensor_copy(index[b][:, 0:ET], K.src_i[:, bass.ds(c * ET, ET)]).then_inc(index_ready, 1)
                pool.tensor_copy(index[b][:, ET:TILES], K.dst_i[:, bass.ds(c * ET, ET)]).then_inc(index_ready, 1)
                pool.wait_ge(index_ready, c * 2 + 2)
                pool.sem_inc(pool_go, 1)
                for j in range(TILES):
                    pool.indirect_dma_start(pairs[b][:, j, :], None, A["x"],
                                            bass.IndirectOffsetOnAxis(index[b][:, j:j + 1], 0)).then_inc(gathered[b], 16)

            over_chunks(pool, body)

        @block.vector
        def _(dve):
            order = Order(dve, steps, 4)

            def centre(kind, c, b, i):
                if kind == NODE:
                    wait(dve, x_loaded[b], i * 32 + 32)
                else:
                    wait(dve, gathered[b], i * (16 * TILES) + 16 * TILES)
                rows_in, rows_out = src_of[kind][b], norm[kind][b]
                order.done(nc.vector.tensor_reduce(total[kind][:, :], rows_in[:, :, :], AX.X, ALU.add))
                order.settle()
                wait(dve, t_done, bank_no(c - 2, kind, GROUPS))
                nc.vector.scalar_tensor_tensor(rows_out[:, :, :], bc(total[kind][:, :].unsqueeze(2), [P, TILES, D]),
                                               -1.0 / D, rows_in[:, :, :], ALU.mult, ALU.add).then_inc(centred[kind], 1)

            def normalise(kind, c, b):
                wait(dve, squared[kind], c + 1)
                nc.vector.tensor_reduce(sqsum[kind][:, :], square[kind][:, :, :], AX.X, ALU.add).then_inc(summed[kind], 1)
                wait(dve, rooted[kind], c + 1)
                order.done(nc.vector.reciprocal(rdev[kind][:, :], dev[kind][:, :]))
                order.settle()
                rows_out = norm[kind][b]
                nc.vector.scalar_tensor_tensor(rows_out[:, :, :], rows_out[:, :, :], 0.0,
                                               bc(rdev[kind][:, :].unsqueeze(2), [P, TILES, D]),
                                               ALU.max, ALU.mult).then_inc(normed[kind], 1)

            def behind(c, b):
                normalise(EDGE, c, b)
                for g in range(GROUPS):
                    wait(dve, outT_done, c * GROUPS + (g + 1))
                    nc.vector.bn_stats(K.stats[0][:, bass.ds(c * GROUPS + g, 1), :].rearrange("p a s -> p (a s)"),
                                       outT[(b + g) % 2][0:D, 0:TG * P]).then_inc(outT_used, 1)

            def body(c, b, i):
                order.chunk(c)
                centre(NODE, c, b, i)
                if not (isinstance(c, int) and c == 0):
                    behind(c - 1, 1 - b)
                else:
                    order.done(nc.vector.engine_nop())
                centre(EDGE, c, b, i)
                normalise(NODE, c, b)

            over_chunks(dve, body)
            order.chunk(CHUNKS)
            behind(CHUNKS - 1, 1)

        @block.scalar
        def _(act):
            def squares(kind, c, b):
                wait(act, centred[kind], c + 1)
                wait(act, summed[kind], c)
                nc.scalar.activation(square[kind][:, :, :], norm[kind][b][:, :, :], ACT.Square).then_inc(squared[kind], 1)

            def root(kind, c):
                wait(act, summed[kind], c + 1)
                nc.scalar.activation(dev[kind][:, :], sqsum[kind][:, :], ACT.Sqrt, bias=K.eps[:, :],
                                     scale=1.0 / D).then_inc(rooted[kind], 1)

            def evacuate(kind, c, b, i):
                stored = (hT_stored, gT_stored)[kind]
                wait(act, stored[b], i * 16)
                if kind == NODE:
                    wait(act, outT_done, c * GROUPS - GROUPS)
                else:
                    wait(act, logit_done, c - 1)
                for g in range(GROUPS):
                    wait(act, t_done, bank_no(c, kind, g + 1))
                    nc.scalar.copy(normT[kind][b][:, g * TG * P:(g + 1) * TG * P],
                                   turned[(kind * GROUPS + g) % 2][0:D, 0:TG * P]).then_inc(t_evac, 1)

            def edge_back(c, b, i):
                root(EDGE, c)
                evacuate(EDGE, c, b, i)
                wait(act, logit_done, c + 1)
                nc.scalar.copy(K.logits[:, :, bass.ds(c * ET, ET)],
                               logit[b][0:P, 0:3 * H * ET].rearrange("p (k j) -> p k j", j=ET)).then_inc(logit_evac, 1)

            def body(c, b, i):
                squares(NODE, c, b)
                if not (isinstance(c, int) and c == 0):
                    edge_back(c - 1, 1 - b, i if b else i - 1)
                squares(EDGE, c, b)
                root(NODE, c)
                evacuate(NODE, c, b, i)
                wait(act, rows_stored[b], i * 32)
                for k in range(RGROUPS):
                    wait(act, rows_done, c * RGROUPS + (k + 1))
                    nc.scalar.copy(out_row[b][:, k * RG * D:(k + 1) * RG * D], rows[k % 2][0:P, 0:RG * D]).then_inc(rows_evac, 1)

            over_chunks(act, body)
            edge_back(CHUNKS - 1, 1, CHUNKS // 2 - 1)

        @block.tensor
        def _(pe):
            def turn(kind, c, b):
                wait(pe, normed[kind], c + 1)
                for g in range(GROUPS):
                    wait(pe, t_evac, bank_no(c, kind, g) - 1)
                    for k in range(TG):
                        last = nc.tensor.transpose(turned[(kind * GROUPS + g) % 2][0:D, k * P:(k + 1) * P],
                                                   norm[kind][b][:, g * TG + k, :], K.eye[:, :])
                    last.then_inc(t_done, 1)

            def edge_back(c, b):
                for g in range(GROUPS):
                    wait(pe, outT_used, c * GROUPS + (g - 1))
                    nc.tensor.matmul(outT[(b + g) % 2][0:D, 0:TG * P], lhsT=K.w_bar[0][:, :],
                                     rhs=normT[NODE][b][:, g * TG * P:(g + 1) * TG * P],
                                     start=True, stop=True).then_inc(outT_done, 1)
                turn(EDGE, c, b)
                edge_logits(nc, K, pe, 0, c, b, normT[EDGE][b], logit[b], t_evac, bank_no(c, EDGE, GROUPS),
                            logit_evac, logit_done)

            def body(c, b, i):
                if not (isinstance(c, int) and c == 0):
                    edge_back(c - 1, 1 - b)
                turn(NODE, c, b)
                dense_rows(nc, K, pe, 0, c, b, normT[NODE][b], rows, t_evac, lambda g: bank_no(c, NODE, g + 1),
                           rows_evac, rows_done)

            over_chunks(pe, body)
            edge_back(CHUNKS - 1, 1)


def dense_rows(nc, K, pe, l, c, b, xT, rows, ready, ready_count, rows_evac, rows_done):
    seen = -1
    for k in range(RGROUPS):
        need = ((k + 1) * RG - 1) // TG
        if need > seen:
            wait(pe, ready, ready_count(need))
            seen = need
        wait(pe, rows_evac, c * RGROUPS + (k - 1))
        for r in range(RG):
            j = k * RG + r
            last = nc.tensor.matmul(rows[k % 2][0:P, r * D:(r + 1) * D], lhsT=xT[:, j * P:(j + 1) * P],
                                    rhs=K.w_bar[l][:, :], start=True, stop=True)
        last.then_inc(rows_done, 1)


def edge_logits(nc, K, pe, l, c, b, xT, out, ready, ready_count, logit_evac, logit_done):
    wait(pe, ready, ready_count)
    wait(pe, logit_evac, c - 1)
    cols = out[0:P, 0:3 * H * ET].rearrange("p (k j) -> p k j", j=ET)
    for j in range(ET):
        nc.tensor.matmul(cols[:, 0:H, j], lhsT=xT[:, j * P:(j + 1) * P], rhs=K.w_att[l][:, 0:H], start=True, stop=True)
        last = nc.tensor.matmul(cols[:, H:3 * H, j], lhsT=xT[:, (ET + j) * P:(ET + j + 1) * P],
                                rhs=K.w_att[l][:, H:3 * H], start=True, stop=True)
    last.then_inc(logit_done, 1)



def edge_softmax(nc, K, l):
    with Stage(nc, f"softmax{l}") as st:
        sb, pair, bank, sem, sems = st.sb, st.pair, st.bank, st.sem, st.sems
        LE = (LANES, EDGES_C)
        lane = [sb(f"lane{k}", LE) for k in range(3)]
        edge, own, work, scan, run_max, run_sum = (sb(n, LE) for n in ("edge", "own", "work", "scan", "run_max", "run_sum"))
        prob, own_prob = sb("prob", LE), sb("own_prob", LE)
        ends, links, start = sb("ends", (1, LANES)), sb("links", (1, LANES + 1)), sb("start", (LANES, 1))
        turned = [bank("turned0"), bank("turned1")]
        link_row, link_col = bank("link_row"), bank("link_col")
        turn_done, turn_used, steps = sem("turn_done"), sem("turn_used"), sem("dve_steps")
        ends_ready, row_done, links_ready, col_done = (sem(n) for n in ("ends_ready", "row_done", "links_ready", "col_done"))
        shifted, probs, alpha_ready, back_done, back_used = (sem(n) for n in ("shifted", "probs", "alpha_ready", "back_done", "back_used"))
        sp_go = sem("sp_go")
        block = st.enter_context(nc.Block())
        FOUR = (4, 4, 2)
        SCANS = 5

        @block.tensor
        def _(pe):
            n = 0
            for k in range(3):
                j = 0
                for cnt in FOUR:
                    wait(pe, turn_used, n - 1)
                    for q in range(cnt):
                        last = nc.tensor.transpose(turned[n % 2][0:LANES, q * P:(q + 1) * P],
                                                   K.logits[:, k * H:(k + 1) * H, :].rearrange(
                                                       "p h (b j) -> p (h b) j", j=ET)[:, :, j + q], K.eye[:, :])
                    last.then_inc(turn_done, 1)
                    j += cnt
                    n += 1
            for s in range(SCANS):
                forward = s in (1, 3)
                pe.wait_ge(ends_ready, s + 1)
                at = EDGES_C - 1 if forward else 0
                nc.tensor.transpose(link_row[0:1, 0:LANES], scan[:, at:at + 1], K.eye[0:LANES, 0:LANES]).then_inc(row_done, 1)
                pe.wait_ge(links_ready, s + 1)
                off = 0 if forward else 1
                nc.tensor.transpose(link_col[0:LANES, 0:1], links[0:1, off:off + LANES], K.eye[0:1, 0:1]).then_inc(col_done, 1)
            pe.wait_ge(alpha_ready, 1)
            for k, lanes in enumerate((prob, own_prob)):
                for half in range(2):
                    m = 2 * k + half
                    wait(pe, back_used, m - 1)
                    for q in range(5):
                        j = half * 5 + q
                        last = nc.tensor.transpose((link_row, link_col)[m % 2][0:P, q * LANES:(q + 1) * LANES],
                                                   lanes[:, j * P:(j + 1) * P], K.eye[0:LANES, 0:LANES])
                    last.then_inc(back_done, 1)

        @block.scalar
        def _(act):
            n = 0
            for k in range(3):
                j = 0
                for cnt in FOUR:
                    act.wait_ge(turn_done, n + 1)
                    nc.scalar.copy(lane[k][:, j * P:(j + cnt) * P], turned[n % 2][0:LANES, 0:cnt * P]).then_inc(turn_used, 1)
                    j += cnt
                    n += 1
            for m, (out, in_) in enumerate(((prob, edge), (own_prob, own))):
                act.wait_ge(shifted, m + 1)
                nc.scalar.activation(out[:, :], in_[:, :], ACT.Exp).then_inc(probs, 1)
            for m in range(4):
                act.wait_ge(back_done, m + 1)
                half = m % 2
                dst = K.alpha[:, m // 2, :, :].rearrange("p l j -> p j l")[:, half * 5:half * 5 + 5, :]
                nc.scalar.copy(dst, (link_row, link_col)[m % 2][0:P, 0:5 * LANES].rearrange("p (j l) -> p j l", j=5)).then_inc(back_used, 1)

        @block.vector
        def _(dve):
            go = Line(dve, steps)
            scans = [0]

            def run_scan(out, keep, data, block_keep, forward, op0, op1, none):
                r = slice(None) if forward else slice(None, None, -1)
                init = none
                for again in range(2):
                    ins = nc.vector.tensor_tensor_scan(out[:, r], keep[:, r], data[:, r], init, op0, op1)
                    if again:
                        go.step(ins)
                        break
                    ins.then_inc(ends_ready, 1)
                    scans[0] += 1
                    n = scans[0]
                    dve.wait_ge(row_done, n)
                    go.step(nc.vector.tensor_copy(ends[:, :], link_row[0:1, 0:LANES]))
                    edge_at, body = (0, slice(1, LANES + 1)) if forward else (LANES, slice(0, LANES))
                    go.step(nc.vector.memset(links[0:1, edge_at:edge_at + 1], none))
                    nc.vector.tensor_tensor_scan(links[0:1, body][:, r], block_keep[0:1, r], ends[0:1, r], none,
                                                 op0, op1).then_inc(links_ready, 1)
                    dve.wait_ge(col_done, n)
                    go.step(nc.vector.tensor_copy(start[:, :], link_col[0:LANES, 0:1]))
                    init = start[:, 0:1]

            def from_tails(out, data):
                go.step(nc.vector.tensor_tensor(work[:, :], K.tail[:, :], data[:, :], ALU.mult))
                run_scan(scan, K.cont_b, work, K.all_b, False, ALU.mult, ALU.add, 0.0)

            dve.wait_ge(turn_used, 9)
            from_tails(scan, lane[1])
            for out, part in ((edge, 0), (own, 2)):
                go.step(nc.vector.tensor_tensor(work[:, :], lane[part][:, :], scan[:, :], ALU.add))
                go.step(nc.vector.scalar_tensor_tensor(out[:, :], work[:, :], SLOPE, work[:, :], ALU.mult, ALU.max))
            go.step(nc.vector.scalar_tensor_tensor(own[:, :], K.cont_b[:, :], -BIG, own[:, :], ALU.mult, ALU.add))
            go.step(nc.vector.tensor_tensor(run_max[:, :], edge[:, :], own[:, :], ALU.max))
            run_scan(scan, K.pen_f, run_max, K.all_pen, True, ALU.add, ALU.max, -BIG)
            from_tails(scan, scan)
            nc.vector.tensor_tensor(edge[:, :], edge[:, :], scan[:, :], ALU.subtract).then_inc(shifted, 1)
            nc.vector.tensor_tensor(own[:, :], own[:, :], scan[:, :], ALU.subtract).then_inc(shifted, 1)
            dve.wait_ge(probs, 2)
            go.step(nc.vector.tensor_tensor(run_sum[:, :], prob[:, :], own_prob[:, :], ALU.add))
            run_scan(scan, K.cont_f, run_sum, K.all_f, True, ALU.mult, ALU.add, 0.0)
            from_tails(scan, scan)
            go.step(nc.vector.tensor_scalar(scan[:, :], scan[:, :], TINY, None, ALU.add))
            go.step(nc.vector.reciprocal(work[:, :], scan[:, :]))
            go.step(nc.vector.tensor_tensor(prob[:, :], prob[:, :], work[:, :], ALU.mult))
            nc.vector.tensor_tensor(own_prob[:, :], own_prob[:, :], work[:, :], ALU.mult).then_inc(alpha_ready, 1)



def aggregate(nc, K, l):
    V = H * D
    with Stage(nc, f"aggr{l}") as st:
        sb, pair, bank, sem, sems = st.sb, st.pair, st.bank, st.sem, st.sems
        xT = pair("xT", [D, COLS])
        dst_row = pair("dst_row", [P, ET, P], i32)
        same = pair("same", [P, ET, P])
        carry = pair("carry", [P, ET, P])
        alpha = pair("alpha_c", [P, 2 * H, ET])
        tails = pair("tails", [P, 2, ET])
        index = pair("index", [P, ET], i32)
        part = pair("part", [P, 2, D])
        out_row = pair("out_row", [P, ET, D])
        base = pair("base", [P, ET, D])
        out_sq, base_sq = sb("out_sq", [P, ET, D]), sb("base_sq", [P, ET, D])
        src_v = [bank("src_v0"), bank("src_v1")]
        dst_v = [bank("dst_v0"), bank("dst_v1")]
        sums = [bank("sums0"), bank("sums1")]
        base_p, stat = bank("base_p"), bank("stat")

        loaded, row_loaded, stored, scattered = (sems(n) for n in ("loaded", "row_loaded", "stored", "scattered"))
        masks_ready, src_done, dst_done, part_ready, sums_done, out_evac = (
            sem(n) for n in ("masks_ready", "src_done", "dst_done", "part_ready", "sums_done", "out_evac"))
        base_done, base_evac, sq_ready, stat_done, stat_used = (
            sem(n) for n in ("base_done", "base_evac", "sq_ready", "stat_done", "stat_used"))
        steps, pool_go, index_ready, blank = (sem(n) for n in ("dve_steps", "pool_go", "index_ready", "blank"))
        sp_go = sem("sp_go")
        block = st.enter_context(nc.Block())

        @block.sync
        def _(sp):
            def store(c, b):
                wait(sp, out_evac, c * ET + ET)
                sp.sem_inc(sp_go, 1)
                dma_rows(sp, K.out_pairs[l][c], out_row[b][:, :, :].rearrange("p j f -> p (j f)"), stored[b])

            def body(c, b, i):
                wait(sp, part_ready, (c - 1) * ET)
                sp.sem_inc(sp_go, 1)
                sp.dma_start(xT[b][:, :], K.pairT[l][c]).then_inc(loaded[b], 16)
                wait(sp, masks_ready, c - 1)
                sp.sem_inc(sp_go, 1)
                sp.dma_start(dst_row[b][:, :, :].rearrange("p j e -> p (j e)"),
                             bc(K.dst_rows[c].unsqueeze(0), [P, EDGES_C])).then_inc(row_loaded[b], 16)
                if not (isinstance(c, int) and c == 0):
                    store(c - 1, 1 - b)

            over_chunks(sp, body)
            store(CHUNKS - 1, 1)
            for b in range(2):
                sp.wait_ge(stored[b], 32 * CHUNKS // 2)

        @block.gpsimd
        def _(pool):
            def body(c, b, i):
                wait(pool, scattered[b], i * (16 * ET))
                pool.sem_inc(pool_go, 1)
                pool.tensor_copy(index[b][:, :], K.tail_i[:, bass.ds(c * ET, ET)]).then_inc(index_ready, 1)
                pool.wait_ge(index_ready, c + 1)
                for j in range(ET):
                    wait(pool, out_evac, c * ET + (j + 1))
                    pool.sem_inc(pool_go, 1)
                    pool.indirect_dma_start(K.out[l][:, :], bass.IndirectOffsetOnAxis(index[b][:, j:j + 1], 0),
                                            out_row[b][:, j, :], None, bounds_check=N - 1,
                                            oob_is_err=False).then_inc(scattered[b], 16)

            over_chunks(pool, body)
            for b in range(2):
                pool.wait_ge(scattered[b], 16 * ET * CHUNKS // 2)

        @block.vector
        def _(dve):
            order = Order(dve, steps, 2 + (2 * H - 1) * ET)
            nc.vector.memset(out_row[1][:, ET - 1, :], 0.0).then_inc(blank, 1)
            nc.vector.memset(K.change[:, :], 0.0).then_inc(blank, 1)

            def body(c, b, i):
                order.chunk(c)
                wait(dve, row_loaded[b], i * 16 + 16)
                wait(dve, stat_done, c - 1)
                order.done(nc.vector.tensor_copy(tails[b][:, 0, :], K.tail_c[:, bass.ds(c * ET, ET)]))
                nc.vector.tensor_copy(tails[b][:, 1, :], K.ntail_c[:, bass.ds(c * ET, ET)])
                order.done(nc.vector.tensor_copy(alpha[b][:, :, :], K.alpha_flat[:, :, bass.ds(c * ET, ET)]))
                nc.vector.tensor_tensor(same[b][:, :, :], dst_row[b][:, :, :],
                                        bc(K.dst_f[:, bass.ds(c * ET, ET)].unsqueeze(2), [P, ET, P]), ALU.is_equal)
                nc.vector.tensor_tensor(carry[b][:, :, :], dst_row[b][:, :, :],
                                        bc(K.prev_last[:, bass.ds(c * ET, ET)].unsqueeze(2), [P, ET, P]),
                                        ALU.is_equal).then_inc(masks_ready, 1)
                order.settle()
                for j in range(ET):
                    s = j % 2
                    wait(dve, src_done, c * ET + (j + 1))
                    wait(dve, dst_done, c * ET + (j + 1))
                    wait(dve, sums_done, c * ET + (j - 1))
                    for h in range(H):
                        for k, v in ((0, src_v[s]), (1, dst_v[s])):
                            out, in_ = part[s][:, k, :], v[0:P, h * D:(h + 1) * D]
                            weight = alpha[b][:, k * H + h, j:j + 1]
                            if h == 0:
                                order.done(nc.vector.tensor_scalar(out, in_, weight, None, ALU.mult))
                            else:
                                order.settle(back=1)
                                ins = nc.vector.scalar_tensor_tensor(out, in_, weight, out, ALU.mult, ALU.add)
                                if h == H - 1 and k == 1:
                                    ins.then_inc(part_ready, 1)
                                else:
                                    order.done(ins)
                wait(dve, stat_done, c + 1)
                nc.vector.tensor_tensor(K.change[:, :], K.change[:, :], stat[0:D, 0:2], ALU.add).then_inc(stat_used, 1)

            dve.wait_ge(blank, 2)
            over_chunks(dve, body)

        @block.scalar
        def _(act):
            def body(c, b, i):
                wait(act, stored[b], i * 32)
                wait(act, scattered[b], i * (16 * ET))
                wait(act, stat_done, c - 1)
                for j in range(ET):
                    if j % RG == RG - 1:
                        wait(act, base_done, c * 2 + (j // RG + 1))
                        k = j // RG
                        nc.scalar.copy(base[b][:, k * RG:(k + 1) * RG, :].rearrange("p j f -> p (j f)"),
                                       base_p[0:P, 0:RG * D]).then_inc(base_evac, 1)
                    wait(act, sums_done, c * ET + (j + 1))
                    nc.scalar.copy(out_row[b][:, j, :], sums[j % 2][0:P, 0:D]).then_inc(out_evac, 1)
                wait(act, stat_done, c)
                wait(act, out_evac, c * ET + ET)
                nc.scalar.activation(out_sq[:, :, :], out_row[b][:, :, :], ACT.Square).then_inc(sq_ready, 1)
                wait(act, base_evac, c * 2 + 2)
                nc.scalar.activation(base_sq[:, :, :], base[b][:, :, :], ACT.Square).then_inc(sq_ready, 1)

            act.wait_ge(blank, 2)
            over_chunks(act, body)

        @block.tensor
        def _(pe):
            def products(c, b, j):
                s = j % 2
                wait(pe, part_ready, c * ET + (j - 1))
                nc.tensor.matmul(src_v[s][0:P, 0:V], lhsT=xT[b][:, j * P:(j + 1) * P], rhs=K.w[l][:, :],
                                 start=True, stop=True).then_inc(src_done, 1)
                own = xT[b][:, (ET + j) * P:(ET + j + 1) * P]
                nc.tensor.matmul(dst_v[s][0:P, 0:V], lhsT=own, rhs=K.w[l][:, :], start=True, stop=True).then_inc(dst_done, 1)
                k, r = j // RG, j % RG
                if r == 0:
                    wait(pe, base_evac, c * 2 + k)
                ins = nc.tensor.matmul(base_p[0:P, r * D:(r + 1) * D], lhsT=own, rhs=K.w_bar[l][:, :], start=True, stop=True)
                if r == RG - 1:
                    ins.then_inc(base_done, 1)

            def body(c, b, i):
                wait(pe, loaded[b], i * 16 + 16)
                products(c, b, 0)
                wait(pe, masks_ready, c + 1)
                for j in range(ET):
                    if j + 1 < ET:
                        products(c, b, j + 1)
                    s = j % 2
                    wait(pe, part_ready, c * ET + (j + 1))
                    wait(pe, out_evac, c * ET + (j - 1))
                    for k in range(2):
                        nc.tensor.matmul(sums[s][0:P, 0:D], lhsT=same[b][:, j, :], rhs=part[s][:, k, :],
                                         start=(k == 0), stop=False)
                    wait(pe, out_evac, c * ET + j)
                    before = out_row[b][:, j - 1, :] if j else out_row[1 - b][:, ET - 1, :]
                    nc.tensor.matmul(sums[s][0:P, 0:D], lhsT=carry[b][:, j, :], rhs=before,
                                     start=False, stop=True).then_inc(sums_done, 1)
                wait(pe, sq_ready, c * 2 + 2)
                wait(pe, stat_used, c)
                for col, (new, old) in enumerate(((out_row[b], base[b]), (out_sq, base_sq))):
                    for k, rows in enumerate((new, old)):
                        for j in range(ET):
                            last = nc.tensor.matmul(stat[0:D, col:col + 1], lhsT=rows[:, j, :], rhs=tails[b][:, k, j:j + 1],
                                                    start=(k == 0 and j == 0), stop=(k == 1 and j == ET - 1))
                last.then_inc(stat_done, 1)

            pe.wait_ge(blank, 2)
            over_chunks(pe, body)



def batch_norm(nc, K, l):
    with Stage(nc, f"norm{l}") as st:
        sb, pair, bank, sem, sems = st.sb, st.pair, st.bank, st.sem, st.sems
        mv = sb("mv", (D, 2))
        mean, ex2, var, root, rroot = (sb(n, (D, 1)) for n in ("mean", "ex2", "var", "root", "rroot"))
        steps, var_ready, root_ready = (sem(n) for n in ("steps", "var_ready", "root_ready"))
        sp_go = sem("sp_go")
        block = st.enter_context(nc.Block())

        @block.scalar
        def _(act):
            act.wait_ge(var_ready, 1)
            nc.scalar.activation(root[:, :], var[:, :], ACT.Sqrt, bias=K.eps[0:D, :]).then_inc(root_ready, 1)

        @block.vector
        def _(dve):
            go = Line(dve, steps)
            go.step(nc.vector.bn_aggr(mv[:, :], K.stats[l][:, :, :].rearrange("p a s -> p (a s)")))
            go.step(nc.vector.tensor_tensor(ex2[:, :], mv[:, 0:1], mv[:, 0:1], ALU.mult))
            go.step(nc.vector.tensor_tensor(ex2[:, :], ex2[:, :], mv[:, 1:2], ALU.add))
            go.step(nc.vector.scalar_tensor_tensor(ex2[:, :], K.change[:, 1:2], 1.0 / N, ex2[:, :], ALU.mult, ALU.add))
            go.step(nc.vector.scalar_tensor_tensor(mean[:, :], K.change[:, 0:1], 1.0 / N, mv[:, 0:1], ALU.mult, ALU.add))
            go.step(nc.vector.tensor_tensor(var[:, :], mean[:, :], mean[:, :], ALU.mult))
            nc.vector.tensor_tensor(var[:, :], ex2[:, :], var[:, :], ALU.subtract).then_inc(var_ready, 1)
            dve.wait_ge(root_ready, 1)
            go.step(nc.vector.reciprocal(rroot[:, :], root[:, :]))
            go.step(nc.vector.tensor_tensor(K.scale[l][:, :], K.gamma[l][:, :], rroot[:, :], ALU.mult))
            go.step(nc.vector.tensor_tensor(mean[:, :], mean[:, :], K.bias[l][:, :], ALU.add))
            go.step(nc.vector.tensor_tensor(mean[:, :], K.bias[l][:, :], mean[:, :], ALU.subtract))
            go.step(nc.vector.scalar_tensor_tensor(K.shift[l][:, :], mean[:, :], K.scale[l][:, :], K.beta[l][:, :],
                                                   ALU.mult, ALU.add))



def second_layer(nc, K, A):
    out0_nodes = K.out[0].rearrange("(c p j) f -> c p (j f)", c=CHUNKS, p=P)
    out1_nodes = K.out[1].rearrange("(c p j) f -> c p (j f)", c=CHUNKS, p=P)
    NODE, EDGE = 0, 1
    with Stage(nc, "second") as st:
        sb, pair, bank, sem, sems = st.sb, st.pair, st.bank, st.sem, st.sems
        row = [pair("row_node", [P, TILES, D]), pair("row_edge", [P, TILES, D])]
        resT = [pair("resT_node", [D, COLS]), pair("resT_edge", [D, COLS])]
        actT = [sb("actT_node", [D, COLS]), sb("actT_edge", [D, COLS])]
        out_row = pair("out_row", [P, TILES * D])
        index = pair("index", [P, ET], i32)
        turned = [bank("turned0"), bank("turned1")]
        rows = [bank("rows0"), bank("rows1")]
        outT = [bank("outT0"), bank("outT1")]
        logit = [bank("logit0"), bank("logit1")]
        row_loaded = [sems("row_node_in"), sems("row_edge_in")]
        res_loaded = [sems("res_node_in"), sems("res_edge_in")]
        res_stored = [sems("res_node_out"), sems("res_edge_out")]
        gathered, rows_stored = sems("gathered"), sems("rows_stored")
        pool_go, index_ready = sem("pool_go"), sem("index_ready")
        t_done, t_evac, rows_done, rows_evac = (sem(n) for n in ("t_done", "t_evac", "rows_done", "rows_evac"))
        added = [sem("added_node"), sem("added_edge")]
        outT_done, outT_used, logit_done, logit_evac = (sem(n) for n in ("outT_done", "outT_used", "logit_done", "logit_evac"))
        sp_go = sem("sp_go")
        block = st.enter_context(nc.Block())

        def bank_no(c, kind, g):
            return c * (2 * GROUPS) + (kind * GROUPS + g)

        @block.sync
        def _(sp):
            def store(c, b):
                wait(sp, added[NODE], c + 1)
                sp.sem_inc(sp_go, 1)
                sp.dma_start(K.x1T[c], resT[NODE][b][:, :]).then_inc(res_stored[NODE][b], 16)
                wait(sp, added[EDGE], c + 1)
                sp.sem_inc(sp_go, 1)
                sp.dma_start(K.pairT[1][c], resT[EDGE][b][:, :]).then_inc(res_stored[EDGE][b], 16)
                wait(sp, rows_evac, c * RGROUPS + RGROUPS)
                sp.sem_inc(sp_go, 1)
                dma_rows(sp, out1_nodes[c], out_row[b][:, :], rows_stored[b])

            def body(c, b, i):
                wait(sp, t_done, bank_no(c - 2, NODE, GROUPS))
                sp.sem_inc(sp_go, 1)
                dma_rows(sp, row[NODE][b][:, :, :].rearrange("p j f -> p (j f)"), out0_nodes[c], row_loaded[NODE][b])
                wait(sp, res_stored[NODE][b], i * 16)
                sp.sem_inc(sp_go, 1)
                wait(sp, outT_done, c * GROUPS - GROUPS)
                sp.sem_inc(sp_go, 1)
                sp.dma_start(resT[NODE][b][:, :], K.h0T[c]).then_inc(res_loaded[NODE][b], 16)
                wait(sp, t_done, bank_no(c - 2, EDGE, GROUPS))
                sp.sem_inc(sp_go, 1)
                dma_rows(sp, row[EDGE][b][:, ET:TILES, :].rearrange("p j f -> p (j f)"), K.out_pairs[0][c], row_loaded[EDGE][b])
                wait(sp, res_stored[EDGE][b], i * 16)
                sp.sem_inc(sp_go, 1)
                wait(sp, logit_done, c - 1)
                sp.sem_inc(sp_go, 1)
                sp.dma_start(resT[EDGE][b][:, :], K.pairT[0][c]).then_inc(res_loaded[EDGE][b], 16)
                if not (isinstance(c, int) and c == 0):
                    store(c - 1, 1 - b)

            over_chunks(sp, body)
            store(CHUNKS - 1, 1)
            for b in range(2):
                sp.wait_ge(res_stored[NODE][b], 16 * CHUNKS // 2)
                sp.wait_ge(res_stored[EDGE][b], 16 * CHUNKS // 2)
                sp.wait_ge(rows_stored[b], 32 * CHUNKS // 2)

        @block.gpsimd
        def _(pool):
            def body(c, b, i):
                wait(pool, gathered[b], i * (16 * ET))
                wait(pool, t_done, bank_no(c - 2, EDGE, GROUPS))
                pool.sem_inc(pool_go, 1)
                pool.tensor_copy(index[b][:, :], K.src_i[:, bass.ds(c * ET, ET)]).then_inc(index_ready, 1)
                pool.wait_ge(index_ready, c + 1)
                pool.sem_inc(pool_go, 1)
                for j in range(ET):
                    pool.indirect_dma_start(row[EDGE][b][:, j, :], None, K.out[0][:, :],
                                            bass.IndirectOffsetOnAxis(index[b][:, j:j + 1], 0)).then_inc(gathered[b], 16)

            over_chunks(pool, body)

        @block.tensor
        def _(pe):
            def turn(kind, c, b, i):
                wait(pe, row_loaded[kind][b], i * 32 + 32)
                if kind == EDGE:
                    wait(pe, gathered[b], i * (16 * ET) + 16 * ET)
                for g in range(GROUPS):
                    wait(pe, t_evac, bank_no(c, kind, g) - 1)
                    for k in range(TG):
                        last = nc.tensor.transpose(turned[(kind * GROUPS + g) % 2][0:D, k * P:(k + 1) * P],
                                                   row[kind][b][:, g * TG + k, :], K.eye[:, :])
                    last.then_inc(t_done, 1)

            def body(c, b, i):
                turn(NODE, c, b, i)
                turn(EDGE, c, b, i)
                dense_rows(nc, K, pe, 1, c, b, resT[NODE][b], rows, added[NODE], lambda g: c + 1, rows_evac, rows_done)
                for g in range(GROUPS):
                    wait(pe, outT_used, c * GROUPS + (g - 1))
                    nc.tensor.matmul(outT[(b + g) % 2][0:D, 0:TG * P], lhsT=K.w_bar[1][:, :],
                                     rhs=resT[NODE][b][:, g * TG * P:(g + 1) * TG * P],
                                     start=True, stop=True).then_inc(outT_done, 1)
                edge_logits(nc, K, pe, 1, c, b, resT[EDGE][b], logit[b], added[EDGE], c + 1, logit_evac, logit_done)

            over_chunks(pe, body)

        @block.scalar
        def _(act):
            def affine_relu(kind, c, b):
                wait(act, added[kind], c)
                for g in range(GROUPS):
                    wait(act, t_done, bank_no(c, kind, g + 1))
                    nc.scalar.activation(actT[kind][:, g * TG * P:(g + 1) * TG * P],
                                         turned[(kind * GROUPS + g) % 2][0:D, 0:TG * P], ACT.Relu,
                                         bias=K.shift[0][:, :], scale=K.scale[0][:, :]).then_inc(t_evac, 1)

            def body(c, b, i):
                affine_relu(NODE, c, b)
                affine_relu(EDGE, c, b)
                wait(act, rows_stored[b], i * 32)
                for k in range(RGROUPS):
                    wait(act, rows_done, c * RGROUPS + (k + 1))
                    nc.scalar.copy(out_row[b][:, k * RG * D:(k + 1) * RG * D], rows[k % 2][0:P, 0:RG * D]).then_inc(rows_evac, 1)
                wait(act, logit_done, c + 1)
                nc.scalar.copy(K.logits[:, :, bass.ds(c * ET, ET)],
                               logit[b][0:P, 0:3 * H * ET].rearrange("p (k j) -> p k j", j=ET)).then_inc(logit_evac, 1)

            over_chunks(act, body)

        @block.vector
        def _(dve):
            def body(c, b, i):
                for kind in (NODE, EDGE):
                    wait(dve, res_loaded[kind][b], i * 16 + 16)
                    wait(dve, t_evac, bank_no(c, kind, GROUPS))
                    nc.vector.tensor_tensor(resT[kind][b][:, :], resT[kind][b][:, :], actT[kind][:, :],
                                            ALU.add).then_inc(added[kind], 1)
                for g in range(GROUPS):
                    wait(dve, outT_done, c * GROUPS + (g + 1))
                    nc.vector.bn_stats(K.stats[1][:, bass.ds(c * GROUPS + g, 1), :].rearrange("p a s -> p (a s)"),
                                       outT[(b + g) % 2][0:D, 0:TG * P]).then_inc(outT_used, 1)

            over_chunks(dve, body)



def third_layer(nc, K, A):
    x_nodes = A["x"].rearrange("(c p j) f -> c p (j f)", c=CHUNKS, p=P)
    out1_nodes = K.out[1].rearrange("(c p j) f -> c p (j f)", c=CHUNKS, p=P)
    y_nodes = K.y.rearrange("(c p j) f -> c p (j f)", c=CHUNKS, p=P)
    attr = K.attr.rearrange("(c j p) f -> c p j f", c=CHUNKS, p=P)
    NODE, EDGE = 0, 1
    HG = (4, 4, 2)
    with Stage(nc, "third") as st:
        sb, pair, bank, sem, sems = st.sb, st.pair, st.bank, st.sem, st.sems
        row = pair("row", [P, TILES, D])
        res = pair("res", [D, COLS])
        xrow = pair("xrow", [P, TILES, D])
        actT = pair("actT", [D, COLS])
        ysum = pair("ysum", [P, TILES, D])
        norm = pair("norm", [P, TILES, D])
        square = sb("square", [P, TILES, D])
        total, sqsum, dev, rdev = (sb(n, [P, TILES]) for n in ("total", "sqsum", "dev", "rdev"))
        index = pair("index", [P, ET], i32)
        ea = sb("ea", [P, ET, D])
        dst_row = sb("dst_row", [P, ET, P], i32)
        same = sb("same", [P, ET, P])
        go_on = sb("go_on", [D, ET, P])
        aggr = pair("aggr", [D, EDGES_C])
        hidden = sb("hidden", [D, 2, EDGES_C])
        final = sb("final", [P, ET, D])
        turned = [bank("turned0"), bank("turned1")]
        yp = [bank("yp0"), bank("yp1")]
        ap = [bank("ap0"), bank("ap1")]
        hp, mp = bank("hp"), bank("mp")

        row_in, res_in, x_in = sems("row_in"), sems("res_in"), sems("x_in")
        y_out = sem("y_out")
        gathered = sems("gathered")
        ea_in, dr_in, final_out = sem("ea_in"), sem("dr_in"), sem("final_out")
        pool_go, index_ready = sem("pool_go"), sem("index_ready")
        t_done, t_evac, y_done, y_evac = (sem(n) for n in ("t_done", "t_evac", "y_done", "y_evac"))
        centred, squared, summed, rooted, normed, y_ready = (
            sem(n) for n in ("centred", "squared", "summed", "rooted", "normed", "y_ready"))
        masks_ready, ap_done, aggr_ready, hp_done, hid_ready, mp_done, final_ready, blank, steps = (
            sem(n) for n in ("masks_ready", "ap_done", "aggr_ready", "hp_done", "hid_ready", "mp_done",
                             "final_ready", "blank", "dve_steps"))
        sp_go = sem("sp_go")
        block = st.enter_context(nc.Block())

        @block.sync
        def _(sp):
            def flat(t):
                return t.rearrange("p j f -> p (j f)")

            def body(c, b, i):
                w = c * 2
                wait(sp, t_done, (w - 1) * GROUPS)
                sp.sem_inc(sp_go, 1)
                dma_rows(sp, flat(row[NODE][:, :, :]), out1_nodes[c], row_in[NODE])
                wait(sp, y_done, (w - 1) * RGROUPS)
                sp.sem_inc(sp_go, 1)
                sp.dma_start(res[NODE][:, :], K.x1T[c]).then_inc(res_in[NODE], 16)
                dma_rows(sp, flat(xrow[NODE][:, :, :]), x_nodes[c], x_in[NODE])
                wait(sp, t_done, w * GROUPS)
                sp.sem_inc(sp_go, 1)
                dma_rows(sp, flat(row[EDGE][:, ET:TILES, :]), K.out_pairs[1][c], row_in[EDGE])
                wait(sp, y_done, w * RGROUPS)
                sp.sem_inc(sp_go, 1)
                sp.dma_start(res[EDGE][:, :], K.pairT[1][c]).then_inc(res_in[EDGE], 16)
                dma_rows(sp, flat(xrow[EDGE][:, :, :]), K.raw_pairs[c], x_in[EDGE])
                wait(sp, masks_ready, c)
                sp.sem_inc(sp_go, 1)
                sp.dma_start(dst_row[:, :, :].rearrange("p j e -> p (j e)"),
                             bc(K.dst_rows[c].unsqueeze(0), [P, EDGES_C])).then_inc(dr_in, 16)
                wait(sp, ap_done, c * ET)
                sp.sem_inc(sp_go, 1)
                dma_rows(sp, ea[:, :, :], attr[c], ea_in)
                wait(sp, y_ready, w + 1)
                sp.sem_inc(sp_go, 1)
                dma_rows(sp, y_nodes[c], flat(ysum[NODE][:, :, :]), y_out)
                wait(sp, final_ready, c * 2 + 2)
                sp.sem_inc(sp_go, 1)
                dma_rows(sp, K.final_pairs[c], flat(final[:, :, :]), final_out)

            over_chunks(sp, body)
            sp.wait_ge(y_out, 32 * CHUNKS)
            sp.wait_ge(final_out, 32 * CHUNKS)

        @block.gpsimd
        def _(pool):
            def body(c, b, i):
                wait(pool, gathered[b], i * (16 * ET))
                wait(pool, t_done, c * (2 * GROUPS))
                pool.sem_inc(pool_go, 1)
                pool.tensor_copy(index[b][:, :], K.src_i[:, bass.ds(c * ET, ET)]).then_inc(index_ready, 1)
                pool.wait_ge(index_ready, c + 1)
                pool.sem_inc(pool_go, 1)
                for j in range(ET):
                    pool.indirect_dma_start(row[EDGE][:, j, :], None, K.out[1][:, :],
                                            bass.IndirectOffsetOnAxis(index[b][:, j:j + 1], 0)).then_inc(gathered[b], 16)

            over_chunks(pool, body)

        @block.tensor
        def _(pe):
            def turn(kind, c, b, i):
                w = c * 2 + kind
                wait(pe, row_in[kind], c * 32 + 32)
                if kind == EDGE:
                    wait(pe, gathered[b], i * (16 * ET) + 16 * ET)
                for g in range(GROUPS):
                    wait(pe, t_evac, w * GROUPS + (g - 1))
                    for k in range(TG):
                        last = nc.tensor.transpose(turned[(kind + g) % 2][0:D, k * P:(k + 1) * P],
                                                   row[kind][:, g * TG + k, :], K.eye[:, :])
                    last.then_inc(t_done, 1)

            def sums(kind, c):
                w = c * 2 + kind
                wait(pe, x_in[kind], c * 32 + 32)
                wait(pe, res_in[kind], c * 16 + 16)
                wait(pe, t_evac, w * GROUPS + GROUPS)
                for k in range(RGROUPS):
                    wait(pe, y_evac, w * RGROUPS + (k - 1))
                    out = yp[k % 2]
                    nc.tensor.matmul(out[0:P, 0:RG * D], lhsT=K.eye[:, :],
                                     rhs=xrow[kind][:, k * RG:(k + 1) * RG, :].rearrange("p j f -> p (j f)"),
                                     start=True, stop=False)
                    for r in range(RG):
                        j = k * RG + r
                        for part in (res[kind], actT[kind]):
                            last = nc.tensor.matmul(out[0:P, r * D:(r + 1) * D], lhsT=part[:, j * P:(j + 1) * P],
                                                    rhs=K.eye[0:D, 0:D], start=False,
                                                    stop=(r == RG - 1 and part is actT[kind]))
                    last.then_inc(y_done, 1)

            def body(c, b, i):
                turn(NODE, c, b, i)
                sums(NODE, c)
                turn(EDGE, c, b, i)
                sums(EDGE, c)
                wait(pe, normed, c * 2 + 2)
                wait(pe, ea_in, c * 32 + 32)
                wait(pe, masks_ready, c + 1)
                for j in range(ET):
                    wait(pe, aggr_ready, c * ET + (j - 1))
                    for k, part in enumerate((norm[EDGE], ea)):
                        last = nc.tensor.matmul(ap[j % 2][0:D, 0:P], lhsT=part[:, j, :], rhs=same[:, j, :],
                                                start=(k == 0), stop=(k == 1))
                    last.then_inc(ap_done, 1)
                at = 0
                for q, cnt in enumerate(HG):
                    wait(pe, aggr_ready, c * ET + (at + cnt))
                    for half in range(2):
                        wait(pe, hid_ready, c * 6 + (2 * q + half))
                        nc.tensor.matmul(hp[0:D, 0:cnt * P], lhsT=K.w1[:, half * D:(half + 1) * D],
                                         rhs=aggr[b][:, at * P:(at + cnt) * P], start=True, stop=True).then_inc(hp_done, 1)
                    at += cnt
                wait(pe, hid_ready, c * 6 + 6)
                for k in range(2):
                    wait(pe, final_ready, c * 2 + k)
                    nc.tensor.matmul(mp[0:P, 0:RG * D], lhsT=K.ones1[:, :], rhs=K.b2_row[:, :], start=True, stop=False)
                    for r in range(RG):
                        j = k * RG + r
                        for half in range(2):
                            last = nc.tensor.matmul(mp[0:P, r * D:(r + 1) * D], lhsT=hidden[:, half, j * P:(j + 1) * P],
                                                    rhs=K.w2[:, half, :], start=False, stop=(r == RG - 1 and half == 1))
                    last.then_inc(mp_done, 1)

            over_chunks(pe, body)

        @block.scalar
        def _(act):
            def item(kind, c):
                w = c * 2 + kind
                wait(act, y_done, (w - 1) * RGROUPS)
                for g in range(GROUPS):
                    wait(act, t_done, w * GROUPS + (g + 1))
                    nc.scalar.activation(actT[kind][:, g * TG * P:(g + 1) * TG * P],
                                         turned[(kind + g) % 2][0:D, 0:TG * P], ACT.Relu,
                                         bias=K.shift[1][:, :], scale=K.scale[1][:, :]).then_inc(t_evac, 1)
                if kind == NODE:
                    wait(act, y_out, c * 32)
                else:
                    wait(act, final_ready, c * 2)
                for k in range(RGROUPS):
                    wait(act, y_done, w * RGROUPS + (k + 1))
                    nc.scalar.copy(ysum[kind][:, k * RG:(k + 1) * RG, :].rearrange("p j f -> p (j f)"),
                                   yp[k % 2][0:P, 0:RG * D]).then_inc(y_evac, 1)
                wait(act, centred, w + 1)
                nc.scalar.activation(square[:, :, :], norm[kind][:, :, :], ACT.Square).then_inc(squared, 1)
                wait(act, summed, w + 1)
                nc.scalar.activation(dev[:, :], sqsum[:, :], ACT.Sqrt, bias=K.eps[:, :], scale=1.0 / D).then_inc(rooted, 1)

            def body(c, b, i):
                item(NODE, c)
                item(EDGE, c)
                at = 0
                for q, cnt in enumerate(HG):
                    for half in range(2):
                        wait(act, hp_done, c * 6 + (2 * q + half + 1))
                        nc.scalar.activation(hidden[:, half, at * P:(at + cnt) * P], hp[0:D, 0:cnt * P], ACT.Relu,
                                             bias=K.b1[:, half:half + 1]).then_inc(hid_ready, 1)
                    at += cnt

            over_chunks(act, body)

        @block.vector
        def _(dve):
            order = Order(dve, steps, 6)

            def item(kind, c):
                w = c * 2 + kind
                y, h = ysum[kind], norm[kind]
                wait(dve, y_evac, w * RGROUPS + RGROUPS)
                order.done(nc.vector.tensor_reduce(total[:, :], y[:, :, :], AX.X, ALU.add))
                order.settle()
                nc.vector.scalar_tensor_tensor(h[:, :, :], bc(total[:, :].unsqueeze(2), [P, TILES, D]),
                                               -1.0 / D, y[:, :, :], ALU.mult, ALU.add).then_inc(centred, 1)
                wait(dve, squared, w + 1)
                nc.vector.tensor_reduce(sqsum[:, :], square[:, :, :], AX.X, ALU.add).then_inc(summed, 1)
                wait(dve, rooted, w + 1)
                order.done(nc.vector.reciprocal(rdev[:, :], dev[:, :]))
                order.settle()
                nc.vector.scalar_tensor_tensor(h[:, :, :], h[:, :, :], 0.0, bc(rdev[:, :].unsqueeze(2), [P, TILES, D]),
                                               ALU.max, ALU.mult).then_inc(normed, 1)
                wait(dve, normed, w + 1)
                tiles = slice(0, TILES) if kind == NODE else slice(ET, TILES)
                order.done(nc.vector.scalar_tensor_tensor(y[:, tiles, :], h[:, tiles, :], K.eps1[:, :], y[:, tiles, :],
                                                          ALU.mult, ALU.add))
                if kind == NODE:
                    order.settle()
                    nc.vector.tensor_tensor(y[:, :, :], y[:, :, :], bc(K.mlp_empty[:, :].unsqueeze(1), [P, TILES, D]),
                                            ALU.add).then_inc(y_ready, 1)
                else:
                    order.settle()
                    dve.sem_inc(y_ready, 1)

            def body(c, b, i):
                order.chunk(c)
                wait(dve, dr_in, c * 16 + 16)
                wait(dve, ap_done, c * ET)
                nc.vector.tensor_tensor(same[:, :, :], dst_row[:, :, :],
                                        bc(K.dst_f[:, bass.ds(c * ET, ET)].unsqueeze(2), [P, ET, P]), ALU.is_equal)
                nc.vector.tensor_tensor(go_on[:, :, :], dst_row[0:D, :, :],
                                        bc(K.prev_b[:, bass.ds(c * ET, ET)].unsqueeze(2), [D, ET, P]),
                                        ALU.is_equal).then_inc(masks_ready, 1)
                item(NODE, c)
                item(EDGE, c)
                wait(dve, hp_done, c * 6 - 6)
                for j in range(ET):
                    wait(dve, ap_done, c * ET + (j + 1))
                    wait(dve, aggr_ready, c * ET + j)
                    before = aggr[b][:, j * P - 1:j * P] if j else aggr[1 - b][:, EDGES_C - 1:EDGES_C]
                    nc.vector.scalar_tensor_tensor(aggr[b][:, j * P:(j + 1) * P], go_on[:, j, :], before,
                                                   ap[j % 2][0:D, 0:P], ALU.mult, ALU.add).then_inc(aggr_ready, 1)
                wait(dve, final_out, c * 32)
                for k in range(2):
                    wait(dve, mp_done, c * 2 + (k + 1))
                    nc.vector.tensor_tensor(final[:, k * RG:(k + 1) * RG, :].rearrange("p j f -> p (j f)"),
                                            mp[0:P, 0:RG * D],
                                            ysum[EDGE][:, ET + k * RG:ET + (k + 1) * RG, :].rearrange("p j f -> p (j f)"),
                                            ALU.add).then_inc(final_ready, 1)

            nc.vector.memset(aggr[1][:, EDGES_C - 1:EDGES_C], 0.0).then_inc(blank, 1)
            dve.wait_ge(blank, 1)
            over_chunks(dve, body)


def scatter_final(nc, K):
    with Stage(nc, "last") as st:
        sb, pair, bank, sem, sems = st.sb, st.pair, st.bank, st.sem, st.sems
        final = pair("final", [P, ET, D])
        index = pair("index", [P, ET], i32)
        loaded, scattered = sems("loaded"), sems("scattered")
        pool_go, index_ready = (sem(n) for n in ("pool_go", "index_ready"))
        sp_go = sem("sp_go")
        block = st.enter_context(nc.Block())

        @block.sync
        def _(sp):
            def body(c, b, i):
                wait(sp, scattered[b], i * (16 * ET))
                sp.sem_inc(sp_go, 1)
                dma_rows(sp, final[b][:, :, :].rearrange("p j f -> p (j f)"), K.final_pairs[c], loaded[b])

            over_chunks(sp, body)

        @block.gpsimd
        def _(pool):
            def body(c, b, i):
                wait(pool, scattered[b], i * (16 * ET))
                pool.sem_inc(pool_go, 1)
                pool.tensor_copy(index[b][:, :], K.tail_i[:, bass.ds(c * ET, ET)]).then_inc(index_ready, 1)
                pool.wait_ge(index_ready, c + 1)
                pool.wait_ge(loaded[b], i * 32 + 32)
                pool.sem_inc(pool_go, 1)
                for j in range(ET):
                    pool.indirect_dma_start(K.y[:, :], bass.IndirectOffsetOnAxis(index[b][:, j:j + 1], 0),
                                            final[b][:, j, :], None, bounds_check=N - 1,
                                            oob_is_err=False).then_inc(scattered[b], 16)

            over_chunks(pool, body)
            for b in range(2):
                pool.wait_ge(scattered[b], 16 * ET * CHUNKS // 2)


def build(nc, A, y):
    K = Core()
    K.y = y
    K.src, K.dst, K.attr = A["src"], A["dst"], A["edge_attr_96"]
    K.dst_rows = K.dst.rearrange("(c e) -> c e", c=CHUNKS)

    def dram(name, shape):
        return nc.dram_tensor(name, shape, fp32, kind="Internal").ap()

    K.out = [dram(f"out_rows{l}", [N, D]) for l in range(LAYERS)]
    K.h0T, K.x1T = dram("h0T", [CHUNKS, D, COLS]), dram("x1T", [CHUNKS, D, COLS])
    K.pairT = [dram(f"pairT{l}", [CHUNKS, D, COLS]) for l in range(LAYERS)]
    K.raw_pairs = dram("raw_pairs", [CHUNKS, P, TILES * D])
    K.out_pairs = [dram(f"out_pairs{l}", [CHUNKS, P, ET * D]) for l in range(LAYERS)]
    K.final_pairs = dram("final_pairs", [CHUNKS, P, ET * D])
    with Stage(nc, "all") as st:
        sb = st.sb
        K.eye, K.eps, K.ones, K.ones1 = sb("eye", (P, P)), sb("eps", (P, 1)), sb("ones", (P, 1)), sb("ones1", (1, P))
        K.w = [sb(f"w_heads{l}", (D, HD)) for l in range(LAYERS)]
        K.w_bar = [sb(f"w_bar{l}", (D, D)) for l in range(LAYERS)]
        K.w_att = [sb(f"w_att{l}", (D, 3 * H)) for l in range(LAYERS)]
        K.bias, K.gamma, K.beta, K.scale, K.shift = (
            [sb(f"{n}{l}", (D, 1)) for l in range(LAYERS)] for n in ("bias", "gamma", "beta", "scale", "shift"))
        K.w1, K.w2, K.b1, K.b2_row = sb("w1", (D, 2 * D)), sb("w2", (D, 2, D)), sb("b1", (D, 2)), sb("b2_row", (1, RG * D))
        K.mlp_empty, K.eps1 = sb("mlp_empty", (P, D)), sb("eps1", (P, 1))
        K.cont_f, K.cont_b, K.tail, K.pen_f = (sb(n, (LANES, EDGES_C)) for n in ("cont_f", "cont_b", "tail", "pen_f"))
        K.all_f, K.all_b, K.all_pen = (sb(n, (1, LANES)) for n in ("all_f", "all_b", "all_pen"))
        K.src_i, K.dst_i, K.tail_i = (sb(n, (P, EDGE_TILES), i32) for n in ("src_i", "dst_i", "tail_i"))
        K.dst_f, K.tail_c, K.ntail_c, K.prev_last = (sb(n, (P, EDGE_TILES)) for n in ("dst_f", "tail_c", "ntail_c", "prev_last"))
        K.prev_b = sb("prev_b", (D, EDGE_TILES))
        K.logits = sb("logits", (P, 3 * H, EDGE_TILES))
        K.alpha = sb("alpha", (P, 2, LANES, ET))
        K.alpha_flat = K.alpha[:, :, :, :].rearrange("p k (h b) j -> p (k h) (b j)", h=H)
        K.stats = [sb(f"stats{l}", (D, CHUNKS * GROUPS, 6)) for l in range(LAYERS)]
        K.change = sb("change", (D, 2))

        prepare(nc, K, A)
        first_layer(nc, K, A)
        edge_softmax(nc, K, 0)
        aggregate(nc, K, 0)
        batch_norm(nc, K, 0)
        second_layer(nc, K, A)
        edge_softmax(nc, K, 1)
        aggregate(nc, K, 1)
        batch_norm(nc, K, 1)
        third_layer(nc, K, A)
        scatter_final(nc, K)


_INS = ["x", "src", "dst", "edge_attr_96", "L0_gnn_W", "L0_gnn_att_src", "L0_gnn_att_dst", "L0_gnn_bias",
        "L0_gnn_gamma", "L0_gnn_beta", "L1_gnn_W1", "L1_gnn_b1", "L1_gnn_W2", "L1_gnn_b2", "L1_gnn_eps"]


def kernel(**inputs):
    import numpy as np
    import concourse.bacc as bacc
    from concourse.bass_utils import run_bass_kernel_spmd

    nc = bacc.Bacc("TRN2", target_bir_lowering=False, num_devices=1)
    arrays, A = {}, {}
    for name in _INS:
        a = np.ascontiguousarray(inputs[name])
        arrays[f"in_{name}"] = a
        A[name] = nc.dram_tensor(f"in_{name}", a.shape, mybir.dt.from_np(a.dtype), kind="ExternalInput").ap()
    y = nc.dram_tensor("out_0", (N, D), fp32, kind="ExternalOutput").ap()
    build(nc, A, y)
    r = run_bass_kernel_spmd(nc, [arrays], core_ids=[0])
    return r.results[0]["out_0"]
```

```python
import concourse.bass as bass
import concourse.mybir as mybir
from contextlib import ExitStack

fp32 = mybir.dt.float32
i32 = mybir.dt.int32
ALU = mybir.AluOpType
ACT = mybir.ActivationFunctionType
AX = mybir.AxisListType

N, E, D, H = 50000, 25000, 96, 4
LAYERS = 2
P = 125
CHUNKS = 20
TILES = 20
ET = TILES // 2
NODES_C = N // CHUNKS
EDGES_C = E // CHUNKS
EDGE_TILES = E // P
COLS = TILES * P
TG = 4
GROUPS = TILES // TG
RG = 5
RGROUPS = TILES // RG
LANES = H * CHUNKS
HD = H * D
SLOPE, EPS, TINY = 0.2, 1e-05, 1e-16
BIG = 1.0e30
assert N == CHUNKS * TILES * P and E == CHUNKS * ET * P


def wait(eng, sem, count):
    if isinstance(count, int) and count <= 0:
        return
    eng.wait_ge(sem, count)


def over_chunks(eng, body):
    for c in range(4):
        body(c, c % 2, c // 2)
    with eng.Fori(2, CHUNKS // 2) as i:
        body(i * 2, 0, i)
        body(i * 2 + 1, 1, i)


def earlier(c, b, j, k):
    return (c, b, j - k) if j >= k else (c - 1, 1 - b, j - k + ET)


class Line:

    def __init__(self, eng, sem):
        self.eng, self.sem, self.n = eng, sem, 0

    def step(self, ins):
        ins.then_inc(self.sem, 1)
        self.n += 1
        self.eng.wait_ge(self.sem, self.n)


class Stage(ExitStack):

    def __init__(self, nc, tag):
        super().__init__()
        self.nc, self.tag, self.used = nc, tag, []

    def sb(self, name, shape, dt=fp32):
        return self.enter_context(self.nc.sbuf_tensor(f"{self.tag}_{name}", list(shape), dt))

    def pair(self, name, shape, dt=fp32):
        return [self.sb(f"{name}{b}", shape, dt) for b in range(2)]

    def bank(self, name):
        return self.enter_context(self.nc.psum_tensor(f"{self.tag}_{name}", [P, 512], fp32))

    def sem(self, name):
        self.used.append(self.nc.alloc_semaphore(f"{self.tag}_{name}"))
        return self.used[-1]

    def sems(self, name):
        return [self.sem(f"{name}{b}") for b in range(2)]

    def __exit__(self, *what):
        done = super().__exit__(*what)
        if what[0] is None and self.used:
            self.nc.clear_and_free_semaphores(self.used)
            self.nc.all_engine_barrier()
        return done


class Core:
    pass


def bc(ap, shape):
    return ap.broadcast_to(shape)



def prepare(nc, K, A):
    with Stage(nc, "prep") as st:
        sb, pair, bank, sem, sems = st.sb, st.pair, st.bank, st.sem, st.sems
        att = [[sb(f"att_{s}{l}", [D, HD]) for s in ("src", "dst")] for l in range(LAYERS)]
        prod = sb("prod", [D, HD])
        raw = [sb(f"raw_{n}", [100, 2, P], i32) for n in ("src", "dst", "next")]
        rawf = [sb(f"rawf_{n}", [100, 2, P]) for n in ("src", "dst", "next")]
        nextc = sb("nextc", [P, EDGE_TILES])
        gap, tail_c = sb("gap", [P, EDGE_TILES]), sb("tail_c", [P, EDGE_TILES])
        lane_d = sb("lane_d", [LANES, EDGES_C], i32)
        lane_n = sb("lane_n", [LANES, EDGES_C], i32)
        lane_p = sb("lane_p", [LANES, EDGES_C], i32)
        allf = sb("allf", [LANES, 1])
        allb = sb("allb", [LANES, 1])
        b1p = sb("b1p", [D, 2])
        b1r = sb("b1r", [D, 2, P])
        pick = sb("pick", [P, D])
        cols = bank("cols")
        rows = bank("rows")
        mlp0 = bank("mlp0")
        loads, blanks, made, dve_s, colsem, pe_s, eye_s = (
            sem(n) for n in ("loads", "blanks", "made", "dve_steps", "cols_ready", "pe_rows", "eye_s"))
        flags_ready, sel_ready, b1_ready, w_ready = (sem(n) for n in ("flags_ready", "sel_ready", "b1_ready", "w_ready"))
        cols_used, pool_mask = sem("cols_used"), sem("pool_mask")
        dst1 = K.dst.rearrange("(a n) -> a n", a=1)
        sp_go = sem("sp_go")
        block = st.enter_context(nc.Block())
        n_loads = [0]

        @block.sync
        def _(sp):
            def load(out, in_):
                sp.dma_start(out, in_).then_inc(loads, 16)
                n_loads[0] += 16

            sp.wait_ge(blanks, 3)
            for n, lst in ((0, K.src), (1, K.dst)):
                load(raw[n][:, :, :], lst.rearrange("(a q p) -> q a p", a=2, q=100))
            load(raw[2][:, 0, :], K.dst[1:100 * P + 1].rearrange("(q p) -> q p", q=100))
            load(raw[2][0:99, 1, :], K.dst[100 * P + 1:199 * P + 1].rearrange("(q p) -> q p", q=99))
            load(raw[2][99:100, 1, 0:P - 1], dst1[:, 199 * P + 1:E])
            last = CHUNKS - 1
            for h in range(H):
                o = h * CHUNKS
                load(lane_d[o:o + CHUNKS, :], K.dst.rearrange("(b e) -> b e", b=CHUNKS))
                load(lane_n[o:o + last, :], K.dst[1:1 + last * EDGES_C].rearrange("(b e) -> b e", b=last))
                load(lane_n[o + last:o + CHUNKS, 0:EDGES_C - 1], dst1[:, last * EDGES_C + 1:E])
                load(lane_p[o:o + 1, 1:EDGES_C], dst1[:, 0:EDGES_C - 1])
                load(lane_p[o + 1:o + CHUNKS, :],
                     K.dst[EDGES_C - 1:E - 1].rearrange("(b e) -> b e", b=last))
            for l in range(LAYERS):
                load(K.w[l][:, :], A["L0_gnn_W"][l, :, :])
                for s, name in enumerate(("L0_gnn_att_src", "L0_gnn_att_dst")):
                    load(att[l][s][:, :], bc(A[name][l:l + 1, :, :].rearrange("l h d -> l (h d)"), [D, HD]))
                load(K.bias[l][:, :], A["L0_gnn_bias"][l:l + 1, :].rearrange("l d -> d l"))
                load(K.gamma[l][:, :], A["L0_gnn_gamma"][l:l + 1, :].rearrange("l d -> d l"))
                load(K.beta[l][:, :], A["L0_gnn_beta"][l:l + 1, :].rearrange("l d -> d l"))
            load(K.w1[:, :], A["L1_gnn_W1"])
            load(K.w2[:, :, :], A["L1_gnn_W2"].rearrange("(k p) n -> p k n", k=2))
            for k in range(2):
                load(K.b1[:, k:k + 1], A["L1_gnn_b1"][k * D:(k + 1) * D].rearrange("(p a) -> p a", a=1))
            load(K.b2b[:, :], bc(A["L1_gnn_b2"].rearrange("(a n) -> a n", a=1), [P, D]))
            load(K.eps1[:, :], bc(A["L1_gnn_eps"].rearrange("(a n) -> a n", a=1), [P, 1]))
            sp.wait_ge(loads, n_loads[0])

        @block.gpsimd
        def _(pool):
            pool.memset(K.eye[:, :], 0.0).then_inc(eye_s, 1)
            pool.memset(pick[:, :], 1.0).then_inc(eye_s, 1)
            pool.wait_ge(eye_s, 2)
            pool.affine_select(out=K.eye[:, :], in_=K.eye[:, :], compare_op=ALU.not_equal, fill=1.0, base=0,
                               pattern=[[-1, P]], channel_multiplier=1).then_inc(sel_ready, 1)
            pool.affine_select(out=pick[:, :], in_=pick[:, :], compare_op=ALU.is_equal, fill=0.0, base=1 - P,
                               pattern=[[0, D]], channel_multiplier=1).then_inc(sel_ready, 1)
            pool.wait_ge(pool_mask, 1)
            pool.affine_select(out=K.prev_last[:, :], in_=K.prev_last[:, :], compare_op=ALU.is_equal,
                               fill=-1.0, base=1 - P, pattern=[[0, EDGE_TILES]],
                               channel_multiplier=1).then_inc(sel_ready, 1)
            pool.wait_ge(sel_ready, 3)

        @block.vector
        def _(dve):
            go = Line(dve, dve_s)
            nc.vector.memset(raw[2][:, :, :], -1).then_inc(blanks, 1)
            nc.vector.memset(lane_n[:, :], -1).then_inc(blanks, 1)
            nc.vector.memset(lane_p[:, :], -1).then_inc(blanks, 1)
            nc.vector.memset(K.eps[:, :], EPS).then_inc(made, 1)
            nc.vector.memset(K.prev_last[:, :], -1.0).then_inc(made, 1)
            dve.wait_ge(made, 2)
            dve.wait_ge(loads, n_loads[0])
            for n in range(3):
                nc.vector.tensor_copy(rawf[n][:, :, :], raw[n][:, :, :]).then_inc(flags_ready, 1)
            go.step(nc.vector.tensor_tensor(K.cont_f[:, :], lane_d[:, :], lane_p[:, :], ALU.is_equal))
            go.step(nc.vector.tensor_tensor(K.cont_b[:, :], lane_d[:, :], lane_n[:, :], ALU.is_equal))
            go.step(nc.vector.tensor_scalar(K.tail[:, :], K.cont_b[:, :], -1.0, 1.0, ALU.mult, ALU.add))
            go.step(nc.vector.tensor_scalar(K.pen_f[:, :], K.cont_f[:, :], BIG, -BIG, ALU.mult, ALU.add))
            go.step(nc.vector.tensor_reduce(allf[:, :], K.cont_f[:, :], AX.X, ALU.min))
            nc.vector.tensor_reduce(allb[:, :], K.cont_b[:, :], AX.X, ALU.min).then_inc(flags_ready, 1)
            dve.wait_ge(pe_s, 1)
            go.step(nc.vector.tensor_copy(K.all_f[:, :], rows[0:1, 0:LANES]))
            go.step(nc.vector.tensor_copy(K.all_b[:, :], rows[0:1, LANES:2 * LANES]))
            go.step(nc.vector.tensor_scalar(K.all_pen[:, :], K.all_f[:, :], BIG, -BIG, ALU.mult, ALU.add))
            dve.wait_ge(colsem, 1)
            go.step(nc.vector.tensor_copy(K.src_i[:, :], cols[:, 0:200]))
            go.step(nc.vector.tensor_copy(K.dst_f[:, :], cols[:, 200:400]))
            nc.vector.tensor_copy(nextc[:, :], rows[:, 200:400]).then_inc(cols_used, 1)
            dve.wait_ge(cols_used, 1)
            go.step(nc.vector.tensor_copy(K.dst_i[:, :], K.dst_f[:, :]))
            go.step(nc.vector.tensor_tensor(tail_c[:, :], K.dst_f[:, :], nextc[:, :], ALU.not_equal))
            go.step(nc.vector.tensor_scalar(gap[:, :], K.dst_f[:, :], -float(N), None, ALU.add))
            go.step(nc.vector.tensor_tensor(gap[:, :], gap[:, :], tail_c[:, :], ALU.mult))
            go.step(nc.vector.tensor_scalar(K.tail_i[:, :], gap[:, :], float(N), None, ALU.add))
            nc.vector.tensor_copy(K.prev_last[:, 1:EDGE_TILES], K.dst_f[:, 0:EDGE_TILES - 1]).then_inc(pool_mask, 1)
            dve.wait_ge(pe_s, 2)
            go.step(nc.vector.memset(K.prev_b[:, :], -1.0))
            go.step(nc.vector.tensor_copy(K.prev_b[:, 1:EDGE_TILES], mlp0[0:D, 200:399]))
            for l in range(LAYERS):
                for k, s in ((0, 0), (1, 1), (2, 0)):
                    go.step(nc.vector.tensor_tensor(prod[:, :], K.w[l][:, :], att[l][s][:, :], ALU.mult))
                    go.step(nc.vector.tensor_reduce(K.w_att[l][:, k * H:(k + 1) * H],
                                                    prod[:, :].rearrange("p (h d) -> p h d", h=H), AX.X, ALU.add))
                go.step(nc.vector.tensor_scalar(K.w[l][:, :], K.w[l][:, :], 1.0 / H, None, ALU.mult))
                go.step(nc.vector.tensor_reduce(K.w_bar[l][:, :], K.w[l][:, :].rearrange("p (h d) -> p d h", h=H),
                                                AX.X, ALU.add))
            go.step(nc.vector.tensor_scalar(K.eps1[:, :], K.eps1[:, :], 1.0, None, ALU.add))
            go.step(nc.vector.tensor_scalar(b1p[:, :], K.b1[:, :], 0.0, None, ALU.max))
            nc.vector.tensor_copy(b1r[:, :, :], bc(b1p[:, :].unsqueeze(2), [D, 2, P])).then_inc(b1_ready, 1)
            dve.wait_ge(w_ready, 1)
            go.step(nc.vector.tensor_tensor(K.mlp_empty[:, :], mlp0[:, 0:D], K.b2b[:, :], ALU.add))

        @block.tensor
        def _(pe):
            pe.wait_ge(sel_ready, 2)
            pe.wait_ge(flags_ready, 4)
            nc.tensor.transpose(rows[0:1, 0:LANES], allf[:, :], K.eye[0:LANES, 0:LANES])
            for a in range(2):
                nc.tensor.transpose(rows[:, 200 + 100 * a:300 + 100 * a], rawf[2][:, a, :], K.eye[0:100, 0:100])
            nc.tensor.transpose(rows[0:1, LANES:2 * LANES], allb[:, :], K.eye[0:LANES, 0:LANES]).then_inc(pe_s, 1)
            for n in range(2):
                for a in range(2):
                    o = 200 * n + 100 * a
                    last = nc.tensor.transpose(cols[:, o:o + 100], rawf[n][:, a, :], K.eye[0:100, 0:100])
            last.then_inc(colsem, 1)
            pe.wait_ge(pool_mask, 1)
            nc.tensor.matmul(mlp0[0:D, 200:400], lhsT=pick[:, :], rhs=K.dst_f[:, :], start=True, stop=True).then_inc(pe_s, 1)
            pe.wait_ge(b1_ready, 1)
            for k in range(2):
                last = nc.tensor.matmul(mlp0[:, 0:D], lhsT=b1r[:, k, :], rhs=K.w2[:, k, :],
                                        start=(k == 0), stop=(k == 1))
            last.then_inc(w_ready, 1)


def dma_rows(eng, out, in_, sem):
    eng.dma_start(out[0:112], in_[0:112]).then_inc(sem, 16)
    eng.dma_start(out[112:P], in_[112:P]).then_inc(sem, 16)



class Layernorm:
    STEPS = 4

    def __init__(self, nc, st, name):
        self.nc = nc
        self.half = st.sb(f"{name}_half", [P, TILES, 6])
        self.msum, self.mdiff, self.var, self.dev, self.factor, self.shift = (
            st.sb(f"{name}_{n}", [P, TILES]) for n in ("msum", "mdiff", "var", "dev", "factor", "shift"))
        self.steps, self.spread, self.rooted, self.ready, self.normed = (
            st.sem(f"{name}_{n}") for n in ("steps", "spread", "rooted", "ready", "normed"))

    def statistics(self, dve, x, n):
        nc = self.nc
        for j in range(TILES):
            ins = nc.vector.bn_stats(self.half[:, j, :], x[:, j, :])
        ins.then_inc(self.steps, 1)
        wait(dve, self.steps, n * self.STEPS + 1)
        nc.vector.tensor_tensor(self.msum[:, :], self.half[:, :, 1], self.half[:, :, 4], ALU.add)
        nc.vector.tensor_tensor(self.var[:, :], self.half[:, :, 2], self.half[:, :, 5], ALU.add)
        nc.vector.tensor_tensor(self.mdiff[:, :], self.half[:, :, 1], self.half[:, :, 4],
                                ALU.subtract).then_inc(self.steps, 1)
        wait(dve, self.steps, n * self.STEPS + 2)
        nc.vector.tensor_tensor(self.mdiff[:, :], self.mdiff[:, :], self.mdiff[:, :], ALU.mult).then_inc(self.steps, 1)
        wait(dve, self.steps, n * self.STEPS + 3)
        nc.vector.scalar_tensor_tensor(self.var[:, :], self.mdiff[:, :], D / 4.0, self.var[:, :],
                                       ALU.mult, ALU.add).then_inc(self.spread, 1)

    def root(self, act, K, n):
        wait(act, self.spread, n + 1)
        self.nc.scalar.activation(self.dev[:, :], self.var[:, :], ACT.Sqrt, bias=K.eps[:, :],
                                  scale=1.0 / D).then_inc(self.rooted, 1)

    def factors(self, dve, n):
        nc = self.nc
        wait(dve, self.normed, n * GROUPS)
        wait(dve, self.rooted, n + 1)
        nc.vector.reciprocal(self.factor[:, :], self.dev[:, :]).then_inc(self.steps, 1)
        wait(dve, self.steps, n * self.STEPS + 4)
        nc.vector.scalar_tensor_tensor(self.shift[:, :], self.msum[:, :], -0.5, self.factor[:, :],
                                       ALU.mult, ALU.mult).then_inc(self.ready, 1)

    def apply_relu(self, act, x, out, n, groups):
        wait(act, self.ready, n + 1)
        for g in groups:
            for j in range(g * TG, (g + 1) * TG):
                ins = self.nc.scalar.activation(out[:, j, :], x[:, j, :], ACT.Relu, bias=self.shift[:, j:j + 1],
                                                scale=self.factor[:, j:j + 1])
            ins.then_inc(self.normed, 1)

    def apply(self, dve, x, out, n):
        wait(dve, self.ready, n + 1)
        for g in range(GROUPS):
            for j in range(g * TG, (g + 1) * TG):
                ins = self.nc.vector.tensor_scalar(out[:, j, :], x[:, j, :], self.factor[:, j:j + 1],
                                                   self.shift[:, j:j + 1], ALU.mult, ALU.add)
            ins.then_inc(self.normed, 1)


def flat(t):
    return t.rearrange("p j f -> p (j f)")


def first(c, at=0):
    return isinstance(c, int) and c <= at



def first_layer(nc, K, A):
    x_nodes = A["x"].rearrange("(c p j) f -> c p (j f)", c=CHUNKS, p=P)
    out0_nodes = K.out[0].rearrange("(c p j) f -> c p (j f)", c=CHUNKS, p=P)
    with Stage(nc, "first") as st:
        sb, pair, bank, sem, sems = st.sb, st.pair, st.bank, st.sem, st.sems
        NODE, EDGE = 0, 1
        x_in = pair("x_in", [P, TILES, D])
        pairs = pair("pairs", [P, TILES, D])
        rows_of = [x_in, pairs]
        norm = [pair("norm_node", [P, TILES, D]), pair("norm_edge", [P, TILES, D])]
        normT = [pair("normT_node", [D, COLS]), pair("normT_edge", [D, COLS])]
        ln = [Layernorm(nc, st, "ln_node"), Layernorm(nc, st, "ln_edge")]
        out_row = pair("out_row", [P, TILES * D])
        index = pair("index", [P, TILES], i32)
        turned = [bank(f"turned{k}") for k in range(4)]
        rows = [bank("rows0"), bank("rows1")]
        logit = [bank("logit0"), bank("logit1")]

        x_loaded, gathered = sems("x_loaded"), sems("gathered")
        raw_stored, hT_stored, rows_stored, gT_stored = (sems(n) for n in ("raw_stored", "hT_stored", "rows_stored", "gT_stored"))
        pool_go, index_ready, sp_go = (sem(n) for n in ("pool_go", "index_ready", "sp_go"))
        t_done, t_evac, rows_done, rows_evac = (sem(n) for n in ("t_done", "t_evac", "rows_done", "rows_evac"))
        logit_done, logit_evac = sem("logit_done"), sem("logit_evac")
        block = st.enter_context(nc.Block())

        @block.sync
        def _(sp):
            def store(c, b, i):
                wait(sp, gathered[b], i * (16 * TILES) + 16 * TILES)
                sp.sem_inc(sp_go, 1)
                dma_rows(sp, K.raw_pairs[c], flat(pairs[b][:, :, :]), raw_stored[b])
                wait(sp, t_evac, bank_no(c, NODE, GROUPS))
                sp.sem_inc(sp_go, 1)
                sp.dma_start(K.h0T[c], normT[NODE][b][:, :]).then_inc(hT_stored[b], 16)
                wait(sp, rows_evac, c * RGROUPS + RGROUPS)
                sp.sem_inc(sp_go, 1)
                dma_rows(sp, out0_nodes[c], out_row[b][:, :], rows_stored[b])
                wait(sp, t_evac, bank_no(c, EDGE, GROUPS))
                sp.sem_inc(sp_go, 1)
                sp.dma_start(K.pairT[0][c], normT[EDGE][b][:, :]).then_inc(gT_stored[b], 16)

            def body(c, b, i):
                wait(sp, ln[NODE].normed, c * GROUPS - GROUPS)
                sp.sem_inc(sp_go, 1)
                dma_rows(sp, flat(x_in[b][:, :, :]), x_nodes[c], x_loaded[b])
                if not first(c, 1):
                    store(c - 2, b, i - 1)

            over_chunks(sp, body)
            for b in range(2):
                store(CHUNKS - 2 + b, b, CHUNKS // 2 - 1)
            for b in range(2):
                for s, per in ((raw_stored, 32), (hT_stored, 16), (rows_stored, 32), (gT_stored, 16)):
                    sp.wait_ge(s[b], per * CHUNKS // 2)

        @block.gpsimd
        def _(pool):
            def body(c, b, i):
                wait(pool, ln[EDGE].normed, c * GROUPS - GROUPS)
                wait(pool, raw_stored[b], i * 32)
                wait(pool, gathered[b], i * (16 * TILES))
                pool.sem_inc(pool_go, 1)
                pool.tensor_copy(index[b][:, 0:ET], K.src_i[:, bass.ds(c * ET, ET)]).then_inc(index_ready, 1)
                pool.tensor_copy(index[b][:, ET:TILES], K.dst_i[:, bass.ds(c * ET, ET)]).then_inc(index_ready, 1)
                pool.wait_ge(index_ready, c * 2 + 2)
                pool.sem_inc(pool_go, 1)
                for j in range(TILES):
                    pool.indirect_dma_start(pairs[b][:, j, :], None, A["x"],
                                            bass.IndirectOffsetOnAxis(index[b][:, j:j + 1], 0)).then_inc(gathered[b], 16)

            over_chunks(pool, body)

        @block.vector
        def _(dve):
            def normalise(kind, c, b):
                ln[kind].factors(dve, c)
                wait(dve, t_done, bank_no(c - 2, kind, GROUPS))
                ln[kind].apply(dve, rows_of[kind][b], norm[kind][b], c)

            def body(c, b, i):
                wait(dve, x_loaded[b], i * 32 + 32)
                ln[NODE].statistics(dve, x_in[b], c)
                if not first(c):
                    normalise(EDGE, c - 1, 1 - b)
                wait(dve, gathered[b], i * (16 * TILES) + 16 * TILES)
                ln[EDGE].statistics(dve, pairs[b], c)
                normalise(NODE, c, b)

            over_chunks(dve, body)
            normalise(EDGE, CHUNKS - 1, 1)

        @block.scalar
        def _(act):
            def evacuate(kind, c, b, i):
                stored = (hT_stored, gT_stored)[kind]
                wait(act, stored[b], i * 16)
                if kind == NODE:
                    wait(act, rows_done, c * RGROUPS - RGROUPS)
                else:
                    wait(act, logit_done, c - 1)
                for g in range(GROUPS):
                    wait(act, t_done, bank_no(c, kind, g + 1))
                    nc.scalar.activation(normT[kind][b][:, g * TG * P:(g + 1) * TG * P],
                                         turned[turn_bank(b, kind, g)][0:D, 0:TG * P], ACT.Relu).then_inc(t_evac, 1)

            def logits(c, b):
                wait(act, logit_done, c + 1)
                nc.scalar.copy(K.logits[:, :, bass.ds(c * ET, ET)],
                               logit[b][0:P, 0:3 * H * ET].rearrange("p (k j) -> p k j", j=ET)).then_inc(logit_evac, 1)

            def body(c, b, i):
                ln[NODE].root(act, K, c)
                if not first(c):
                    evacuate(EDGE, c - 1, 1 - b, i if b else i - 1)
                ln[EDGE].root(act, K, c)
                evacuate(NODE, c, b, i)
                if not first(c):
                    logits(c - 1, 1 - b)
                wait(act, rows_stored[b], i * 32)
                for k in range(RGROUPS):
                    wait(act, rows_done, c * RGROUPS + (k + 1))
                    nc.scalar.copy(out_row[b][:, k * RG * D:(k + 1) * RG * D], rows[k % 2][0:P, 0:RG * D]).then_inc(rows_evac, 1)

            over_chunks(act, body)
            evacuate(EDGE, CHUNKS - 1, 1, CHUNKS // 2 - 1)
            logits(CHUNKS - 1, 1)

        @block.tensor
        def _(pe):
            def turn(kind, c, b):
                for g in range(GROUPS):
                    wait(pe, ln[kind].normed, c * GROUPS + (g + 1))
                    turn_group(nc, K, pe, kind, c, b, g, norm[kind][b], turned, t_evac, t_done)

            def logits(c, b):
                edge_logits(nc, K, pe, 0, c, b, normT[EDGE][b], logit[b], t_evac, bank_no(c, EDGE, GROUPS),
                            logit_evac, logit_done)

            def body(c, b, i):
                if not first(c):
                    turn(EDGE, c - 1, 1 - b)
                turn(NODE, c, b)
                if not first(c):
                    logits(c - 1, 1 - b)
                dense_rows(nc, K, pe, 0, c, b, normT[NODE][b], rows, t_evac, lambda g: bank_no(c, NODE, g + 1),
                           rows_evac, rows_done)

            over_chunks(pe, body)
            turn(EDGE, CHUNKS - 1, 1)
            logits(CHUNKS - 1, 1)


def bank_no(c, kind, g):
    return c * (2 * GROUPS) + (kind * GROUPS + g)


def turn_bank(b, kind, g):
    return (2 * b + kind * GROUPS + g) % 4


def turn_group(nc, K, pe, kind, c, b, g, rows, turned, t_evac, t_done):
    wait(pe, t_evac, bank_no(c, kind, g) - 3)
    for k in range(TG):
        last = nc.tensor.transpose(turned[turn_bank(b, kind, g)][0:D, k * P:(k + 1) * P],
                                   rows[:, g * TG + k, :], K.eye[:, :])
    last.then_inc(t_done, 1)


def dense_rows(nc, K, pe, l, c, b, xT, rows, ready, ready_count, rows_evac, rows_done):
    seen = -1
    for k in range(RGROUPS):
        need = ((k + 1) * RG - 1) // TG
        if need > seen:
            wait(pe, ready, ready_count(need))
            seen = need
        wait(pe, rows_evac, c * RGROUPS + (k - 1))
        for r in range(RG):
            j = k * RG + r
            last = nc.tensor.matmul(rows[k % 2][0:P, r * D:(r + 1) * D], lhsT=xT[:, j * P:(j + 1) * P],
                                    rhs=K.w_bar[l][:, :], start=True, stop=True)
        last.then_inc(rows_done, 1)


def edge_logits(nc, K, pe, l, c, b, xT, out, ready, ready_count, logit_evac, logit_done):
    wait(pe, ready, ready_count)
    wait(pe, logit_evac, c - 1)
    cols = out[0:P, 0:3 * H * ET].rearrange("p (k j) -> p k j", j=ET)
    for j in range(ET):
        nc.tensor.matmul(cols[:, 0:H, j], lhsT=xT[:, j * P:(j + 1) * P], rhs=K.w_att[l][:, 0:H], start=True, stop=True)
        last = nc.tensor.matmul(cols[:, H:3 * H, j], lhsT=xT[:, (ET + j) * P:(ET + j + 1) * P],
                                rhs=K.w_att[l][:, H:3 * H], start=True, stop=True)
    last.then_inc(logit_done, 1)



def edge_softmax(nc, K, l):
    with Stage(nc, f"softmax{l}") as st:
        sb, pair, bank, sem, sems = st.sb, st.pair, st.bank, st.sem, st.sems
        LE = (LANES, EDGES_C)
        lane = [sb(f"lane{k}", LE) for k in range(3)]
        edge, own, work, scan, run_max, run_sum = (sb(n, LE) for n in ("edge", "own", "work", "scan", "run_max", "run_sum"))
        prob, own_prob = sb("prob", LE), sb("own_prob", LE)
        ends, links, start = sb("ends", (1, LANES)), sb("links", (1, LANES + 1)), sb("start", (LANES, 1))
        turned = [bank("turned0"), bank("turned1")]
        link_row, link_col = bank("link_row"), bank("link_col")
        turn_done, turn_used, steps = sem("turn_done"), sem("turn_used"), sem("dve_steps")
        ends_ready, row_done, links_ready, col_done = (sem(n) for n in ("ends_ready", "row_done", "links_ready", "col_done"))
        shifted, probs, alpha_ready, back_done, back_used = (sem(n) for n in ("shifted", "probs", "alpha_ready", "back_done", "back_used"))
        sp_go = sem("sp_go")
        block = st.enter_context(nc.Block())
        FOUR = (4, 4, 2)
        SCANS = 5

        @block.tensor
        def _(pe):
            n = 0
            for k in range(3):
                j = 0
                for cnt in FOUR:
                    wait(pe, turn_used, n - 1)
                    for q in range(cnt):
                        last = nc.tensor.transpose(turned[n % 2][0:LANES, q * P:(q + 1) * P],
                                                   K.logits[:, k * H:(k + 1) * H, :].rearrange(
                                                       "p h (b j) -> p (h b) j", j=ET)[:, :, j + q], K.eye[:, :])
                    last.then_inc(turn_done, 1)
                    j += cnt
                    n += 1
            for s in range(SCANS):
                forward = s in (1, 3)
                pe.wait_ge(ends_ready, s + 1)
                at = EDGES_C - 1 if forward else 0
                nc.tensor.transpose(link_row[0:1, 0:LANES], scan[:, at:at + 1], K.eye[0:LANES, 0:LANES]).then_inc(row_done, 1)
                pe.wait_ge(links_ready, s + 1)
                off = 0 if forward else 1
                nc.tensor.transpose(link_col[0:LANES, 0:1], links[0:1, off:off + LANES], K.eye[0:1, 0:1]).then_inc(col_done, 1)
            pe.wait_ge(alpha_ready, 1)
            for k, lanes in enumerate((prob, own_prob)):
                for half in range(2):
                    m = 2 * k + half
                    wait(pe, back_used, m - 1)
                    for q in range(5):
                        j = half * 5 + q
                        last = nc.tensor.transpose((link_row, link_col)[m % 2][0:P, q * LANES:(q + 1) * LANES],
                                                   lanes[:, j * P:(j + 1) * P], K.eye[0:LANES, 0:LANES])
                    last.then_inc(back_done, 1)

        @block.scalar
        def _(act):
            n = 0
            for k in range(3):
                j = 0
                for cnt in FOUR:
                    act.wait_ge(turn_done, n + 1)
                    nc.scalar.copy(lane[k][:, j * P:(j + cnt) * P], turned[n % 2][0:LANES, 0:cnt * P]).then_inc(turn_used, 1)
                    j += cnt
                    n += 1
            for m, (out, in_) in enumerate(((prob, edge), (own_prob, own))):
                act.wait_ge(shifted, m + 1)
                nc.scalar.activation(out[:, :], in_[:, :], ACT.Exp).then_inc(probs, 1)
            for m in range(4):
                act.wait_ge(back_done, m + 1)
                half = m % 2
                dst = K.alpha[:, m // 2, :, :].rearrange("p l j -> p j l")[:, half * 5:half * 5 + 5, :]
                nc.scalar.copy(dst, (link_row, link_col)[m % 2][0:P, 0:5 * LANES].rearrange("p (j l) -> p j l", j=5)).then_inc(back_used, 1)

        @block.vector
        def _(dve):
            go = Line(dve, steps)
            scans = [0]

            def run_scan(out, keep, data, block_keep, forward, op0, op1, none):
                r = slice(None) if forward else slice(None, None, -1)
                init = none
                for again in range(2):
                    ins = nc.vector.tensor_tensor_scan(out[:, r], keep[:, r], data[:, r], init, op0, op1)
                    if again:
                        go.step(ins)
                        break
                    ins.then_inc(ends_ready, 1)
                    scans[0] += 1
                    n = scans[0]
                    dve.wait_ge(row_done, n)
                    go.step(nc.vector.tensor_copy(ends[:, :], link_row[0:1, 0:LANES]))
                    edge_at, body = (0, slice(1, LANES + 1)) if forward else (LANES, slice(0, LANES))
                    go.step(nc.vector.memset(links[0:1, edge_at:edge_at + 1], none))
                    nc.vector.tensor_tensor_scan(links[0:1, body][:, r], block_keep[0:1, r], ends[0:1, r], none,
                                                 op0, op1).then_inc(links_ready, 1)
                    dve.wait_ge(col_done, n)
                    go.step(nc.vector.tensor_copy(start[:, :], link_col[0:LANES, 0:1]))
                    init = start[:, 0:1]

            def from_tails(out, data):
                go.step(nc.vector.tensor_tensor(work[:, :], K.tail[:, :], data[:, :], ALU.mult))
                run_scan(scan, K.cont_b, work, K.all_b, False, ALU.mult, ALU.add, 0.0)

            dve.wait_ge(turn_used, 9)
            from_tails(scan, lane[1])
            for out, part in ((edge, 0), (own, 2)):
                go.step(nc.vector.tensor_tensor(work[:, :], lane[part][:, :], scan[:, :], ALU.add))
                go.step(nc.vector.scalar_tensor_tensor(out[:, :], work[:, :], SLOPE, work[:, :], ALU.mult, ALU.max))
            go.step(nc.vector.scalar_tensor_tensor(own[:, :], K.cont_b[:, :], -BIG, own[:, :], ALU.mult, ALU.add))
            go.step(nc.vector.tensor_tensor(run_max[:, :], edge[:, :], own[:, :], ALU.max))
            run_scan(scan, K.pen_f, run_max, K.all_pen, True, ALU.add, ALU.max, -BIG)
            from_tails(scan, scan)
            nc.vector.tensor_tensor(edge[:, :], edge[:, :], scan[:, :], ALU.subtract).then_inc(shifted, 1)
            nc.vector.tensor_tensor(own[:, :], own[:, :], scan[:, :], ALU.subtract).then_inc(shifted, 1)
            dve.wait_ge(probs, 2)
            go.step(nc.vector.tensor_tensor(run_sum[:, :], prob[:, :], own_prob[:, :], ALU.add))
            run_scan(scan, K.cont_f, run_sum, K.all_f, True, ALU.mult, ALU.add, 0.0)
            from_tails(scan, scan)
            go.step(nc.vector.tensor_scalar(scan[:, :], scan[:, :], TINY, None, ALU.add))
            go.step(nc.vector.reciprocal(work[:, :], scan[:, :]))
            go.step(nc.vector.tensor_tensor(prob[:, :], prob[:, :], work[:, :], ALU.mult))
            nc.vector.tensor_tensor(own_prob[:, :], own_prob[:, :], work[:, :], ALU.mult).then_inc(alpha_ready, 1)



def aggregate(nc, K, l):
    V = H * D
    with Stage(nc, f"aggr{l}") as st:
        sb, pair, bank, sem, sems = st.sb, st.pair, st.bank, st.sem, st.sems
        xT = pair("xT", [D, COLS])
        dst_row = pair("dst_row", [P, ET, P], i32)
        same = pair("same", [P, ET, P])
        carry = pair("carry", [P, ET, P])
        alpha = pair("alpha_c", [P, 2 * H, ET])
        index = pair("index", [P, ET], i32)
        prod = [sb(f"prod{k}", [P, 2 * H, D]) for k in range(4)]
        part = [sb(f"part{k}", [P, D]) for k in range(4)]
        out_row = pair("out_row", [P, ET, D])
        src_v = [bank("src_v0"), bank("src_v1")]
        dst_v = [bank("dst_v0"), bank("dst_v1")]
        sums = [bank("sums0"), bank("sums1")]

        loaded, row_loaded, stored, scattered = (sems(n) for n in ("loaded", "row_loaded", "stored", "scattered"))
        masks_ready, alpha_ready, src_done, dst_done, src_prod, dst_prod, part_ready, sums_done, out_evac = (
            sem(n) for n in ("masks_ready", "alpha_ready", "src_done", "dst_done", "src_prod", "dst_prod",
                             "part_ready", "sums_done", "out_evac"))
        pool_go, index_ready, blank, sp_go = (sem(n) for n in ("pool_go", "index_ready", "blank", "sp_go"))
        block = st.enter_context(nc.Block())

        @block.sync
        def _(sp):
            def store(c, b):
                wait(sp, out_evac, c * ET + ET)
                sp.sem_inc(sp_go, 1)
                dma_rows(sp, K.out_pairs[l][c], flat(out_row[b][:, :, :]), stored[b])

            def body(c, b, i):
                wait(sp, dst_done, (c - 1) * ET)
                sp.sem_inc(sp_go, 1)
                sp.dma_start(xT[b][:, :], K.pairT[l][c]).then_inc(loaded[b], 16)
                wait(sp, masks_ready, (c - 1) * (ET // 2))
                sp.sem_inc(sp_go, 1)
                sp.dma_start(dst_row[b][:, :, :].rearrange("p j e -> p (j e)"),
                             bc(K.dst_rows[c].unsqueeze(0), [P, EDGES_C])).then_inc(row_loaded[b], 16)
                if not first(c):
                    store(c - 1, 1 - b)

            over_chunks(sp, body)
            store(CHUNKS - 1, 1)
            for b in range(2):
                sp.wait_ge(stored[b], 32 * CHUNKS // 2)

        def place(b, j):
            return (b * ET + j) % 4

        @block.gpsimd
        def _(pool):
            def scatter(c, b, i):
                wait(pool, scattered[b], i * (16 * ET))
                pool.sem_inc(pool_go, 1)
                pool.tensor_copy(index[b][:, :], K.tail_i[:, bass.ds(c * ET, ET)]).then_inc(index_ready, 1)
                pool.wait_ge(index_ready, c + 1)
                for j in range(ET):
                    wait(pool, out_evac, c * ET + (j + 1))
                    pool.sem_inc(pool_go, 1)
                    pool.indirect_dma_start(K.out[l][:, :], bass.IndirectOffsetOnAxis(index[b][:, j:j + 1], 0),
                                            out_row[b][:, j, :], None, bounds_check=N - 1,
                                            oob_is_err=False).then_inc(scattered[b], 16)

            def body(c, b, i):
                if not first(c):
                    scatter(c - 1, 1 - b, i if b else i - 1)

            over_chunks(pool, body)
            scatter(CHUNKS - 1, 1, CHUNKS // 2 - 1)
            for b in range(2):
                pool.wait_ge(scattered[b], 16 * ET * CHUNKS // 2)

        @block.vector
        def _(dve):
            nc.vector.memset(out_row[1][:, ET - 1, :], 0.0).then_inc(blank, 1)

            def add_heads(c, b, j):
                q = place(b, j)
                wait(dve, src_prod, c * ET + (j + 1))
                wait(dve, dst_prod, c * ET + (j + 1))
                wait(dve, sums_done, c * ET + (j - 3))
                nc.vector.tensor_reduce(part[q][:, :], prod[q][:, :, :].rearrange("p k f -> p f k"),
                                        AX.X, ALU.add).then_inc(part_ready, 1)

            def masks(c, b, j):
                rows, at = dst_row[b][:, j:j + 2, :], bass.ds(c * ET + j, 2)
                nc.vector.tensor_tensor(same[b][:, j:j + 2, :], rows,
                                        bc(K.dst_f[:, at].unsqueeze(2), [P, 2, P]), ALU.is_equal)
                nc.vector.tensor_tensor(carry[b][:, j:j + 2, :], rows,
                                        bc(K.prev_last[:, at].unsqueeze(2), [P, 2, P]), ALU.is_equal).then_inc(masks_ready, 1)

            def body(c, b, i):
                wait(dve, src_prod, (c - 1) * ET)
                wait(dve, dst_prod, (c - 1) * ET)
                nc.vector.tensor_copy(alpha[b][:, :, :], K.alpha_flat[:, :, bass.ds(c * ET, ET)]).then_inc(alpha_ready, 1)
                wait(dve, alpha_ready, c + 1)
                for j in range(ET):
                    s, q = j % 2, place(b, j)
                    wait(dve, src_done, c * ET + (j + 1))
                    wait(dve, part_ready, c * ET + (j - 3))
                    nc.vector.tensor_tensor(prod[q][:, 0:H, :], src_v[s][0:P, 0:V].rearrange("p (h f) -> p h f", h=H),
                                            bc(alpha[b][:, 0:H, j].unsqueeze(2), [P, H, D]), ALU.mult).then_inc(src_prod, 1)
                    if j or not first(c):
                        add_heads(*earlier(c, b, j, 1))
                    if j == 0:
                        wait(dve, row_loaded[b], i * 16 + 16)
                        wait(dve, sums_done, (c - 1) * ET)
                    if j % 2 == 0:
                        masks(c, b, j)

            dve.wait_ge(blank, 1)
            over_chunks(dve, body)
            add_heads(CHUNKS - 1, 1, ET - 1)

        @block.scalar
        def _(act):
            def out(c, b, j, i):
                if j == 0:
                    wait(act, stored[b], i * 32)
                    wait(act, scattered[b], i * (16 * ET))
                wait(act, sums_done, c * ET + (j + 1))
                nc.scalar.copy(out_row[b][:, j, :], sums[j % 2][0:P, 0:D]).then_inc(out_evac, 1)

            def body(c, b, i):
                wait(act, alpha_ready, c + 1)
                for j in range(ET):
                    s, q = j % 2, place(b, j)
                    wait(act, dst_done, c * ET + (j + 1))
                    wait(act, part_ready, c * ET + (j - 3))
                    for h in range(H):
                        last = nc.scalar.activation(prod[q][:, H + h, :], dst_v[s][0:P, h * D:(h + 1) * D], ACT.Copy,
                                                    scale=alpha[b][:, H + h, j:j + 1])
                    last.then_inc(dst_prod, 1)
                    if j >= 2 or not first(c):
                        out(*earlier(c, b, j, 2), i)

            act.wait_ge(blank, 1)
            over_chunks(act, body)
            for j in (ET - 2, ET - 1):
                out(CHUNKS - 1, 1, j, None)

        @block.tensor
        def _(pe):
            def run_sums(c, b, j):
                s, q = j % 2, place(b, j)
                if j % 2 == 0:
                    wait(pe, masks_ready, c * (ET // 2) + (j // 2 + 1))
                wait(pe, part_ready, c * ET + (j + 1))
                wait(pe, out_evac, c * ET + (j - 1))
                nc.tensor.matmul(sums[s][0:P, 0:D], lhsT=same[b][:, j, :], rhs=part[q][:, :], start=True, stop=False)
                wait(pe, out_evac, c * ET + j)
                before = out_row[b][:, j - 1, :] if j else out_row[1 - b][:, ET - 1, :]
                nc.tensor.matmul(sums[s][0:P, 0:D], lhsT=carry[b][:, j, :], rhs=before,
                                 start=False, stop=True).then_inc(sums_done, 1)

            def body(c, b, i):
                wait(pe, loaded[b], i * 16 + 16)
                for j in range(ET):
                    s = j % 2
                    wait(pe, src_prod, c * ET + (j - 1))
                    nc.tensor.matmul(src_v[s][0:P, 0:V], lhsT=xT[b][:, j * P:(j + 1) * P], rhs=K.w[l][:, :],
                                     start=True, stop=True).then_inc(src_done, 1)
                    wait(pe, dst_prod, c * ET + (j - 1))
                    nc.tensor.matmul(dst_v[s][0:P, 0:V], lhsT=xT[b][:, (ET + j) * P:(ET + j + 1) * P], rhs=K.w[l][:, :],
                                     start=True, stop=True).then_inc(dst_done, 1)
                    if j >= 2 or not first(c):
                        run_sums(*earlier(c, b, j, 2))

            pe.wait_ge(blank, 1)
            over_chunks(pe, body)
            for j in (ET - 2, ET - 1):
                run_sums(CHUNKS - 1, 1, j)



def batch_norm(nc, K, l):
    nodes = K.out[l].rearrange("(c p j) f -> c p (j f)", c=CHUNKS, p=P)
    BANKS = 8
    with Stage(nc, f"norm{l}") as st:
        sb, pair, bank, sem, sems = st.sb, st.pair, st.bank, st.sem, st.sems
        row = [sb(f"row{k}", [P, TILES, D]) for k in range(2)]
        stats = sb("stats", [D, CHUNKS * GROUPS, 6])
        mv = sb("mv", (D, 2))
        mean, root, rroot = (sb(n, (D, 1)) for n in ("mean", "root", "rroot"))
        turned = [bank(f"turned{k}") for k in range(BANKS)]
        loaded = sems("loaded")
        t_done, t_used, steps, var_ready, root_ready, sp_go = (
            sem(n) for n in ("t_done", "t_used", "steps", "var_ready", "root_ready", "sp_go"))
        block = st.enter_context(nc.Block())

        @block.sync
        def _(sp):
            def body(c, b, i):
                wait(sp, t_done, (c - 1) * GROUPS)
                sp.sem_inc(sp_go, 1)
                dma_rows(sp, flat(row[b][:, :, :]), nodes[c], loaded[b])

            over_chunks(sp, body)

        def place(b, g):
            return 4 * b + g % 4

        @block.tensor
        def _(pe):
            def body(c, b, i):
                wait(pe, loaded[b], i * 32 + 32)
                for g in range(GROUPS):
                    wait(pe, t_used, c * GROUPS + (1 if g == 4 else g + 1 - 2 * GROUPS if g else 5 - 2 * GROUPS))
                    for k in range(TG):
                        last = nc.tensor.transpose(turned[place(b, g)][0:D, k * P:(k + 1) * P],
                                                   row[b][:, g * TG + k, :], K.eye[:, :])
                    last.then_inc(t_done, 1)

            over_chunks(pe, body)

        @block.scalar
        def _(act):
            act.wait_ge(var_ready, 1)
            nc.scalar.activation(root[:, :], mv[:, 1:2], ACT.Sqrt, bias=K.eps[0:D, :]).then_inc(root_ready, 1)

        @block.vector
        def _(dve):
            def body(c, b, i):
                for g in range(GROUPS):
                    wait(dve, t_done, c * GROUPS + (g + 1))
                    nc.vector.bn_stats(stats[:, bass.ds(c * GROUPS + g, 1), :].rearrange("p a s -> p (a s)"),
                                       turned[place(b, g)][0:D, 0:TG * P]).then_inc(t_used, 1)

            over_chunks(dve, body)
            dve.wait_ge(t_used, CHUNKS * GROUPS)
            nc.vector.bn_aggr(mv[:, :], stats[:, :, :].rearrange("p a s -> p (a s)")).then_inc(var_ready, 1)
            go = Line(dve, steps)
            dve.wait_ge(root_ready, 1)
            go.step(nc.vector.reciprocal(rroot[:, :], root[:, :]))
            go.step(nc.vector.tensor_tensor(K.scale[l][:, :], K.gamma[l][:, :], rroot[:, :], ALU.mult))
            go.step(nc.vector.tensor_tensor(mean[:, :], mv[:, 0:1], K.bias[l][:, :], ALU.add))
            go.step(nc.vector.tensor_tensor(mean[:, :], K.bias[l][:, :], mean[:, :], ALU.subtract))
            go.step(nc.vector.scalar_tensor_tensor(K.shift[l][:, :], mean[:, :], K.scale[l][:, :], K.beta[l][:, :],
                                                   ALU.mult, ALU.add))



def second_layer(nc, K, A):
    out0_nodes = K.out[0].rearrange("(c p j) f -> c p (j f)", c=CHUNKS, p=P)
    out1_nodes = K.out[1].rearrange("(c p j) f -> c p (j f)", c=CHUNKS, p=P)
    NODE, EDGE = 0, 1
    with Stage(nc, "second") as st:
        sb, pair, bank, sem, sems = st.sb, st.pair, st.bank, st.sem, st.sems
        row = [pair("row_node", [P, TILES, D]), pair("row_edge", [P, TILES, D])]
        resT = [pair("resT_node", [D, COLS]), pair("resT_edge", [D, COLS])]
        actT = [sb("actT_node", [D, COLS]), sb("actT_edge", [D, COLS])]
        out_row = pair("out_row", [P, TILES * D])
        index = pair("index", [P, ET], i32)
        turned = [bank(f"turned{k}") for k in range(4)]
        rows = [bank("rows0"), bank("rows1")]
        logit = [bank("logit0"), bank("logit1")]
        row_loaded = [sems("row_node_in"), sems("row_edge_in")]
        res_loaded = [sems("res_node_in"), sems("res_edge_in")]
        res_stored = [sems("res_node_out"), sems("res_edge_out")]
        gathered, rows_stored = sems("gathered"), sems("rows_stored")
        pool_go, index_ready, sp_go = sem("pool_go"), sem("index_ready"), sem("sp_go")
        t_done, t_evac, rows_done, rows_evac = (sem(n) for n in ("t_done", "t_evac", "rows_done", "rows_evac"))
        added = [sem("added_node"), sem("added_edge")]
        logit_done, logit_evac = sem("logit_done"), sem("logit_evac")
        block = st.enter_context(nc.Block())

        @block.sync
        def _(sp):
            def load(c, b, i):
                wait(sp, t_done, bank_no(c - 2, NODE, GROUPS))
                sp.sem_inc(sp_go, 1)
                dma_rows(sp, flat(row[NODE][b][:, :, :]), out0_nodes[c], row_loaded[NODE][b])
                wait(sp, res_stored[NODE][b], i * 16)
                sp.sem_inc(sp_go, 1)
                wait(sp, rows_done, c * RGROUPS - RGROUPS)
                sp.sem_inc(sp_go, 1)
                sp.dma_start(resT[NODE][b][:, :], K.h0T[c]).then_inc(res_loaded[NODE][b], 16)
                wait(sp, t_done, bank_no(c - 2, EDGE, GROUPS))
                sp.sem_inc(sp_go, 1)
                dma_rows(sp, flat(row[EDGE][b][:, ET:TILES, :]), K.out_pairs[0][c], row_loaded[EDGE][b])
                wait(sp, res_stored[EDGE][b], i * 16)
                sp.sem_inc(sp_go, 1)
                wait(sp, logit_done, c - 1)
                sp.sem_inc(sp_go, 1)
                sp.dma_start(resT[EDGE][b][:, :], K.pairT[0][c]).then_inc(res_loaded[EDGE][b], 16)

            def store(c, b):
                wait(sp, added[NODE], c + 1)
                sp.sem_inc(sp_go, 1)
                sp.dma_start(K.x1T[c], resT[NODE][b][:, :]).then_inc(res_stored[NODE][b], 16)
                wait(sp, added[EDGE], c + 1)
                sp.sem_inc(sp_go, 1)
                sp.dma_start(K.pairT[1][c], resT[EDGE][b][:, :]).then_inc(res_stored[EDGE][b], 16)
                wait(sp, rows_evac, c * RGROUPS + RGROUPS)
                sp.sem_inc(sp_go, 1)
                dma_rows(sp, out1_nodes[c], out_row[b][:, :], rows_stored[b])

            def body(c, b, i):
                load(c, b, i)
                if not first(c):
                    store(c - 1, 1 - b)

            over_chunks(sp, body)
            store(CHUNKS - 1, 1)
            for b in range(2):
                sp.wait_ge(res_stored[NODE][b], 16 * CHUNKS // 2)
                sp.wait_ge(res_stored[EDGE][b], 16 * CHUNKS // 2)
                sp.wait_ge(rows_stored[b], 32 * CHUNKS // 2)

        @block.gpsimd
        def _(pool):
            def body(c, b, i):
                wait(pool, gathered[b], i * (16 * ET))
                wait(pool, t_done, bank_no(c - 2, EDGE, GROUPS))
                pool.sem_inc(pool_go, 1)
                pool.tensor_copy(index[b][:, :], K.src_i[:, bass.ds(c * ET, ET)]).then_inc(index_ready, 1)
                pool.wait_ge(index_ready, c + 1)
                pool.sem_inc(pool_go, 1)
                for j in range(ET):
                    pool.indirect_dma_start(row[EDGE][b][:, j, :], None, K.out[0][:, :],
                                            bass.IndirectOffsetOnAxis(index[b][:, j:j + 1], 0)).then_inc(gathered[b], 16)

            over_chunks(pool, body)

        @block.tensor
        def _(pe):
            def turn(kind, c, b, i):
                wait(pe, row_loaded[kind][b], i * 32 + 32)
                if kind == EDGE:
                    wait(pe, gathered[b], i * (16 * ET) + 16 * ET)
                for g in range(GROUPS):
                    turn_group(nc, K, pe, kind, c, b, g, row[kind][b], turned, t_evac, t_done)

            def body(c, b, i):
                turn(NODE, c, b, i)
                turn(EDGE, c, b, i)
                dense_rows(nc, K, pe, 1, c, b, resT[NODE][b], rows, added[NODE], lambda g: c + 1, rows_evac, rows_done)
                edge_logits(nc, K, pe, 1, c, b, resT[EDGE][b], logit[b], added[EDGE], c + 1, logit_evac, logit_done)

            over_chunks(pe, body)

        @block.scalar
        def _(act):
            def affine_relu(kind, c, b):
                wait(act, added[kind], c)
                for g in range(GROUPS):
                    wait(act, t_done, bank_no(c, kind, g + 1))
                    nc.scalar.activation(actT[kind][:, g * TG * P:(g + 1) * TG * P],
                                         turned[turn_bank(b, kind, g)][0:D, 0:TG * P], ACT.Relu,
                                         bias=K.shift[0][:, :], scale=K.scale[0][:, :]).then_inc(t_evac, 1)

            def body(c, b, i):
                affine_relu(NODE, c, b)
                affine_relu(EDGE, c, b)
                wait(act, rows_stored[b], i * 32)
                for k in range(RGROUPS):
                    wait(act, rows_done, c * RGROUPS + (k + 1))
                    nc.scalar.copy(out_row[b][:, k * RG * D:(k + 1) * RG * D], rows[k % 2][0:P, 0:RG * D]).then_inc(rows_evac, 1)
                wait(act, logit_done, c + 1)
                nc.scalar.copy(K.logits[:, :, bass.ds(c * ET, ET)],
                               logit[b][0:P, 0:3 * H * ET].rearrange("p (k j) -> p k j", j=ET)).then_inc(logit_evac, 1)

            over_chunks(act, body)

        @block.vector
        def _(dve):
            def body(c, b, i):
                for kind in (NODE, EDGE):
                    wait(dve, res_loaded[kind][b], i * 16 + 16)
                    wait(dve, t_evac, bank_no(c, kind, GROUPS))
                    nc.vector.tensor_tensor(resT[kind][b][:, :], resT[kind][b][:, :], actT[kind][:, :],
                                            ALU.add).then_inc(added[kind], 1)

            over_chunks(dve, body)



def last_bank(c, g):
    return c * GROUPS + (0, 2 - GROUPS, 3 - GROUPS, 4 - GROUPS, 1)[g]


def third_nodes(nc, K, A):
    x_nodes = A["x"].rearrange("(c p j) f -> c p (j f)", c=CHUNKS, p=P)
    out1_nodes = K.out[1].rearrange("(c p j) f -> c p (j f)", c=CHUNKS, p=P)
    y_nodes = K.y.rearrange("(c p j) f -> c p (j f)", c=CHUNKS, p=P)
    with Stage(nc, "nodes") as st:
        sb, pair, bank, sem, sems = st.sb, st.pair, st.bank, st.sem, st.sems
        row, xrow = pair("row", [P, TILES, D]), pair("xrow", [P, TILES, D])
        resT = pair("resT", [D, COLS])
        actT = sb("actT", [D, COLS])
        ysum, norm, final = (pair(n, [P, TILES, D]) for n in ("ysum", "norm", "final"))
        ln = Layernorm(nc, st, "ln")
        src_row = pair("src_row", [P, ET, D])
        index = pair("index", [P, ET], i32)
        turned = [bank(f"turned{k}") for k in range(4)]
        yp = [bank(f"yp{k}") for k in range(4)]
        row_in, res_in, x_in, y_out, gathered, src_out = (
            sems(n) for n in ("row_in", "res_in", "x_in", "y_out", "gathered", "src_out"))
        t_done, t_evac, added, y_done, y_evac, relu_done, final_half, final_ready, pool_go, index_ready, sp_go = (
            sem(n) for n in ("t_done", "t_evac", "added", "y_done", "y_evac", "relu_done", "final_half", "final_ready",
                             "pool_go", "index_ready", "sp_go"))
        block = st.enter_context(nc.Block())

        @block.sync
        def _(sp):
            def store(c, b):
                wait(sp, final_ready, c + 1)
                sp.sem_inc(sp_go, 1)
                dma_rows(sp, y_nodes[c], flat(final[b][:, :, :]), y_out[b])

            def store_src(c, b, i):
                wait(sp, gathered[b], i * (16 * ET) + 16 * ET)
                sp.sem_inc(sp_go, 1)
                dma_rows(sp, K.src_rows[c], flat(src_row[b][:, :, :]), src_out[b])

            def body(c, b, i):
                wait(sp, t_done, (c - 1) * GROUPS)
                sp.sem_inc(sp_go, 1)
                dma_rows(sp, flat(row[b][:, :, :]), out1_nodes[c], row_in[b])
                wait(sp, y_done, (c - 1) * RGROUPS)
                sp.sem_inc(sp_go, 1)
                sp.dma_start(resT[b][:, :], K.x1T[c]).then_inc(res_in[b], 16)
                dma_rows(sp, flat(xrow[b][:, :, :]), x_nodes[c], x_in[b])
                if not first(c):
                    store_src(c - 1, 1 - b, i if b else i - 1)
                if not first(c, 1):
                    store(c - 2, b)

            over_chunks(sp, body)
            store_src(CHUNKS - 1, 1, CHUNKS // 2 - 1)
            for c in (CHUNKS - 2, CHUNKS - 1):
                store(c, c % 2)
            for b in range(2):
                sp.wait_ge(y_out[b], 32 * CHUNKS // 2)
                sp.wait_ge(src_out[b], 32 * CHUNKS // 2)

        @block.gpsimd
        def _(pool):
            def body(c, b, i):
                wait(pool, src_out[b], i * 32)
                pool.sem_inc(pool_go, 1)
                pool.tensor_copy(index[b][:, :], K.src_i[:, bass.ds(c * ET, ET)]).then_inc(index_ready, 1)
                pool.wait_ge(index_ready, c + 1)
                pool.sem_inc(pool_go, 1)
                for j in range(ET):
                    pool.indirect_dma_start(src_row[b][:, j, :], None, K.out[1][:, :],
                                            bass.IndirectOffsetOnAxis(index[b][:, j:j + 1], 0)).then_inc(gathered[b], 16)

            over_chunks(pool, body)

        @block.tensor
        def _(pe):
            def body(c, b, i):
                wait(pe, row_in[b], i * 32 + 32)
                for g in range(GROUPS):
                    wait(pe, t_evac, last_bank(c, g))
                    for k in range(TG):
                        last = nc.tensor.transpose(turned[g % 4][0:D, k * P:(k + 1) * P], row[b][:, g * TG + k, :], K.eye[:, :])
                    last.then_inc(t_done, 1)
                wait(pe, x_in[b], i * 32 + 32)
                for k in range(RGROUPS):
                    wait(pe, y_evac, c * RGROUPS + (k + 1 - RGROUPS))
                    nc.tensor.matmul(yp[k][0:P, 0:RG * D], lhsT=K.eye[:, :], rhs=flat(xrow[b][:, k * RG:(k + 1) * RG, :]),
                                     start=True, stop=False)
                    if k == 0:
                        wait(pe, added, c + 1)
                    for r in range(RG):
                        j = k * RG + r
                        last = nc.tensor.matmul(yp[k][0:P, r * D:(r + 1) * D], lhsT=resT[b][:, j * P:(j + 1) * P],
                                                rhs=K.eye[0:D, 0:D], start=False, stop=(r == RG - 1))
                    last.then_inc(y_done, 1)

            over_chunks(pe, body)

        @block.scalar
        def _(act):
            def relu(c, b):
                for g in range(GROUPS):
                    wait(act, ln.normed, c * GROUPS + (g + 1))
                    rows = flat(norm[b][:, g * TG:(g + 1) * TG, :])
                    nc.scalar.activation(rows, rows, ACT.Relu).then_inc(relu_done, 1)

            def body(c, b, i):
                wait(act, added, c)
                for g in range(GROUPS):
                    wait(act, t_done, c * GROUPS + (g + 1))
                    nc.scalar.activation(actT[:, g * TG * P:(g + 1) * TG * P], turned[g % 4][0:D, 0:TG * P], ACT.Relu,
                                         bias=K.shift[1][:, :], scale=K.scale[1][:, :]).then_inc(t_evac, 1)
                if not first(c):
                    ln.root(act, K, c - 1)
                    relu(c - 1, 1 - b)
                wait(act, final_ready, c - 1)
                for k in range(RGROUPS):
                    wait(act, y_done, c * RGROUPS + (k + 1))
                    nc.scalar.copy(flat(ysum[b][:, k * RG:(k + 1) * RG, :]), yp[k][0:P, 0:RG * D]).then_inc(y_evac, 1)

            over_chunks(act, body)
            ln.root(act, K, CHUNKS - 1)
            relu(CHUNKS - 1, 1)

        @block.vector
        def _(dve):
            def finish(c, b, i):
                wait(dve, relu_done, c * GROUPS + GROUPS)
                wait(dve, y_out[b], i * 32)
                nc.vector.scalar_tensor_tensor(final[b][:, :, :], norm[b][:, :, :], K.eps1[:, :],
                                               ysum[b][:, :, :], ALU.mult, ALU.add).then_inc(final_half, 1)
                wait(dve, final_half, c + 1)
                nc.vector.tensor_tensor(final[b][:, :, :], final[b][:, :, :],
                                        bc(K.mlp_empty[:, :].unsqueeze(1), [P, TILES, D]), ALU.add).then_inc(final_ready, 1)

            def layernorm(c, b):
                wait(dve, y_evac, c * RGROUPS + RGROUPS)
                ln.statistics(dve, ysum[b], c)
                ln.factors(dve, c)
                ln.apply(dve, ysum[b], norm[b], c)

            def body(c, b, i):
                if not first(c, 1):
                    finish(c - 2, b, i - 1)
                wait(dve, res_in[b], i * 16 + 16)
                wait(dve, t_evac, c * GROUPS + GROUPS)
                nc.vector.tensor_tensor(resT[b][:, :], resT[b][:, :], actT[:, :], ALU.add).then_inc(added, 1)
                if not first(c):
                    layernorm(c - 1, 1 - b)

            over_chunks(dve, body)
            finish(CHUNKS - 2, 0, CHUNKS // 2 - 1)
            layernorm(CHUNKS - 1, 1)
            finish(CHUNKS - 1, 1, CHUNKS // 2 - 1)



def third_edges(nc, K, A):
    attr = K.attr.rearrange("(c j p) f -> c p j f", c=CHUNKS, p=P)
    HG = (4, 4, 2)
    with Stage(nc, "edges") as st:
        sb, pair, bank, sem, sems = st.sb, st.pair, st.bank, st.sem, st.sems
        row, xrow = pair("row", [P, TILES, D]), pair("xrow", [P, TILES, D])
        resT = pair("resT", [D, COLS])
        actT = sb("actT", [D, COLS])
        ysum, norm = pair("ysum", [P, TILES, D]), pair("norm", [P, TILES, D])
        ln = Layernorm(nc, st, "ln")
        msg = pair("msg", [P, ET, D])
        dst_row = sb("dst_row", [P, ET, P], i32)
        same = pair("same", [P, ET, P])
        go_on = pair("go_on", [D, ET, P])
        aggr = pair("aggr", [D, EDGES_C])
        hidden = sb("hidden", [D, 2, EDGES_C])
        base_row = pair("base_row", [P, ET, D])
        final = pair("final", [P, ET, D])
        index = pair("index", [P, ET], i32)
        turned = [bank("turned0"), bank("turned1")]
        yp = [bank("yp0"), bank("yp1")]
        ap = [bank("ap0"), bank("ap1")]
        hp = [bank("hp0"), bank("hp1")]
        row_in, res_in, x_in, ea_in, scattered = (sems(n) for n in ("row_in", "res_in", "x_in", "ea_in", "scattered"))
        dr_in = sem("dr_in")
        t_done, t_evac, added, y_done, y_sum, masks_ready, msg_ready, ap_done, aggr_ready = (
            sem(n) for n in ("t_done", "t_evac", "added", "y_done", "y_sum", "masks_ready", "msg_ready", "ap_done", "aggr_ready"))
        hp_done, hid_ready, mp_done, final_ready, blank, base_half, base_ready, pool_go, index_ready, sp_go = (
            sem(n) for n in ("hp_done", "hid_ready", "mp_done", "final_ready", "blank", "base_half", "base_ready",
                             "pool_go", "index_ready", "sp_go"))
        LAST = CHUNKS // 2 - 1
        SRC_GROUPS, DST_GROUPS = range(-(-ET // TG)), range(-(-ET // TG), GROUPS)
        block = st.enter_context(nc.Block())

        @block.sync
        def _(sp):
            def load(c, b):
                wait(sp, t_done, (c - 1) * GROUPS)
                sp.sem_inc(sp_go, 1)
                dma_rows(sp, flat(row[b][:, 0:ET, :]), K.src_rows[c], row_in[b])
                dma_rows(sp, flat(row[b][:, ET:TILES, :]), K.out_pairs[1][c], row_in[b])
                wait(sp, y_done, (c - 1) * RGROUPS)
                sp.sem_inc(sp_go, 1)
                sp.dma_start(resT[b][:, :], K.pairT[1][c]).then_inc(res_in[b], 16)
                wait(sp, y_sum, (c - 1) * RGROUPS)
                sp.sem_inc(sp_go, 1)
                dma_rows(sp, flat(xrow[b][:, :, :]), K.raw_pairs[c], x_in[b])

            def load_edges(c, b):
                wait(sp, masks_ready, c)
                sp.sem_inc(sp_go, 1)
                sp.dma_start(dst_row[:, :, :].rearrange("p j e -> p (j e)"),
                             bc(K.dst_rows[c].unsqueeze(0), [P, EDGES_C])).then_inc(dr_in, 16)
                wait(sp, ap_done, (c - 1) * ET)
                sp.sem_inc(sp_go, 1)
                dma_rows(sp, msg[b][:, :, :], attr[c], ea_in[b])

            def body(c, b, i):
                load(c, b)
                if not first(c):
                    load_edges(c - 1, 1 - b)

            over_chunks(sp, body)
            load_edges(CHUNKS - 1, 1)

        @block.gpsimd
        def _(pool):
            def messages(c, b, i):
                wait(pool, ea_in[b], i * 32 + 32)
                wait(pool, ln.normed, c * GROUPS + len(SRC_GROUPS))
                pool.sem_inc(pool_go, 1)
                pool.tensor_tensor(flat(msg[b][:, :, :]), flat(norm[b][:, 0:ET, :]), flat(msg[b][:, :, :]),
                                   ALU.add).then_inc(msg_ready, 1)

            def scatter(c, b, i):
                wait(pool, scattered[b], i * (16 * ET))
                pool.sem_inc(pool_go, 1)
                pool.tensor_copy(index[b][:, :], K.tail_i[:, bass.ds(c * ET, ET)]).then_inc(index_ready, 1)
                pool.wait_ge(index_ready, c + 1)
                wait(pool, final_ready, c * 2 + 2)
                pool.sem_inc(pool_go, 1)
                for j in range(ET):
                    pool.indirect_dma_start(K.y[:, :], bass.IndirectOffsetOnAxis(index[b][:, j:j + 1], 0),
                                            final[b][:, j, :], None, bounds_check=N - 1,
                                            oob_is_err=False).then_inc(scattered[b], 16)

            def body(c, b, i):
                if not first(c, 2):
                    scatter(c - 3, 1 - b, i - 1 if b else i - 2)
                if not first(c):
                    messages(c - 1, 1 - b, i if b else i - 1)

            over_chunks(pool, body)
            scatter(CHUNKS - 3, 1, LAST - 1)
            messages(CHUNKS - 1, 1, LAST)
            scatter(CHUNKS - 2, 0, LAST)
            scatter(CHUNKS - 1, 1, LAST)
            for b in range(2):
                pool.wait_ge(scattered[b], 16 * ET * CHUNKS // 2)

        @block.tensor
        def _(pe):
            def run_sums(c, b):
                wait(pe, msg_ready, c + 1)
                wait(pe, masks_ready, c + 1)
                for j in range(ET):
                    wait(pe, aggr_ready, c * ET + (j - 1))
                    nc.tensor.matmul(ap[j % 2][0:D, 0:P], lhsT=msg[b][:, j, :], rhs=same[b][:, j, :],
                                     start=True, stop=True).then_inc(ap_done, 1)

            def hide(c, b):
                at = 0
                for q, cnt in enumerate(HG):
                    wait(pe, aggr_ready, c * ET + (at + cnt))
                    for half in range(2):
                        wait(pe, hid_ready, c * 6 + (2 * q + half - 1))
                        nc.tensor.matmul(hp[half][0:D, 0:cnt * P], lhsT=K.w1[:, half * D:(half + 1) * D],
                                         rhs=aggr[b][:, at * P:(at + cnt) * P], start=True, stop=True).then_inc(hp_done, 1)
                    at += cnt

            def mlp(c, b):
                wait(pe, hid_ready, c * 6 + 6)
                for k in range(2):
                    for r in range(RG):
                        j = k * RG + r
                        for half in range(2):
                            last = nc.tensor.matmul(turned[k][0:P, r * D:(r + 1) * D], lhsT=hidden[:, half, j * P:(j + 1) * P],
                                                    rhs=K.w2[:, half, :], start=(half == 0), stop=(half == 1))
                    last.then_inc(mp_done, 1)

            def body(c, b, i):
                wait(pe, row_in[b], i * 64 + 64)
                for g in range(GROUPS):
                    if g < 2:
                        wait(pe, final_ready, (c - 3) * 2 + (g + 1))
                    else:
                        wait(pe, t_evac, c * GROUPS + (g - 1))
                    for k in range(TG):
                        last = nc.tensor.transpose(turned[g % 2][0:D, k * P:(k + 1) * P],
                                                   row[b][:, g * TG + k, :], K.eye[:, :])
                    last.then_inc(t_done, 1)
                if not first(c, 1):
                    run_sums(c - 2, b)
                    hide(c - 2, b)
                wait(pe, added, c + 1)
                for k in range(RGROUPS):
                    wait(pe, y_sum, c * RGROUPS + (k - 1))
                    for r in range(RG):
                        j = k * RG + r
                        last = nc.tensor.matmul(yp[k % 2][0:P, r * D:(r + 1) * D], lhsT=resT[b][:, j * P:(j + 1) * P],
                                                rhs=K.eye[0:D, 0:D], start=True, stop=True)
                    last.then_inc(y_done, 1)
                if not first(c, 1):
                    mlp(c - 2, b)

            over_chunks(pe, body)
            for c in (CHUNKS - 2, CHUNKS - 1):
                run_sums(c, c % 2)
                hide(c, c % 2)
                wait(pe, final_ready, c * 2)
                mlp(c, c % 2)

        @block.scalar
        def _(act):
            def hide(c, b):
                wait(act, mp_done, c * 2)
                at = 0
                for q, cnt in enumerate(HG):
                    for half in range(2):
                        wait(act, hp_done, c * 6 + (2 * q + half + 1))
                        nc.scalar.activation(hidden[:, half, at * P:(at + cnt) * P], hp[half][0:D, 0:cnt * P], ACT.Relu,
                                             bias=K.b1[:, half:half + 1]).then_inc(hid_ready, 1)
                    at += cnt

            def apply(c, b, groups):
                wait(act, base_ready, c - 1)
                wait(act, msg_ready, c - 1)
                ln.apply_relu(act, ysum[b], norm[b], c, groups)

            def body(c, b, i):
                wait(act, added, c)
                for g in range(GROUPS):
                    wait(act, t_done, c * GROUPS + (g + 1))
                    nc.scalar.activation(actT[:, g * TG * P:(g + 1) * TG * P], turned[g % 2][0:D, 0:TG * P],
                                         ACT.Relu, bias=K.shift[1][:, :], scale=K.scale[1][:, :]).then_inc(t_evac, 1)
                if not first(c):
                    apply(c - 1, 1 - b, SRC_GROUPS)
                if not first(c, 1):
                    hide(c - 2, b)
                if not first(c):
                    apply(c - 1, 1 - b, DST_GROUPS)
                ln.root(act, K, c)

            over_chunks(act, body)
            apply(CHUNKS - 1, 1, range(GROUPS))
            hide(CHUNKS - 2, 0)
            hide(CHUNKS - 1, 1)

        @block.vector
        def _(dve):
            def masks(c, b):
                wait(dve, dr_in, c * 16 + 16)
                wait(dve, aggr_ready, (c - 1) * ET)
                nc.vector.tensor_tensor(same[b][:, :, :], dst_row[:, :, :],
                                        bc(K.dst_f[:, bass.ds(c * ET, ET)].unsqueeze(2), [P, ET, P]), ALU.is_equal)
                nc.vector.tensor_tensor(go_on[b][:, :, :], dst_row[0:D, :, :],
                                        bc(K.prev_b[:, bass.ds(c * ET, ET)].unsqueeze(2), [D, ET, P]),
                                        ALU.is_equal).then_inc(masks_ready, 1)

            def sums(c, b):
                wait(dve, hp_done, c * 6 - 6)
                for j in range(ET):
                    wait(dve, ap_done, c * ET + (j + 1))
                    wait(dve, aggr_ready, c * ET + j)
                    before = aggr[b][:, j * P - 1:j * P] if j else aggr[1 - b][:, EDGES_C - 1:EDGES_C]
                    nc.vector.scalar_tensor_tensor(aggr[b][:, j * P:(j + 1) * P], go_on[b][:, j, :], before,
                                                   ap[j % 2][0:D, 0:P], ALU.mult, ALU.add).then_inc(aggr_ready, 1)

            def base(c, b):
                y = base_row[b][:, :, :]
                wait(dve, ln.normed, c * GROUPS + GROUPS)
                wait(dve, final_ready, (c - 1) * 2)
                nc.vector.scalar_tensor_tensor(y, norm[b][:, ET:TILES, :], K.eps1[:, :], ysum[b][:, ET:TILES, :],
                                               ALU.mult, ALU.add).then_inc(base_half, 1)
                wait(dve, base_half, c + 1)
                nc.vector.tensor_tensor(y, y, bc(K.b2b[:, :].unsqueeze(1), [P, ET, D]), ALU.add).then_inc(base_ready, 1)

            def finish(c, b, i):
                wait(dve, scattered[b], i * (16 * ET))
                wait(dve, base_ready, c + 1)
                for k in range(2):
                    wait(dve, mp_done, c * 2 + (k + 1))
                    nc.vector.tensor_tensor(flat(final[b][:, k * RG:(k + 1) * RG, :]), turned[k][0:P, 0:RG * D],
                                            flat(base_row[b][:, k * RG:(k + 1) * RG, :]), ALU.add).then_inc(final_ready, 1)

            def body(c, b, i):
                if not first(c, 1):
                    sums(c - 2, b)
                wait(dve, res_in[b], i * 16 + 16)
                wait(dve, t_evac, c * GROUPS + GROUPS)
                nc.vector.tensor_tensor(resT[b][:, :], resT[b][:, :], actT[:, :], ALU.add).then_inc(added, 1)
                if not first(c):
                    masks(c - 1, 1 - b)
                wait(dve, x_in[b], i * 32 + 32)
                wait(dve, base_ready, c - 1)
                for k in range(RGROUPS):
                    wait(dve, y_done, c * RGROUPS + (k + 1))
                    nc.vector.tensor_tensor(flat(ysum[b][:, k * RG:(k + 1) * RG, :]), yp[k % 2][0:P, 0:RG * D],
                                            flat(xrow[b][:, k * RG:(k + 1) * RG, :]), ALU.add).then_inc(y_sum, 1)
                wait(dve, y_sum, c * RGROUPS + RGROUPS)
                ln.statistics(dve, ysum[b], c)
                if not first(c, 1):
                    finish(c - 2, b, i - 1)
                if not first(c):
                    base(c - 1, 1 - b)
                ln.factors(dve, c)

            nc.vector.memset(aggr[1][:, EDGES_C - 1:EDGES_C], 0.0).then_inc(blank, 1)
            dve.wait_ge(blank, 1)
            over_chunks(dve, body)
            masks(CHUNKS - 1, 1)
            base(CHUNKS - 1, 1)
            for c in (CHUNKS - 2, CHUNKS - 1):
                sums(c, c % 2)
                finish(c, c % 2, LAST)


def build(nc, A, y):
    K = Core()
    K.y = y
    K.src, K.dst, K.attr = A["src"], A["dst"], A["edge_attr_96"]
    K.dst_rows = K.dst.rearrange("(c e) -> c e", c=CHUNKS)

    def dram(name, shape):
        return nc.dram_tensor(name, shape, fp32, kind="Internal").ap()

    K.out = [dram(f"out_rows{l}", [N, D]) for l in range(LAYERS)]
    K.h0T, K.x1T = dram("h0T", [CHUNKS, D, COLS]), dram("x1T", [CHUNKS, D, COLS])
    K.pairT = [dram(f"pairT{l}", [CHUNKS, D, COLS]) for l in range(LAYERS)]
    K.raw_pairs = dram("raw_pairs", [CHUNKS, P, TILES * D])
    K.out_pairs = [dram(f"out_pairs{l}", [CHUNKS, P, ET * D]) for l in range(LAYERS)]
    K.src_rows = dram("src_rows", [CHUNKS, P, ET * D])
    with Stage(nc, "all") as st:
        sb = st.sb
        K.eye, K.eps = sb("eye", (P, P)), sb("eps", (P, 1))
        K.w = [sb(f"w_heads{l}", (D, HD)) for l in range(LAYERS)]
        K.w_bar = [sb(f"w_bar{l}", (D, D)) for l in range(LAYERS)]
        K.w_att = [sb(f"w_att{l}", (D, 3 * H)) for l in range(LAYERS)]
        K.bias, K.gamma, K.beta, K.scale, K.shift = (
            [sb(f"{n}{l}", (D, 1)) for l in range(LAYERS)] for n in ("bias", "gamma", "beta", "scale", "shift"))
        K.w1, K.w2, K.b1 = sb("w1", (D, 2 * D)), sb("w2", (D, 2, D)), sb("b1", (D, 2))
        K.mlp_empty, K.b2b, K.eps1 = sb("mlp_empty", (P, D)), sb("b2b", (P, D)), sb("eps1", (P, 1))
        K.src_i, K.dst_i, K.tail_i = (sb(n, (P, EDGE_TILES), i32) for n in ("src_i", "dst_i", "tail_i"))
        K.dst_f, K.prev_last = (sb(n, (P, EDGE_TILES)) for n in ("dst_f", "prev_last"))
        K.prev_b = sb("prev_b", (D, EDGE_TILES))
        with Stage(nc, "gat") as gat:
            K.cont_f, K.cont_b, K.tail, K.pen_f = (gat.sb(n, (LANES, EDGES_C)) for n in ("cont_f", "cont_b", "tail", "pen_f"))
            K.all_f, K.all_b, K.all_pen = (gat.sb(n, (1, LANES)) for n in ("all_f", "all_b", "all_pen"))
            K.logits = gat.sb("logits", (P, 3 * H, EDGE_TILES))
            K.alpha = gat.sb("alpha", (P, 2, LANES, ET))
            K.alpha_flat = K.alpha[:, :, :, :].rearrange("p k (h b) j -> p (k h) (b j)", h=H)
            prepare(nc, K, A)
            first_layer(nc, K, A)
            edge_softmax(nc, K, 0)
            aggregate(nc, K, 0)
            batch_norm(nc, K, 0)
            second_layer(nc, K, A)
            edge_softmax(nc, K, 1)
            aggregate(nc, K, 1)
        batch_norm(nc, K, 1)
        third_nodes(nc, K, A)
        third_edges(nc, K, A)


_INS = ["x", "src", "dst", "edge_attr_96", "L0_gnn_W", "L0_gnn_att_src", "L0_gnn_att_dst", "L0_gnn_bias",
        "L0_gnn_gamma", "L0_gnn_beta", "L1_gnn_W1", "L1_gnn_b1", "L1_gnn_W2", "L1_gnn_b2", "L1_gnn_eps"]


def kernel(**inputs):
    import numpy as np
    import concourse.bacc as bacc
    from concourse.bass_utils import run_bass_kernel_spmd

    nc = bacc.Bacc("TRN2", target_bir_lowering=False, num_devices=1)
    arrays, A = {}, {}
    for name in _INS:
        a = np.ascontiguousarray(inputs[name])
        arrays[f"in_{name}"] = a
        A[name] = nc.dram_tensor(f"in_{name}", a.shape, mybir.dt.from_np(a.dtype), kind="ExternalInput").ap()
    y = nc.dram_tensor("out_0", (N, D), fp32, kind="ExternalOutput").ap()
    build(nc, A, y)
    r = run_bass_kernel_spmd(nc, [arrays], core_ids=[0])
    return r.results[0]["out_0"]
```

```python
import concourse.bass as bass
import concourse.mybir as mybir
from contextlib import ExitStack

fp32 = mybir.dt.float32
i32 = mybir.dt.int32
ALU = mybir.AluOpType
ACT = mybir.ActivationFunctionType
AX = mybir.AxisListType

N, E, D, H = 50000, 25000, 96, 4
LAYERS = 2
P = 125
CHUNKS = 20
TILES = 20
ET = TILES // 2
EDGES_C = E // CHUNKS
EDGE_TILES = E // P
COLS = TILES * P
TG = 4
GROUPS = TILES // TG
RG = 5
RGROUPS = TILES // RG
LANES = H * CHUNKS
HD = H * D
SLOPE, EPS, TINY = 0.2, 1e-05, 1e-16
BIG = 1.0e30
assert N == CHUNKS * TILES * P and E == CHUNKS * ET * P


def wait(eng, sem, count):
    if isinstance(count, int) and count <= 0:
        return
    eng.wait_ge(sem, count)


def over_chunks(eng, body, buffers=2):
    for c in range(4):
        body(c, c % buffers, c // buffers)
    with eng.Fori(4 // buffers, CHUNKS // buffers) as i:
        for b in range(buffers):
            body(i * buffers + b, b, i)


def earlier(c, b, j, k):
    return (c, b, j - k) if j >= k else (c - 1, 1 - b, j - k + ET)


class Line:

    def __init__(self, eng, sem):
        self.eng, self.sem, self.n = eng, sem, 0

    def step(self, ins):
        ins.then_inc(self.sem, 1)
        self.n += 1
        self.eng.wait_ge(self.sem, self.n)


class Stage(ExitStack):

    def __init__(self, nc, tag):
        super().__init__()
        self.nc, self.tag, self.used = nc, tag, []

    def sb(self, name, shape, dt=fp32):
        return self.enter_context(self.nc.sbuf_tensor(f"{self.tag}_{name}", list(shape), dt))

    def pair(self, name, shape, dt=fp32):
        return [self.sb(f"{name}{b}", shape, dt) for b in range(2)]

    def bank(self, name):
        return self.enter_context(self.nc.psum_tensor(f"{self.tag}_{name}", [P, 512], fp32))

    def sem(self, name):
        self.used.append(self.nc.alloc_semaphore(f"{self.tag}_{name}"))
        return self.used[-1]

    def sems(self, name):
        return [self.sem(f"{name}{b}") for b in range(2)]

    def __exit__(self, *what):
        done = super().__exit__(*what)
        if what[0] is None and self.used:
            self.nc.clear_and_free_semaphores(self.used)
            self.nc.all_engine_barrier()
        return done


class Core:
    pass


def bc(ap, shape):
    return ap.broadcast_to(shape)



def prepare(nc, K, A):
    with Stage(nc, "prep") as st:
        sb, bank, sem = st.sb, st.bank, st.sem
        att = [[sb(f"att_{s}{l}", [D, HD]) for s in ("src", "dst")] for l in range(LAYERS)]
        prod = sb("prod", [D, HD])
        raw = [sb(f"raw_{n}", [100, 2, P], i32) for n in ("src", "dst", "next")]
        rawf = [sb(f"rawf_{n}", [100, 2, P]) for n in ("src", "dst", "next")]
        nextc = sb("nextc", [P, EDGE_TILES])
        gap, tail_c = sb("gap", [P, EDGE_TILES]), sb("tail_c", [P, EDGE_TILES])
        lane_d = sb("lane_d", [LANES, EDGES_C], i32)
        lane_n = sb("lane_n", [LANES, EDGES_C], i32)
        lane_p = sb("lane_p", [LANES, EDGES_C], i32)
        allf = sb("allf", [LANES, 1])
        allb = sb("allb", [LANES, 1])
        b1p = sb("b1p", [D, 2])
        b1r = sb("b1r", [D, 2, P])
        pick = sb("pick", [P, D])
        cols = bank("cols")
        rows = bank("rows")
        mlp0 = bank("mlp0")
        ids_in, lanes_in, weights_in, blanks, made, dve_s, colsem, pe_s, eye_s = (
            sem(n) for n in ("ids_in", "lanes_in", "weights_in", "blanks", "made", "dve_steps", "cols_ready", "pe_rows", "eye_s"))
        flags_ready, sel_ready, b1_ready, w_ready = (sem(n) for n in ("flags_ready", "sel_ready", "b1_ready", "w_ready"))
        cols_used, pool_mask = sem("cols_used"), sem("pool_mask")
        dst1 = K.dst.rearrange("(a n) -> a n", a=1)
        block = st.enter_context(nc.Block())
        n_loads = {}

        @block.sync
        def _(sp):
            def load(out, in_, sem):
                sp.dma_start(out, in_).then_inc(sem, 16)
                n_loads[sem] = n_loads.get(sem, 0) + 16

            for n, lst in ((0, K.src), (1, K.dst)):
                load(raw[n][:, :, :], lst.rearrange("(a q p) -> q a p", a=2, q=100), ids_in)
            sp.wait_ge(blanks, 3)
            load(raw[2][:, 0, :], K.dst[1:100 * P + 1].rearrange("(q p) -> q p", q=100), ids_in)
            load(raw[2][0:99, 1, :], K.dst[100 * P + 1:199 * P + 1].rearrange("(q p) -> q p", q=99), ids_in)
            load(raw[2][99:100, 1, 0:P - 1], dst1[:, 199 * P + 1:E], ids_in)
            last = CHUNKS - 1
            for h in range(H):
                o = h * CHUNKS
                load(lane_d[o:o + CHUNKS, :], K.dst.rearrange("(b e) -> b e", b=CHUNKS), lanes_in)
                load(lane_n[o:o + last, :], K.dst[1:1 + last * EDGES_C].rearrange("(b e) -> b e", b=last), lanes_in)
                load(lane_n[o + last:o + CHUNKS, 0:EDGES_C - 1], dst1[:, last * EDGES_C + 1:E], lanes_in)
                load(lane_p[o:o + 1, 1:EDGES_C], dst1[:, 0:EDGES_C - 1], lanes_in)
                load(lane_p[o + 1:o + CHUNKS, :],
                     K.dst[EDGES_C - 1:E - 1].rearrange("(b e) -> b e", b=last), lanes_in)
            sp.wait_ge(ids_in, n_loads[ids_in])
            sp.wait_ge(lanes_in, n_loads[lanes_in])

        @block.scalar
        def _(act):
            def load(out, in_):
                act.dma_start(out, in_).then_inc(weights_in, 16)
                n_loads[weights_in] = n_loads.get(weights_in, 0) + 16

            for l in range(LAYERS):
                load(K.w[l][:, :], A["L0_gnn_W"][l, :, :])
                for s, name in enumerate(("L0_gnn_att_src", "L0_gnn_att_dst")):
                    load(att[l][s][:, :], bc(A[name][l:l + 1, :, :].rearrange("l h d -> l (h d)"), [D, HD]))
                load(K.bias[l][:, :], A["L0_gnn_bias"][l:l + 1, :].rearrange("l d -> d l"))
                load(K.gamma[l][:, :], A["L0_gnn_gamma"][l:l + 1, :].rearrange("l d -> d l"))
                load(K.beta[l][:, :], A["L0_gnn_beta"][l:l + 1, :].rearrange("l d -> d l"))
            load(K.w1[:, :], A["L1_gnn_W1"])
            load(K.w2[:, :, :], A["L1_gnn_W2"].rearrange("(k p) n -> p k n", k=2))
            for k in range(2):
                load(K.b1[:, k:k + 1], A["L1_gnn_b1"][k * D:(k + 1) * D].rearrange("(p a) -> p a", a=1))
            load(K.b2b[:, :], bc(A["L1_gnn_b2"].rearrange("(a n) -> a n", a=1), [P, D]))
            load(K.eps1[:, :], bc(A["L1_gnn_eps"].rearrange("(a n) -> a n", a=1), [P, 1]))
            act.wait_ge(weights_in, n_loads[weights_in])

        @block.gpsimd
        def _(pool):
            pool.memset(K.eye[:, :], 0.0).then_inc(eye_s, 1)
            pool.memset(pick[:, :], 1.0).then_inc(eye_s, 1)
            pool.wait_ge(eye_s, 2)
            pool.affine_select(out=K.eye[:, :], in_=K.eye[:, :], compare_op=ALU.not_equal, fill=1.0, base=0,
                               pattern=[[-1, P]], channel_multiplier=1).then_inc(sel_ready, 1)
            pool.affine_select(out=pick[:, :], in_=pick[:, :], compare_op=ALU.is_equal, fill=0.0, base=1 - P,
                               pattern=[[0, D]], channel_multiplier=1).then_inc(sel_ready, 1)
            pool.wait_ge(pool_mask, 1)
            pool.affine_select(out=K.prev_last[:, :], in_=K.prev_last[:, :], compare_op=ALU.is_equal,
                               fill=-1.0, base=1 - P, pattern=[[0, EDGE_TILES]],
                               channel_multiplier=1).then_inc(sel_ready, 1)
            pool.wait_ge(sel_ready, 3)

        @block.vector
        def _(dve):
            go = Line(dve, dve_s)
            nc.vector.memset(raw[2][:, :, :], -1).then_inc(blanks, 1)
            nc.vector.memset(lane_n[:, :], -1).then_inc(blanks, 1)
            nc.vector.memset(lane_p[:, :], -1).then_inc(blanks, 1)
            nc.vector.memset(K.eps[:, :], EPS).then_inc(made, 1)
            nc.vector.memset(K.prev_last[:, :], -1.0).then_inc(made, 1)
            dve.wait_ge(made, 2)
            dve.wait_ge(ids_in, n_loads[ids_in])
            for n in range(3):
                nc.vector.tensor_copy(rawf[n][:, :, :], raw[n][:, :, :]).then_inc(flags_ready, 1)
            dve.wait_ge(colsem, 1)
            go.step(nc.vector.tensor_copy(K.src_i[:, :], cols[:, 0:200]))
            go.step(nc.vector.tensor_copy(K.dst_f[:, :], cols[:, 200:400]))
            nc.vector.tensor_copy(nextc[:, :], rows[:, 200:400]).then_inc(cols_used, 1)
            dve.wait_ge(cols_used, 1)
            go.step(nc.vector.tensor_copy(K.dst_i[:, :], K.dst_f[:, :]))
            go.step(nc.vector.tensor_tensor(tail_c[:, :], K.dst_f[:, :], nextc[:, :], ALU.not_equal))
            go.step(nc.vector.tensor_scalar(gap[:, :], K.dst_f[:, :], -float(N), None, ALU.add))
            go.step(nc.vector.tensor_tensor(gap[:, :], gap[:, :], tail_c[:, :], ALU.mult))
            go.step(nc.vector.tensor_scalar(K.tail_i[:, :], gap[:, :], float(N), None, ALU.add))
            nc.vector.tensor_copy(K.prev_last[:, 1:EDGE_TILES], K.dst_f[:, 0:EDGE_TILES - 1]).then_inc(pool_mask, 1)
            dve.wait_ge(pe_s, 1)
            go.step(nc.vector.memset(K.prev_b[:, :], -1.0))
            go.step(nc.vector.tensor_copy(K.prev_b[:, 1:EDGE_TILES], mlp0[0:D, 200:399]))
            dve.wait_ge(lanes_in, n_loads[lanes_in])
            go.step(nc.vector.tensor_tensor(K.cont_f[:, :], lane_d[:, :], lane_p[:, :], ALU.is_equal))
            go.step(nc.vector.tensor_tensor(K.cont_b[:, :], lane_d[:, :], lane_n[:, :], ALU.is_equal))
            go.step(nc.vector.tensor_scalar(K.tail[:, :], K.cont_b[:, :], -1.0, 1.0, ALU.mult, ALU.add))
            go.step(nc.vector.tensor_scalar(K.pen_f[:, :], K.cont_f[:, :], BIG, -BIG, ALU.mult, ALU.add))
            go.step(nc.vector.tensor_reduce(allf[:, :], K.cont_f[:, :], AX.X, ALU.min))
            nc.vector.tensor_reduce(allb[:, :], K.cont_b[:, :], AX.X, ALU.min).then_inc(flags_ready, 1)
            dve.wait_ge(weights_in, n_loads[weights_in])
            for l in range(LAYERS):
                for k, s in ((0, 0), (1, 1), (2, 0)):
                    go.step(nc.vector.tensor_tensor(prod[:, :], K.w[l][:, :], att[l][s][:, :], ALU.mult))
                    go.step(nc.vector.tensor_reduce(K.w_att[l][:, k * H:(k + 1) * H],
                                                    prod[:, :].rearrange("p (h d) -> p h d", h=H), AX.X, ALU.add))
                go.step(nc.vector.tensor_scalar(K.w[l][:, :], K.w[l][:, :], 1.0 / H, None, ALU.mult))
                go.step(nc.vector.tensor_reduce(K.w_bar[l][:, :], K.w[l][:, :].rearrange("p (h d) -> p d h", h=H),
                                                AX.X, ALU.add))
            go.step(nc.vector.tensor_scalar(K.eps1[:, :], K.eps1[:, :], 1.0, None, ALU.add))
            go.step(nc.vector.tensor_scalar(b1p[:, :], K.b1[:, :], 0.0, None, ALU.max))
            nc.vector.tensor_copy(b1r[:, :, :], bc(b1p[:, :].unsqueeze(2), [D, 2, P])).then_inc(b1_ready, 1)
            dve.wait_ge(pe_s, 2)
            go.step(nc.vector.tensor_copy(K.all_f[:, :], rows[0:1, 0:LANES]))
            go.step(nc.vector.tensor_copy(K.all_b[:, :], rows[0:1, LANES:2 * LANES]))
            go.step(nc.vector.tensor_scalar(K.all_pen[:, :], K.all_f[:, :], BIG, -BIG, ALU.mult, ALU.add))
            dve.wait_ge(w_ready, 1)
            go.step(nc.vector.tensor_tensor(K.mlp_empty[:, :], mlp0[:, 0:D], K.b2b[:, :], ALU.add))

        @block.tensor
        def _(pe):
            pe.wait_ge(sel_ready, 2)
            pe.wait_ge(flags_ready, 3)
            for a in range(2):
                nc.tensor.transpose(rows[:, 200 + 100 * a:300 + 100 * a], rawf[2][:, a, :], K.eye[0:100, 0:100])
            for n in range(2):
                for a in range(2):
                    o = 200 * n + 100 * a
                    last = nc.tensor.transpose(cols[:, o:o + 100], rawf[n][:, a, :], K.eye[0:100, 0:100])
            last.then_inc(colsem, 1)
            pe.wait_ge(pool_mask, 1)
            nc.tensor.matmul(mlp0[0:D, 200:400], lhsT=pick[:, :], rhs=K.dst_f[:, :], start=True, stop=True).then_inc(pe_s, 1)
            pe.wait_ge(flags_ready, 4)
            nc.tensor.transpose(rows[0:1, 0:LANES], allf[:, :], K.eye[0:LANES, 0:LANES])
            nc.tensor.transpose(rows[0:1, LANES:2 * LANES], allb[:, :], K.eye[0:LANES, 0:LANES]).then_inc(pe_s, 1)
            pe.wait_ge(b1_ready, 1)
            for k in range(2):
                last = nc.tensor.matmul(mlp0[:, 0:D], lhsT=b1r[:, k, :], rhs=K.w2[:, k, :],
                                        start=(k == 0), stop=(k == 1))
            last.then_inc(w_ready, 1)


def dma_rows(eng, out, in_, sem):
    eng.dma_start(out[0:112], in_[0:112]).then_inc(sem, 16)
    eng.dma_start(out[112:P], in_[112:P]).then_inc(sem, 16)



class Layernorm:
    STEPS = 4

    def __init__(self, nc, st, name, groups=GROUPS):
        self.nc, self.groups = nc, groups
        self.half = st.sb(f"{name}_half", [P, TILES, 6])
        self.msum, self.mdiff, self.var, self.dev, self.factor, self.shift = (
            st.sb(f"{name}_{n}", [P, TILES]) for n in ("msum", "mdiff", "var", "dev", "factor", "shift"))
        self.steps, self.spread, self.rooted, self.ready, self.normed = (
            st.sem(f"{name}_{n}") for n in ("steps", "spread", "rooted", "ready", "normed"))

    def statistics(self, dve, x, n):
        nc = self.nc
        for j in range(TILES):
            ins = nc.vector.bn_stats(self.half[:, j, :], x[:, j, :])
        ins.then_inc(self.steps, 1)
        wait(dve, self.steps, n * self.STEPS + 1)
        nc.vector.tensor_tensor(self.msum[:, :], self.half[:, :, 1], self.half[:, :, 4], ALU.add)
        nc.vector.tensor_tensor(self.var[:, :], self.half[:, :, 2], self.half[:, :, 5], ALU.add)
        nc.vector.tensor_tensor(self.mdiff[:, :], self.half[:, :, 1], self.half[:, :, 4],
                                ALU.subtract).then_inc(self.steps, 1)
        wait(dve, self.steps, n * self.STEPS + 2)
        nc.vector.tensor_tensor(self.mdiff[:, :], self.mdiff[:, :], self.mdiff[:, :], ALU.mult).then_inc(self.steps, 1)
        wait(dve, self.steps, n * self.STEPS + 3)
        nc.vector.scalar_tensor_tensor(self.var[:, :], self.mdiff[:, :], D / 4.0, self.var[:, :],
                                       ALU.mult, ALU.add).then_inc(self.spread, 1)

    def root(self, act, K, n):
        wait(act, self.spread, n + 1)
        self.nc.scalar.activation(self.dev[:, :], self.var[:, :], ACT.Sqrt, bias=K.eps[:, :],
                                  scale=1.0 / D).then_inc(self.rooted, 1)

    def factors(self, dve, n):
        nc = self.nc
        wait(dve, self.normed, n * self.groups)
        wait(dve, self.rooted, n + 1)
        nc.vector.reciprocal(self.factor[:, :], self.dev[:, :]).then_inc(self.steps, 1)
        wait(dve, self.steps, n * self.STEPS + 4)
        nc.vector.scalar_tensor_tensor(self.shift[:, :], self.msum[:, :], -0.5, self.factor[:, :],
                                       ALU.mult, ALU.mult).then_inc(self.ready, 1)

    def apply_relu(self, act, x, out, n):
        wait(act, self.ready, n + 1)
        for g in range(GROUPS):
            for j in range(g * TG, (g + 1) * TG):
                ins = self.nc.scalar.activation(out[:, j, :], x[:, j, :], ACT.Relu, bias=self.shift[:, j:j + 1],
                                                scale=self.factor[:, j:j + 1])
            ins.then_inc(self.normed, 1)

    def apply(self, dve, x, out, n):
        wait(dve, self.ready, n + 1)
        for g in range(self.groups):
            for j in range(g * TG, (g + 1) * TG):
                ins = self.nc.vector.tensor_scalar(out[:, j, :], x[:, j, :], self.factor[:, j:j + 1],
                                                   self.shift[:, j:j + 1], ALU.mult, ALU.add)
            ins.then_inc(self.normed, 1)


def flat(t):
    return t.rearrange("p j f -> p (j f)")


def first(c, at=0):
    return isinstance(c, int) and c <= at



def first_layer(nc, K, A):
    x_nodes = A["x"].rearrange("(c p j) f -> c p (j f)", c=CHUNKS, p=P)
    out0_nodes = K.out[0].rearrange("(c p j) f -> c p (j f)", c=CHUNKS, p=P)
    with Stage(nc, "first") as st:
        pair, bank, sem, sems = st.pair, st.bank, st.sem, st.sems
        NODE, EDGE = 0, 1
        x_in = pair("x_in", [P, TILES, D])
        pairs = pair("pairs", [P, TILES, D])
        rows_of = [x_in, pairs]
        norm = [pair("norm_node", [P, TILES, D]), pair("norm_edge", [P, TILES, D])]
        normT = [pair("normT_node", [D, COLS]), pair("normT_edge", [D, COLS])]
        ln = [Layernorm(nc, st, "ln_node"), Layernorm(nc, st, "ln_edge")]
        out_row = pair("out_row", [P, TILES * D])
        index = pair("index", [P, TILES], i32)
        turned = [bank(f"turned{k}") for k in range(4)]
        rows = [bank("rows0"), bank("rows1")]
        logit = [bank("logit0"), bank("logit1")]

        x_loaded, gathered = sems("x_loaded"), sems("gathered")
        raw_stored, hT_stored, rows_stored, gT_stored = (sems(n) for n in ("raw_stored", "hT_stored", "rows_stored", "gT_stored"))
        pool_go, index_ready, sp_go = (sem(n) for n in ("pool_go", "index_ready", "sp_go"))
        t_done, t_evac, rows_done, rows_evac = (sem(n) for n in ("t_done", "t_evac", "rows_done", "rows_evac"))
        logit_done, logit_evac = sem("logit_done"), sem("logit_evac")
        block = st.enter_context(nc.Block())

        @block.sync
        def _(sp):
            def store_raw(c, b, i):
                wait(sp, gathered[b], i * (16 * TILES) + 16 * TILES)
                sp.sem_inc(sp_go, 1)
                dma_rows(sp, K.raw_pairs[c], flat(pairs[b][:, :, :]), raw_stored[b])

            def store_nodes(c, b):
                wait(sp, t_evac, bank_no(c, NODE, GROUPS))
                sp.sem_inc(sp_go, 1)
                sp.dma_start(K.h0T[c], normT[NODE][b][:, :]).then_inc(hT_stored[b], 16)
                wait(sp, rows_evac, c * RGROUPS + RGROUPS)
                sp.sem_inc(sp_go, 1)
                dma_rows(sp, out0_nodes[c], out_row[b][:, :], rows_stored[b])

            def store_edges(c, b):
                wait(sp, t_evac, bank_no(c, EDGE, GROUPS))
                sp.sem_inc(sp_go, 1)
                sp.dma_start(K.pairT[0][c], normT[EDGE][b][:, :]).then_inc(gT_stored[b], 16)

            def body(c, b, i):
                wait(sp, ln[NODE].normed, c * GROUPS - GROUPS)
                sp.sem_inc(sp_go, 1)
                dma_rows(sp, flat(x_in[b][:, :, :]), x_nodes[c], x_loaded[b])
                if not first(c):
                    store_raw(c - 1, 1 - b, i if b else i - 1)
                if not first(c, 1):
                    store_nodes(c - 2, b)
                    store_edges(c - 2, b)

            over_chunks(sp, body)
            store_nodes(CHUNKS - 2, 0)
            store_raw(CHUNKS - 1, 1, CHUNKS // 2 - 1)
            store_edges(CHUNKS - 2, 0)
            store_nodes(CHUNKS - 1, 1)
            store_edges(CHUNKS - 1, 1)
            for b in range(2):
                for s, per in ((raw_stored, 32), (hT_stored, 16), (rows_stored, 32), (gT_stored, 16)):
                    sp.wait_ge(s[b], per * CHUNKS // 2)

        @block.gpsimd
        def _(pool):
            def body(c, b, i):
                wait(pool, ln[EDGE].normed, c * GROUPS - GROUPS)
                wait(pool, raw_stored[b], i * 32)
                wait(pool, gathered[b], i * (16 * TILES))
                pool.sem_inc(pool_go, 1)
                pool.tensor_copy(index[b][:, 0:ET], K.src_i[:, bass.ds(c * ET, ET)]).then_inc(index_ready, 1)
                pool.tensor_copy(index[b][:, ET:TILES], K.dst_i[:, bass.ds(c * ET, ET)]).then_inc(index_ready, 1)
                pool.wait_ge(index_ready, c * 2 + 2)
                pool.sem_inc(pool_go, 1)
                for j in range(TILES):
                    pool.indirect_dma_start(pairs[b][:, j, :], None, A["x"],
                                            bass.IndirectOffsetOnAxis(index[b][:, j:j + 1], 0)).then_inc(gathered[b], 16)

            over_chunks(pool, body)

        @block.vector
        def _(dve):
            def normalise(kind, c, b):
                ln[kind].factors(dve, c)
                wait(dve, t_done, bank_no(c - 2, kind, GROUPS))
                ln[kind].apply(dve, rows_of[kind][b], norm[kind][b], c)

            def body(c, b, i):
                wait(dve, x_loaded[b], i * 32 + 32)
                ln[NODE].statistics(dve, x_in[b], c)
                if not first(c):
                    normalise(EDGE, c - 1, 1 - b)
                wait(dve, gathered[b], i * (16 * TILES) + 16 * TILES)
                ln[EDGE].statistics(dve, pairs[b], c)
                normalise(NODE, c, b)

            over_chunks(dve, body)
            normalise(EDGE, CHUNKS - 1, 1)

        @block.scalar
        def _(act):
            def evacuate(kind, c, b, i):
                stored = (hT_stored, gT_stored)[kind]
                wait(act, stored[b], i * 16)
                if kind == NODE:
                    wait(act, rows_done, c * RGROUPS - RGROUPS)
                else:
                    wait(act, logit_done, c - 1)
                for g in range(GROUPS):
                    wait(act, t_done, bank_no(c, kind, g + 1))
                    nc.scalar.activation(normT[kind][b][:, g * TG * P:(g + 1) * TG * P],
                                         turned[turn_bank(b, kind, g)][0:D, 0:TG * P], ACT.Relu).then_inc(t_evac, 1)

            def logits(c, b):
                wait(act, logit_done, c + 1)
                nc.scalar.copy(K.logits[:, :, bass.ds(c * ET, ET)],
                               logit[b][0:P, 0:3 * H * ET].rearrange("p (k j) -> p k j", j=ET)).then_inc(logit_evac, 1)

            def body(c, b, i):
                ln[NODE].root(act, K, c)
                if not first(c):
                    evacuate(EDGE, c - 1, 1 - b, i if b else i - 1)
                ln[EDGE].root(act, K, c)
                evacuate(NODE, c, b, i)
                wait(act, rows_stored[b], i * 32)
                for k in range(RGROUPS):
                    wait(act, rows_done, c * RGROUPS + (k + 1))
                    nc.scalar.copy(out_row[b][:, k * RG * D:(k + 1) * RG * D], rows[k % 2][0:P, 0:RG * D]).then_inc(rows_evac, 1)
                if not first(c):
                    logits(c - 1, 1 - b)

            over_chunks(act, body)
            evacuate(EDGE, CHUNKS - 1, 1, CHUNKS // 2 - 1)
            logits(CHUNKS - 1, 1)

        @block.tensor
        def _(pe):
            def turn(kind, c, b):
                for g in range(GROUPS):
                    wait(pe, ln[kind].normed, c * GROUPS + (g + 1))
                    turn_group(nc, K, pe, kind, c, b, g, norm[kind][b], turned, t_evac, t_done)

            def logits(c, b):
                edge_logits(nc, K, pe, 0, c, b, normT[EDGE][b], logit[b], t_evac, bank_no(c, EDGE, GROUPS),
                            logit_evac, logit_done)

            def body(c, b, i):
                if not first(c):
                    turn(EDGE, c - 1, 1 - b)
                turn(NODE, c, b)
                dense_rows(nc, K, pe, 0, c, b, normT[NODE][b], rows, t_evac, lambda g: bank_no(c, NODE, g + 1),
                           rows_evac, rows_done)
                if not first(c):
                    logits(c - 1, 1 - b)

            over_chunks(pe, body)
            turn(EDGE, CHUNKS - 1, 1)
            logits(CHUNKS - 1, 1)


def bank_no(c, kind, g):
    return c * (2 * GROUPS) + (kind * GROUPS + g)


def turn_bank(b, kind, g):
    return (2 * b + kind * GROUPS + g) % 4


def turn_group(nc, K, pe, kind, c, b, g, rows, turned, t_evac, t_done):
    wait(pe, t_evac, bank_no(c, kind, g) - 3)
    for k in range(TG):
        last = nc.tensor.transpose(turned[turn_bank(b, kind, g)][0:D, k * P:(k + 1) * P],
                                   rows[:, g * TG + k, :], K.eye[:, :])
    last.then_inc(t_done, 1)


def dense_rows(nc, K, pe, l, c, b, xT, rows, ready, ready_count, rows_evac, rows_done):
    seen = -1
    for k in range(RGROUPS):
        need = ((k + 1) * RG - 1) // TG
        if need > seen:
            wait(pe, ready, ready_count(need))
            seen = need
        wait(pe, rows_evac, c * RGROUPS + (k - 1))
        for r in range(RG):
            j = k * RG + r
            last = nc.tensor.matmul(rows[k % 2][0:P, r * D:(r + 1) * D], lhsT=xT[:, j * P:(j + 1) * P],
                                    rhs=K.w_bar[l][:, :], start=True, stop=True)
        last.then_inc(rows_done, 1)


def edge_logits(nc, K, pe, l, c, b, xT, out, ready, ready_count, logit_evac, logit_done):
    wait(pe, ready, ready_count)
    wait(pe, logit_evac, c - 1)
    cols = out[0:P, 0:3 * H * ET].rearrange("p (k j) -> p k j", j=ET)
    for j in range(ET):
        nc.tensor.matmul(cols[:, 0:H, j], lhsT=xT[:, j * P:(j + 1) * P], rhs=K.w_att[l][:, 0:H], start=True, stop=True)
        last = nc.tensor.matmul(cols[:, H:3 * H, j], lhsT=xT[:, (ET + j) * P:(ET + j + 1) * P],
                                rhs=K.w_att[l][:, H:3 * H], start=True, stop=True)
    last.then_inc(logit_done, 1)



def edge_softmax(nc, K, l):
    with Stage(nc, f"softmax{l}") as st:
        sb, bank, sem = st.sb, st.bank, st.sem
        LE = (LANES, EDGES_C)
        lane = [sb(f"lane{k}", LE) for k in range(3)]
        edge, own, work, scan, run_max, run_sum = (sb(n, LE) for n in ("edge", "own", "work", "scan", "run_max", "run_sum"))
        prob, own_prob = sb("prob", LE), sb("own_prob", LE)
        ends, links, start = sb("ends", (1, LANES)), sb("links", (1, LANES + 1)), sb("start", (LANES, 1))
        turned = [bank("turned0"), bank("turned1")]
        link_row, link_col = bank("link_row"), bank("link_col")
        turn_done, turn_used, steps = sem("turn_done"), sem("turn_used"), sem("dve_steps")
        ends_ready, row_done, links_ready, col_done = (sem(n) for n in ("ends_ready", "row_done", "links_ready", "col_done"))
        shifted, probs, alpha_ready, back_done, back_used = (sem(n) for n in ("shifted", "probs", "alpha_ready", "back_done", "back_used"))
        block = st.enter_context(nc.Block())
        FOUR = (4, 4, 2)
        SCANS = 5

        @block.tensor
        def _(pe):
            n = 0
            for k in range(3):
                j = 0
                for cnt in FOUR:
                    wait(pe, turn_used, n - 1)
                    for q in range(cnt):
                        last = nc.tensor.transpose(turned[n % 2][0:LANES, q * P:(q + 1) * P],
                                                   K.logits[:, k * H:(k + 1) * H, :].rearrange(
                                                       "p h (b j) -> p (h b) j", j=ET)[:, :, j + q], K.eye[:, :])
                    last.then_inc(turn_done, 1)
                    j += cnt
                    n += 1
            for s in range(SCANS):
                forward = s in (1, 3)
                pe.wait_ge(ends_ready, s + 1)
                at = EDGES_C - 1 if forward else 0
                nc.tensor.transpose(link_row[0:1, 0:LANES], scan[:, at:at + 1], K.eye[0:LANES, 0:LANES]).then_inc(row_done, 1)
                pe.wait_ge(links_ready, s + 1)
                off = 0 if forward else 1
                nc.tensor.transpose(link_col[0:LANES, 0:1], links[0:1, off:off + LANES], K.eye[0:1, 0:1]).then_inc(col_done, 1)
            pe.wait_ge(alpha_ready, 1)
            for k, lanes in enumerate((prob, own_prob)):
                for half in range(2):
                    m = 2 * k + half
                    wait(pe, back_used, m - 1)
                    for q in range(5):
                        j = half * 5 + q
                        last = nc.tensor.transpose((link_row, link_col)[m % 2][0:P, q * LANES:(q + 1) * LANES],
                                                   lanes[:, j * P:(j + 1) * P], K.eye[0:LANES, 0:LANES])
                    last.then_inc(back_done, 1)

        @block.scalar
        def _(act):
            n = 0
            for k in range(3):
                j = 0
                for cnt in FOUR:
                    act.wait_ge(turn_done, n + 1)
                    nc.scalar.copy(lane[k][:, j * P:(j + cnt) * P], turned[n % 2][0:LANES, 0:cnt * P]).then_inc(turn_used, 1)
                    j += cnt
                    n += 1
            for m, (out, in_) in enumerate(((prob, edge), (own_prob, own))):
                act.wait_ge(shifted, m + 1)
                nc.scalar.activation(out[:, :], in_[:, :], ACT.Exp).then_inc(probs, 1)
            for m in range(4):
                act.wait_ge(back_done, m + 1)
                half = m % 2
                dst = K.alpha[:, m // 2, :, :].rearrange("p l j -> p j l")[:, half * 5:half * 5 + 5, :]
                nc.scalar.copy(dst, (link_row, link_col)[m % 2][0:P, 0:5 * LANES].rearrange("p (j l) -> p j l", j=5)).then_inc(back_used, 1)

        @block.vector
        def _(dve):
            go = Line(dve, steps)
            scans = [0]

            def run_scan(out, keep, data, block_keep, forward, op0, op1, none):
                r = slice(None) if forward else slice(None, None, -1)
                init = none
                for again in range(2):
                    ins = nc.vector.tensor_tensor_scan(out[:, r], keep[:, r], data[:, r], init, op0, op1)
                    if again:
                        go.step(ins)
                        break
                    ins.then_inc(ends_ready, 1)
                    scans[0] += 1
                    n = scans[0]
                    dve.wait_ge(row_done, n)
                    go.step(nc.vector.tensor_copy(ends[:, :], link_row[0:1, 0:LANES]))
                    edge_at, body = (0, slice(1, LANES + 1)) if forward else (LANES, slice(0, LANES))
                    go.step(nc.vector.memset(links[0:1, edge_at:edge_at + 1], none))
                    nc.vector.tensor_tensor_scan(links[0:1, body][:, r], block_keep[0:1, r], ends[0:1, r], none,
                                                 op0, op1).then_inc(links_ready, 1)
                    dve.wait_ge(col_done, n)
                    go.step(nc.vector.tensor_copy(start[:, :], link_col[0:LANES, 0:1]))
                    init = start[:, 0:1]

            def from_tails(out, data):
                go.step(nc.vector.tensor_tensor(work[:, :], K.tail[:, :], data[:, :], ALU.mult))
                run_scan(scan, K.cont_b, work, K.all_b, False, ALU.mult, ALU.add, 0.0)

            dve.wait_ge(turn_used, 9)
            from_tails(scan, lane[1])
            for out, part in ((edge, 0), (own, 2)):
                go.step(nc.vector.tensor_tensor(work[:, :], lane[part][:, :], scan[:, :], ALU.add))
                go.step(nc.vector.scalar_tensor_tensor(out[:, :], work[:, :], SLOPE, work[:, :], ALU.mult, ALU.max))
            go.step(nc.vector.scalar_tensor_tensor(own[:, :], K.cont_b[:, :], -BIG, own[:, :], ALU.mult, ALU.add))
            go.step(nc.vector.tensor_tensor(run_max[:, :], edge[:, :], own[:, :], ALU.max))
            run_scan(scan, K.pen_f, run_max, K.all_pen, True, ALU.add, ALU.max, -BIG)
            from_tails(scan, scan)
            nc.vector.tensor_tensor(edge[:, :], edge[:, :], scan[:, :], ALU.subtract).then_inc(shifted, 1)
            nc.vector.tensor_tensor(own[:, :], own[:, :], scan[:, :], ALU.subtract).then_inc(shifted, 1)
            dve.wait_ge(probs, 2)
            go.step(nc.vector.tensor_tensor(run_sum[:, :], prob[:, :], own_prob[:, :], ALU.add))
            run_scan(scan, K.cont_f, run_sum, K.all_f, True, ALU.mult, ALU.add, 0.0)
            from_tails(scan, scan)
            go.step(nc.vector.tensor_scalar(scan[:, :], scan[:, :], TINY, None, ALU.add))
            go.step(nc.vector.reciprocal(work[:, :], scan[:, :]))
            go.step(nc.vector.tensor_tensor(prob[:, :], prob[:, :], work[:, :], ALU.mult))
            nc.vector.tensor_tensor(own_prob[:, :], own_prob[:, :], work[:, :], ALU.mult).then_inc(alpha_ready, 1)



def aggregate(nc, K, l):
    V = H * D
    with Stage(nc, f"aggr{l}") as st:
        sb, pair, bank, sem, sems = st.sb, st.pair, st.bank, st.sem, st.sems
        xT = pair("xT", [D, COLS])
        dst_row = pair("dst_row", [P, ET, P], i32)
        same = pair("same", [P, ET, P])
        carry = pair("carry", [P, ET, P])
        alpha = pair("alpha_c", [P, 2 * H, ET])
        index = pair("index", [P, ET], i32)
        prod = [sb(f"prod{k}", [P, 2 * H, D]) for k in range(4)]
        part = [sb(f"part{k}", [P, D]) for k in range(4)]
        out_row = pair("out_row", [P, ET, D])
        src_v = [bank("src_v0"), bank("src_v1")]
        dst_v = [bank("dst_v0"), bank("dst_v1")]
        sums = [bank("sums0"), bank("sums1")]

        loaded, row_loaded, stored, scattered = (sems(n) for n in ("loaded", "row_loaded", "stored", "scattered"))
        masks_ready, alpha_ready, src_done, dst_done, src_prod, dst_prod, part_ready, sums_done, out_evac = (
            sem(n) for n in ("masks_ready", "alpha_ready", "src_done", "dst_done", "src_prod", "dst_prod",
                             "part_ready", "sums_done", "out_evac"))
        pool_go, index_ready, blank, sp_go = (sem(n) for n in ("pool_go", "index_ready", "blank", "sp_go"))
        block = st.enter_context(nc.Block())

        @block.sync
        def _(sp):
            def store(c, b):
                wait(sp, out_evac, c * ET + ET)
                sp.sem_inc(sp_go, 1)
                dma_rows(sp, K.out_pairs[l][c], flat(out_row[b][:, :, :]), stored[b])

            def body(c, b, i):
                wait(sp, dst_done, (c - 1) * ET)
                sp.sem_inc(sp_go, 1)
                sp.dma_start(xT[b][:, :], K.pairT[l][c]).then_inc(loaded[b], 16)
                wait(sp, masks_ready, (c - 1) * (ET // 2))
                sp.sem_inc(sp_go, 1)
                sp.dma_start(dst_row[b][:, :, :].rearrange("p j e -> p (j e)"),
                             bc(K.dst_rows[c].unsqueeze(0), [P, EDGES_C])).then_inc(row_loaded[b], 16)
                if not first(c):
                    store(c - 1, 1 - b)

            over_chunks(sp, body)
            store(CHUNKS - 1, 1)
            for b in range(2):
                sp.wait_ge(stored[b], 32 * CHUNKS // 2)

        def place(b, j):
            return (b * ET + j) % 4

        @block.gpsimd
        def _(pool):
            def scatter(c, b, i):
                wait(pool, scattered[b], i * (16 * ET))
                pool.sem_inc(pool_go, 1)
                pool.tensor_copy(index[b][:, :], K.tail_i[:, bass.ds(c * ET, ET)]).then_inc(index_ready, 1)
                pool.wait_ge(index_ready, c + 1)
                for j in range(ET):
                    wait(pool, out_evac, c * ET + (j + 1))
                    pool.sem_inc(pool_go, 1)
                    pool.indirect_dma_start(K.out[l][:, :], bass.IndirectOffsetOnAxis(index[b][:, j:j + 1], 0),
                                            out_row[b][:, j, :], None, bounds_check=N - 1,
                                            oob_is_err=False).then_inc(scattered[b], 16)

            def body(c, b, i):
                if not first(c):
                    scatter(c - 1, 1 - b, i if b else i - 1)

            over_chunks(pool, body)
            scatter(CHUNKS - 1, 1, CHUNKS // 2 - 1)
            for b in range(2):
                pool.wait_ge(scattered[b], 16 * ET * CHUNKS // 2)

        @block.vector
        def _(dve):
            nc.vector.memset(out_row[1][:, ET - 1, :], 0.0).then_inc(blank, 1)

            def add_heads(c, b, j):
                q = place(b, j)
                wait(dve, src_prod, c * ET + (j + 1))
                wait(dve, dst_prod, c * ET + (j + 1))
                wait(dve, sums_done, c * ET + (j - 3))
                nc.vector.tensor_reduce(part[q][:, :], prod[q][:, :, :].rearrange("p k f -> p f k"),
                                        AX.X, ALU.add).then_inc(part_ready, 1)

            def masks(c, b, j):
                rows, at = dst_row[b][:, j:j + 2, :], bass.ds(c * ET + j, 2)
                nc.vector.tensor_tensor(same[b][:, j:j + 2, :], rows,
                                        bc(K.dst_f[:, at].unsqueeze(2), [P, 2, P]), ALU.is_equal)
                nc.vector.tensor_tensor(carry[b][:, j:j + 2, :], rows,
                                        bc(K.prev_last[:, at].unsqueeze(2), [P, 2, P]), ALU.is_equal).then_inc(masks_ready, 1)

            def body(c, b, i):
                wait(dve, src_prod, (c - 1) * ET)
                wait(dve, dst_prod, (c - 1) * ET)
                nc.vector.tensor_copy(alpha[b][:, :, :], K.alpha_flat[:, :, bass.ds(c * ET, ET)]).then_inc(alpha_ready, 1)
                wait(dve, alpha_ready, c + 1)
                for j in range(ET):
                    s, q = j % 2, place(b, j)
                    wait(dve, src_done, c * ET + (j + 1))
                    wait(dve, part_ready, c * ET + (j - 3))
                    nc.vector.tensor_tensor(prod[q][:, 0:H, :], src_v[s][0:P, 0:V].rearrange("p (h f) -> p h f", h=H),
                                            bc(alpha[b][:, 0:H, j].unsqueeze(2), [P, H, D]), ALU.mult).then_inc(src_prod, 1)
                    if j or not first(c):
                        add_heads(*earlier(c, b, j, 1))
                    if j == 0:
                        wait(dve, row_loaded[b], i * 16 + 16)
                        wait(dve, sums_done, (c - 1) * ET)
                    if j % 2 == 0:
                        masks(c, b, j)

            dve.wait_ge(blank, 1)
            over_chunks(dve, body)
            add_heads(CHUNKS - 1, 1, ET - 1)

        @block.scalar
        def _(act):
            def out(c, b, j, i):
                if j == 0:
                    wait(act, stored[b], i * 32)
                    wait(act, scattered[b], i * (16 * ET))
                wait(act, sums_done, c * ET + (j + 1))
                nc.scalar.copy(out_row[b][:, j, :], sums[j % 2][0:P, 0:D]).then_inc(out_evac, 1)

            def body(c, b, i):
                wait(act, alpha_ready, c + 1)
                for j in range(ET):
                    s, q = j % 2, place(b, j)
                    wait(act, dst_done, c * ET + (j + 1))
                    wait(act, part_ready, c * ET + (j - 3))
                    for h in range(H):
                        last = nc.scalar.activation(prod[q][:, H + h, :], dst_v[s][0:P, h * D:(h + 1) * D], ACT.Copy,
                                                    scale=alpha[b][:, H + h, j:j + 1])
                    last.then_inc(dst_prod, 1)
                    if j >= 2 or not first(c):
                        out(*earlier(c, b, j, 2), i)

            act.wait_ge(blank, 1)
            over_chunks(act, body)
            for j in (ET - 2, ET - 1):
                out(CHUNKS - 1, 1, j, None)

        @block.tensor
        def _(pe):
            def run_sums(c, b, j):
                s, q = j % 2, place(b, j)
                if j % 2 == 0:
                    wait(pe, masks_ready, c * (ET // 2) + (j // 2 + 1))
                wait(pe, part_ready, c * ET + (j + 1))
                wait(pe, out_evac, c * ET + (j - 1))
                nc.tensor.matmul(sums[s][0:P, 0:D], lhsT=same[b][:, j, :], rhs=part[q][:, :], start=True, stop=False)
                wait(pe, out_evac, c * ET + j)
                before = out_row[b][:, j - 1, :] if j else out_row[1 - b][:, ET - 1, :]
                nc.tensor.matmul(sums[s][0:P, 0:D], lhsT=carry[b][:, j, :], rhs=before,
                                 start=False, stop=True).then_inc(sums_done, 1)

            def body(c, b, i):
                wait(pe, loaded[b], i * 16 + 16)
                for j in range(ET):
                    s = j % 2
                    wait(pe, src_prod, c * ET + (j - 1))
                    nc.tensor.matmul(src_v[s][0:P, 0:V], lhsT=xT[b][:, j * P:(j + 1) * P], rhs=K.w[l][:, :],
                                     start=True, stop=True).then_inc(src_done, 1)
                    wait(pe, dst_prod, c * ET + (j - 1))
                    nc.tensor.matmul(dst_v[s][0:P, 0:V], lhsT=xT[b][:, (ET + j) * P:(ET + j + 1) * P], rhs=K.w[l][:, :],
                                     start=True, stop=True).then_inc(dst_done, 1)
                    if j >= 2 or not first(c):
                        run_sums(*earlier(c, b, j, 2))

            pe.wait_ge(blank, 1)
            over_chunks(pe, body)
            for j in (ET - 2, ET - 1):
                run_sums(CHUNKS - 1, 1, j)



def batch_norm(nc, K, l):
    nodes = K.out[l].rearrange("(c p j) f -> c p (j f)", c=CHUNKS, p=P)
    BANKS, BUFFERS = 8, 4
    with Stage(nc, f"norm{l}") as st:
        sb, bank, sem = st.sb, st.bank, st.sem
        row = [sb(f"row{k}", [P, TILES, D]) for k in range(BUFFERS)]
        stats = sb("stats", [D, CHUNKS * GROUPS, 6])
        mv = sb("mv", (D, 2))
        mean, root, rroot = (sb(n, (D, 1)) for n in ("mean", "root", "rroot"))
        turned = [bank(f"turned{k}") for k in range(BANKS)]
        loaded = [sem(f"loaded{k}") for k in range(BUFFERS)]
        t_done, t_used, steps, var_ready, root_ready, sp_go = (
            sem(n) for n in ("t_done", "t_used", "steps", "var_ready", "root_ready", "sp_go"))
        block = st.enter_context(nc.Block())

        @block.sync
        def _(sp):
            def body(c, b, i):
                wait(sp, t_done, (c - 3) * GROUPS)
                sp.sem_inc(sp_go, 1)
                dma_rows(sp, flat(row[b][:, :, :]), nodes[c], loaded[b])

            over_chunks(sp, body, BUFFERS)

        def place(b, g):
            return 4 * (b % 2) + g % 4

        @block.tensor
        def _(pe):
            def body(c, b, i):
                wait(pe, loaded[b], i * 32 + 32)
                for g in range(GROUPS):
                    wait(pe, t_used, c * GROUPS + (1 if g == 4 else g + 1 - 2 * GROUPS if g else 5 - 2 * GROUPS))
                    for k in range(TG):
                        last = nc.tensor.transpose(turned[place(b, g)][0:D, k * P:(k + 1) * P],
                                                   row[b][:, g * TG + k, :], K.eye[:, :])
                    last.then_inc(t_done, 1)

            over_chunks(pe, body, BUFFERS)

        @block.scalar
        def _(act):
            act.wait_ge(var_ready, 1)
            nc.scalar.activation(root[:, :], mv[:, 1:2], ACT.Sqrt, bias=K.eps[0:D, :]).then_inc(root_ready, 1)

        @block.vector
        def _(dve):
            def body(c, b, i):
                for g in range(GROUPS):
                    wait(dve, t_done, c * GROUPS + (g + 1))
                    nc.vector.bn_stats(stats[:, bass.ds(c * GROUPS + g, 1), :].rearrange("p a s -> p (a s)"),
                                       turned[place(b, g)][0:D, 0:TG * P]).then_inc(t_used, 1)

            over_chunks(dve, body, BUFFERS)
            dve.wait_ge(t_used, CHUNKS * GROUPS)
            nc.vector.bn_aggr(mv[:, :], stats[:, :, :].rearrange("p a s -> p (a s)")).then_inc(var_ready, 1)
            go = Line(dve, steps)
            dve.wait_ge(root_ready, 1)
            go.step(nc.vector.reciprocal(rroot[:, :], root[:, :]))
            go.step(nc.vector.tensor_tensor(K.scale[l][:, :], K.gamma[l][:, :], rroot[:, :], ALU.mult))
            go.step(nc.vector.tensor_tensor(mean[:, :], mv[:, 0:1], K.bias[l][:, :], ALU.add))
            go.step(nc.vector.tensor_tensor(mean[:, :], K.bias[l][:, :], mean[:, :], ALU.subtract))
            go.step(nc.vector.scalar_tensor_tensor(K.shift[l][:, :], mean[:, :], K.scale[l][:, :], K.beta[l][:, :],
                                                   ALU.mult, ALU.add))



def second_layer(nc, K, A):
    out0_nodes = K.out[0].rearrange("(c p j) f -> c p (j f)", c=CHUNKS, p=P)
    out1_nodes = K.out[1].rearrange("(c p j) f -> c p (j f)", c=CHUNKS, p=P)
    NODE, EDGE = 0, 1
    with Stage(nc, "second") as st:
        sb, pair, bank, sem, sems = st.sb, st.pair, st.bank, st.sem, st.sems
        row = [pair("row_node", [P, TILES, D]), pair("row_edge", [P, TILES, D])]
        resT = [pair("resT_node", [D, COLS]), pair("resT_edge", [D, COLS])]
        actT = [sb("actT_node", [D, COLS]), sb("actT_edge", [D, COLS])]
        out_row = pair("out_row", [P, TILES * D])
        index = pair("index", [P, ET], i32)
        turned = [bank(f"turned{k}") for k in range(4)]
        rows = [bank("rows0"), bank("rows1")]
        logit = [bank("logit0"), bank("logit1")]
        row_loaded = [sems("row_node_in"), sems("row_edge_in")]
        res_loaded = [sems("res_node_in"), sems("res_edge_in")]
        res_stored = [sems("res_node_out"), sems("res_edge_out")]
        gathered, rows_stored = sems("gathered"), sems("rows_stored")
        pool_go, index_ready, sp_go = sem("pool_go"), sem("index_ready"), sem("sp_go")
        t_done, t_evac, rows_done, rows_evac = (sem(n) for n in ("t_done", "t_evac", "rows_done", "rows_evac"))
        added = [sem("added_node"), sem("added_edge")]
        logit_done, logit_evac = sem("logit_done"), sem("logit_evac")
        block = st.enter_context(nc.Block())

        @block.sync
        def _(sp):
            def load(c, b, i):
                wait(sp, t_done, bank_no(c - 2, NODE, GROUPS))
                sp.sem_inc(sp_go, 1)
                dma_rows(sp, flat(row[NODE][b][:, :, :]), out0_nodes[c], row_loaded[NODE][b])
                wait(sp, res_stored[NODE][b], i * 16)
                sp.sem_inc(sp_go, 1)
                wait(sp, rows_done, c * RGROUPS - RGROUPS)
                sp.sem_inc(sp_go, 1)
                sp.dma_start(resT[NODE][b][:, :], K.h0T[c]).then_inc(res_loaded[NODE][b], 16)
                wait(sp, t_done, bank_no(c - 2, EDGE, GROUPS))
                sp.sem_inc(sp_go, 1)
                dma_rows(sp, flat(row[EDGE][b][:, ET:TILES, :]), K.out_pairs[0][c], row_loaded[EDGE][b])
                wait(sp, res_stored[EDGE][b], i * 16)
                sp.sem_inc(sp_go, 1)
                wait(sp, logit_done, c - 1)
                sp.sem_inc(sp_go, 1)
                sp.dma_start(resT[EDGE][b][:, :], K.pairT[0][c]).then_inc(res_loaded[EDGE][b], 16)

            def store(c, b):
                wait(sp, added[NODE], c + 1)
                sp.sem_inc(sp_go, 1)
                sp.dma_start(K.x1T[c], resT[NODE][b][:, :]).then_inc(res_stored[NODE][b], 16)
                wait(sp, added[EDGE], c + 1)
                sp.sem_inc(sp_go, 1)
                sp.dma_start(K.pairT[1][c], resT[EDGE][b][:, :]).then_inc(res_stored[EDGE][b], 16)
                wait(sp, rows_evac, c * RGROUPS + RGROUPS)
                sp.sem_inc(sp_go, 1)
                dma_rows(sp, out1_nodes[c], out_row[b][:, :], rows_stored[b])

            def body(c, b, i):
                load(c, b, i)
                if not first(c):
                    store(c - 1, 1 - b)

            over_chunks(sp, body)
            store(CHUNKS - 1, 1)
            for b in range(2):
                sp.wait_ge(res_stored[NODE][b], 16 * CHUNKS // 2)
                sp.wait_ge(res_stored[EDGE][b], 16 * CHUNKS // 2)
                sp.wait_ge(rows_stored[b], 32 * CHUNKS // 2)

        @block.gpsimd
        def _(pool):
            def body(c, b, i):
                wait(pool, gathered[b], i * (16 * ET))
                wait(pool, t_done, bank_no(c - 2, EDGE, GROUPS))
                pool.sem_inc(pool_go, 1)
                pool.tensor_copy(index[b][:, :], K.src_i[:, bass.ds(c * ET, ET)]).then_inc(index_ready, 1)
                pool.wait_ge(index_ready, c + 1)
                pool.sem_inc(pool_go, 1)
                for j in range(ET):
                    pool.indirect_dma_start(row[EDGE][b][:, j, :], None, K.out[0][:, :],
                                            bass.IndirectOffsetOnAxis(index[b][:, j:j + 1], 0)).then_inc(gathered[b], 16)

            over_chunks(pool, body)

        @block.tensor
        def _(pe):
            def turn(kind, c, b, i):
                wait(pe, row_loaded[kind][b], i * 32 + 32)
                if kind == EDGE:
                    wait(pe, gathered[b], i * (16 * ET) + 16 * ET)
                for g in range(GROUPS):
                    turn_group(nc, K, pe, kind, c, b, g, row[kind][b], turned, t_evac, t_done)

            def body(c, b, i):
                turn(NODE, c, b, i)
                turn(EDGE, c, b, i)
                dense_rows(nc, K, pe, 1, c, b, resT[NODE][b], rows, added[NODE], lambda g: c + 1, rows_evac, rows_done)
                edge_logits(nc, K, pe, 1, c, b, resT[EDGE][b], logit[b], added[EDGE], c + 1, logit_evac, logit_done)

            over_chunks(pe, body)

        @block.scalar
        def _(act):
            def affine_relu(kind, c, b):
                wait(act, added[kind], c)
                for g in range(GROUPS):
                    wait(act, t_done, bank_no(c, kind, g + 1))
                    nc.scalar.activation(actT[kind][:, g * TG * P:(g + 1) * TG * P],
                                         turned[turn_bank(b, kind, g)][0:D, 0:TG * P], ACT.Relu,
                                         bias=K.shift[0][:, :], scale=K.scale[0][:, :]).then_inc(t_evac, 1)

            def body(c, b, i):
                affine_relu(NODE, c, b)
                affine_relu(EDGE, c, b)
                wait(act, rows_stored[b], i * 32)
                for k in range(RGROUPS):
                    wait(act, rows_done, c * RGROUPS + (k + 1))
                    nc.scalar.copy(out_row[b][:, k * RG * D:(k + 1) * RG * D], rows[k % 2][0:P, 0:RG * D]).then_inc(rows_evac, 1)
                wait(act, logit_done, c + 1)
                nc.scalar.copy(K.logits[:, :, bass.ds(c * ET, ET)],
                               logit[b][0:P, 0:3 * H * ET].rearrange("p (k j) -> p k j", j=ET)).then_inc(logit_evac, 1)

            over_chunks(act, body)

        @block.vector
        def _(dve):
            def body(c, b, i):
                for kind in (NODE, EDGE):
                    wait(dve, res_loaded[kind][b], i * 16 + 16)
                    wait(dve, t_evac, bank_no(c, kind, GROUPS))
                    nc.vector.tensor_tensor(resT[kind][b][:, :], resT[kind][b][:, :], actT[kind][:, :],
                                            ALU.add).then_inc(added[kind], 1)

            over_chunks(dve, body)



def last_bank(c, g):
    return c * GROUPS + (0, 2 - GROUPS, 3 - GROUPS, 4 - GROUPS, 1)[g]


def third_nodes(nc, K, A):
    x_nodes = A["x"].rearrange("(c p j) f -> c p (j f)", c=CHUNKS, p=P)
    out1_nodes = K.out[1].rearrange("(c p j) f -> c p (j f)", c=CHUNKS, p=P)
    y_nodes = K.y.rearrange("(c p j) f -> c p (j f)", c=CHUNKS, p=P)
    with Stage(nc, "nodes") as st:
        sb, pair, bank, sem, sems = st.sb, st.pair, st.bank, st.sem, st.sems
        row, xrow = pair("row", [P, TILES, D]), pair("xrow", [P, TILES, D])
        resT = pair("resT", [D, COLS])
        actT = sb("actT", [D, COLS])
        ysum, norm, final = (pair(n, [P, TILES, D]) for n in ("ysum", "norm", "final"))
        DVE_GROUPS = 3
        ln = Layernorm(nc, st, "ln", DVE_GROUPS)
        src_row = pair("src_row", [P, ET, D])
        index = pair("index", [P, ET], i32)
        turned = [bank(f"turned{k}") for k in range(4)]
        yp = [bank(f"yp{k}") for k in range(4)]
        row_in, res_in, x_in, y_out, gathered, src_out = (
            sems(n) for n in ("row_in", "res_in", "x_in", "y_out", "gathered", "src_out"))
        t_done, t_evac, added, y_done, y_evac, relu_done, final_half, final_ready, pool_go, index_ready, x_added, sp_go = (
            sem(n) for n in ("t_done", "t_evac", "added", "y_done", "y_evac", "relu_done", "final_half", "final_ready",
                             "pool_go", "index_ready", "x_added", "sp_go"))
        block = st.enter_context(nc.Block())

        @block.sync
        def _(sp):
            def store(c, b):
                wait(sp, final_ready, c + 1)
                sp.sem_inc(sp_go, 1)
                dma_rows(sp, y_nodes[c], flat(final[b][:, :, :]), y_out[b])

            def store_src(c, b, i):
                wait(sp, gathered[b], i * (16 * ET) + 16 * ET)
                sp.sem_inc(sp_go, 1)
                dma_rows(sp, K.src_rows[c], flat(src_row[b][:, :, :]), src_out[b])

            def body(c, b, i):
                wait(sp, t_done, (c - 1) * GROUPS)
                sp.sem_inc(sp_go, 1)
                dma_rows(sp, flat(row[b][:, :, :]), out1_nodes[c], row_in[b])
                wait(sp, y_done, (c - 1) * RGROUPS)
                sp.sem_inc(sp_go, 1)
                sp.dma_start(resT[b][:, :], K.x1T[c]).then_inc(res_in[b], 16)
                wait(sp, x_added, c - 1)
                sp.sem_inc(sp_go, 1)
                dma_rows(sp, flat(xrow[b][:, :, :]), x_nodes[c], x_in[b])
                if not first(c):
                    store_src(c - 1, 1 - b, i if b else i - 1)
                if not first(c, 2):
                    store(c - 3, 1 - b)

            over_chunks(sp, body)
            store_src(CHUNKS - 1, 1, CHUNKS // 2 - 1)
            for c in (CHUNKS - 3, CHUNKS - 2, CHUNKS - 1):
                store(c, c % 2)
            for b in range(2):
                sp.wait_ge(y_out[b], 32 * CHUNKS // 2)
                sp.wait_ge(src_out[b], 32 * CHUNKS // 2)

        @block.gpsimd
        def _(pool):
            def add_x(c, b, i):
                wait(pool, x_in[b], i * 32 + 32)
                wait(pool, y_evac, c * RGROUPS + RGROUPS)
                pool.sem_inc(pool_go, 1)
                pool.tensor_tensor(ysum[b][:, :, :], ysum[b][:, :, :], xrow[b][:, :, :], ALU.add).then_inc(x_added, 1)

            def body(c, b, i):
                wait(pool, src_out[b], i * 32)
                pool.sem_inc(pool_go, 1)
                pool.tensor_copy(index[b][:, :], K.src_i[:, bass.ds(c * ET, ET)]).then_inc(index_ready, 1)
                pool.wait_ge(index_ready, c + 1)
                pool.sem_inc(pool_go, 1)
                for j in range(ET):
                    pool.indirect_dma_start(src_row[b][:, j, :], None, K.out[1][:, :],
                                            bass.IndirectOffsetOnAxis(index[b][:, j:j + 1], 0)).then_inc(gathered[b], 16)
                if not first(c):
                    add_x(c - 1, 1 - b, i if b else i - 1)

            over_chunks(pool, body)
            add_x(CHUNKS - 1, 1, CHUNKS // 2 - 1)

        @block.tensor
        def _(pe):
            def turn_back(c, b):
                wait(pe, added, c + 1)
                for k in range(RGROUPS):
                    wait(pe, y_evac, c * RGROUPS + (k + 1 - RGROUPS))
                    for r in range(RG):
                        j = k * RG + r
                        last = nc.tensor.matmul(yp[k][0:P, r * D:(r + 1) * D], lhsT=resT[b][:, j * P:(j + 1) * P],
                                                rhs=K.eye[0:D, 0:D], start=True, stop=True)
                    last.then_inc(y_done, 1)

            def body(c, b, i):
                wait(pe, row_in[b], i * 32 + 32)
                for g in range(GROUPS):
                    wait(pe, t_evac, last_bank(c, g))
                    for k in range(TG):
                        last = nc.tensor.transpose(turned[g % 4][0:D, k * P:(k + 1) * P], row[b][:, g * TG + k, :], K.eye[:, :])
                    last.then_inc(t_done, 1)
                if not first(c):
                    turn_back(c - 1, 1 - b)

            over_chunks(pe, body)
            turn_back(CHUNKS - 1, 1)

        @block.scalar
        def _(act):
            def relu(c, b):
                wait(act, ln.ready, c + 1)
                for j in range(DVE_GROUPS * TG, TILES):
                    last = nc.scalar.activation(norm[b][:, j, :], ysum[b][:, j, :], ACT.Relu, bias=ln.shift[:, j:j + 1],
                                                scale=ln.factor[:, j:j + 1])
                last.then_inc(relu_done, 1)
                for g in range(DVE_GROUPS):
                    wait(act, ln.normed, c * DVE_GROUPS + (g + 1))
                    rows = flat(norm[b][:, g * TG:(g + 1) * TG, :])
                    nc.scalar.activation(rows, rows, ACT.Relu).then_inc(relu_done, 1)

            def copy_out(c, b, banks):
                wait(act, final_ready, c - 1)
                for k in banks:
                    wait(act, y_done, c * RGROUPS + (k + 1))
                    nc.scalar.copy(flat(ysum[b][:, k * RG:(k + 1) * RG, :]), yp[k][0:P, 0:RG * D]).then_inc(y_evac, 1)

            def body(c, b, i):
                wait(act, added, c)
                for g in range(GROUPS):
                    wait(act, t_done, c * GROUPS + (g + 1))
                    nc.scalar.activation(actT[:, g * TG * P:(g + 1) * TG * P], turned[g % 4][0:D, 0:TG * P], ACT.Relu,
                                         bias=K.shift[1][:, :], scale=K.scale[1][:, :]).then_inc(t_evac, 1)
                if not first(c):
                    copy_out(c - 1, 1 - b, range(RGROUPS - 1))
                if not first(c, 1):
                    ln.root(act, K, c - 2)
                if not first(c):
                    copy_out(c - 1, 1 - b, (RGROUPS - 1,))
                if not first(c, 1):
                    relu(c - 2, b)

            over_chunks(act, body)
            ln.root(act, K, CHUNKS - 2)
            copy_out(CHUNKS - 1, 1, range(RGROUPS))
            relu(CHUNKS - 2, 0)
            ln.root(act, K, CHUNKS - 1)
            relu(CHUNKS - 1, 1)

        @block.vector
        def _(dve):
            def finish(c, b, i):
                wait(dve, relu_done, (c + 1) * (DVE_GROUPS + 1))
                wait(dve, y_out[b], i * 32)
                nc.vector.scalar_tensor_tensor(final[b][:, :, :], norm[b][:, :, :], K.eps1[:, :],
                                               ysum[b][:, :, :], ALU.mult, ALU.add).then_inc(final_half, 1)
                wait(dve, final_half, c + 1)
                nc.vector.tensor_tensor(final[b][:, :, :], final[b][:, :, :],
                                        bc(K.mlp_empty[:, :].unsqueeze(1), [P, TILES, D]), ALU.add).then_inc(final_ready, 1)

            def layernorm(c, b):
                wait(dve, x_added, c + 1)
                ln.statistics(dve, ysum[b], c)
                ln.factors(dve, c)
                ln.apply(dve, ysum[b], norm[b], c)

            def body(c, b, i):
                if not first(c, 2):
                    finish(c - 3, 1 - b, i - 1 if b else i - 2)
                wait(dve, res_in[b], i * 16 + 16)
                wait(dve, t_evac, c * GROUPS + GROUPS)
                nc.vector.tensor_tensor(resT[b][:, :], resT[b][:, :], actT[:, :], ALU.add).then_inc(added, 1)
                if not first(c, 1):
                    layernorm(c - 2, b)

            over_chunks(dve, body)
            finish(CHUNKS - 3, 1, CHUNKS // 2 - 2)
            layernorm(CHUNKS - 2, 0)
            finish(CHUNKS - 2, 0, CHUNKS // 2 - 1)
            layernorm(CHUNKS - 1, 1)
            finish(CHUNKS - 1, 1, CHUNKS // 2 - 1)



def third_edges(nc, K, A):
    attr = K.attr.rearrange("(c j p) f -> c p j f", c=CHUNKS, p=P)
    HG = (TG, TG, ET - 2 * TG)
    with Stage(nc, "edges") as st:
        sb, pair, bank, sem, sems = st.sb, st.pair, st.bank, st.sem, st.sems
        row, xrow = pair("row", [P, TILES, D]), pair("xrow", [P, TILES, D])
        resT = pair("resT", [D, COLS])
        actT = sb("actT", [D, COLS])
        ysum, norm = pair("ysum", [P, TILES, D]), pair("norm", [P, TILES, D])
        ln = Layernorm(nc, st, "ln")
        msg = pair("msg", [P, ET, D])
        dst_row = sb("dst_row", [P, ET, P], i32)
        same = pair("same", [P, ET, P])
        go_on = pair("go_on", [D, ET, P])
        aggr = pair("aggr", [D, EDGES_C])
        hidden = sb("hidden", [D, 2, EDGES_C])
        base_row = pair("base_row", [P, ET, D])
        final = pair("final", [P, ET, D])
        index = pair("index", [P, ET], i32)
        turned = [bank("turned0"), bank("turned1")]
        ap = [bank(f"ap{q}") for q in range(len(HG))]
        hp = [bank("hp0"), bank("hp1")]
        mp = [bank("mp0"), hp[1]]
        row_in, res_in, x_in, ea_in, scattered = (sems(n) for n in ("row_in", "res_in", "x_in", "ea_in", "scattered"))
        dr_in, same_ready, go_on_ready = sem("dr_in"), sem("same_ready"), sem("go_on_ready")
        t_done, t_evac, added, y_done, y_sum, msg_ready, ap_done, aggr_ready = (
            sem(n) for n in ("t_done", "t_evac", "added", "y_done", "y_sum", "msg_ready", "ap_done", "aggr_ready"))
        hp_done, hid_ready, mp_done, final_ready, blank, base_half, base_ready, pool_go, index_ready, sp_go = (
            sem(n) for n in ("hp_done", "hid_ready", "mp_done", "final_ready", "blank", "base_half", "base_ready",
                             "pool_go", "index_ready", "sp_go"))
        LAST = CHUNKS // 2 - 1
        SRC_GROUPS = -(-ET // TG)
        block = st.enter_context(nc.Block())

        @block.sync
        def _(sp):
            def load(c, b):
                wait(sp, t_done, (c - 1) * GROUPS)
                sp.sem_inc(sp_go, 1)
                dma_rows(sp, flat(row[b][:, 0:ET, :]), K.src_rows[c], row_in[b])
                dma_rows(sp, flat(row[b][:, ET:TILES, :]), K.out_pairs[1][c], row_in[b])
                wait(sp, y_done, (c - 1) * RGROUPS)
                sp.sem_inc(sp_go, 1)
                sp.dma_start(resT[b][:, :], K.pairT[1][c]).then_inc(res_in[b], 16)
                wait(sp, y_sum, (c - 1) * RGROUPS)
                sp.sem_inc(sp_go, 1)
                dma_rows(sp, flat(xrow[b][:, :, :]), K.raw_pairs[c], x_in[b])

            def load_edges(c, b):
                wait(sp, go_on_ready, c)
                sp.sem_inc(sp_go, 1)
                sp.dma_start(dst_row[:, :, :].rearrange("p j e -> p (j e)"),
                             bc(K.dst_rows[c].unsqueeze(0), [P, EDGES_C])).then_inc(dr_in, 16)
                wait(sp, ap_done, (c - 1) * len(HG))
                sp.sem_inc(sp_go, 1)
                dma_rows(sp, msg[b][:, :, :], attr[c], ea_in[b])

            def body(c, b, i):
                load(c, b)
                if not first(c):
                    load_edges(c - 1, 1 - b)

            over_chunks(sp, body)
            load_edges(CHUNKS - 1, 1)

        @block.gpsimd
        def _(pool):
            def messages(c, b, i):
                wait(pool, ea_in[b], i * 32 + 32)
                wait(pool, ln.normed, c * GROUPS + SRC_GROUPS)
                pool.sem_inc(pool_go, 1)
                pool.tensor_tensor(flat(msg[b][:, :, :]), flat(norm[b][:, 0:ET, :]), flat(msg[b][:, :, :]),
                                   ALU.add).then_inc(msg_ready, 1)

            def add_b2(c, b):
                wait(pool, y_sum, c * RGROUPS + RGROUPS)
                wait(pool, final_ready, (c - 1) * 2)
                pool.sem_inc(pool_go, 1)
                pool.tensor_tensor(base_row[b][:, :, :], ysum[b][:, ET:TILES, :],
                                   bc(K.b2b[:, :].unsqueeze(1), [P, ET, D]), ALU.add).then_inc(base_half, 1)

            def scatter(c, b, i):
                wait(pool, scattered[b], i * (16 * ET))
                pool.sem_inc(pool_go, 1)
                pool.tensor_copy(index[b][:, :], K.tail_i[:, bass.ds(c * ET, ET)]).then_inc(index_ready, 1)
                pool.wait_ge(index_ready, c + 1)
                wait(pool, final_ready, c * 2 + 2)
                pool.sem_inc(pool_go, 1)
                for j in range(ET):
                    pool.indirect_dma_start(K.y[:, :], bass.IndirectOffsetOnAxis(index[b][:, j:j + 1], 0),
                                            final[b][:, j, :], None, bounds_check=N - 1,
                                            oob_is_err=False).then_inc(scattered[b], 16)

            def body(c, b, i):
                if not first(c):
                    messages(c - 1, 1 - b, i if b else i - 1)
                    add_b2(c - 1, 1 - b)
                if not first(c, 2):
                    scatter(c - 3, 1 - b, i - 1 if b else i - 2)

            over_chunks(pool, body)
            messages(CHUNKS - 1, 1, LAST)
            add_b2(CHUNKS - 1, 1)
            scatter(CHUNKS - 3, 1, LAST - 1)
            scatter(CHUNKS - 2, 0, LAST)
            scatter(CHUNKS - 1, 1, LAST)
            for b in range(2):
                pool.wait_ge(scattered[b], 16 * ET * CHUNKS // 2)

        @block.tensor
        def _(pe):
            def run_sums(c, b):
                wait(pe, msg_ready, c + 1)
                wait(pe, same_ready, c + 1)
                wait(pe, aggr_ready, c * ET)
                at = 0
                for q, cnt in enumerate(HG):
                    for j in range(at, at + cnt):
                        last = nc.tensor.matmul(ap[q][0:D, (j - at) * P:(j - at + 1) * P], lhsT=msg[b][:, j, :],
                                                rhs=same[b][:, j, :], start=True, stop=True)
                    last.then_inc(ap_done, 1)
                    at += cnt

            def hide(c, b):
                wait(pe, final_ready, c * 2)
                at = 0
                for q, cnt in enumerate(HG):
                    wait(pe, aggr_ready, c * ET + (at + cnt))
                    for half in range(2):
                        wait(pe, hid_ready, c * 6 + (2 * q + half - 1))
                        nc.tensor.matmul(hp[half][0:D, 0:cnt * P], lhsT=K.w1[:, half * D:(half + 1) * D],
                                         rhs=aggr[b][:, at * P:(at + cnt) * P], start=True, stop=True).then_inc(hp_done, 1)
                    at += cnt

            def mlp(c):
                wait(pe, hid_ready, c * 6 + 6)
                for k in range(2):
                    if k == 0:
                        wait(pe, final_ready, c * 2 - 1)
                    for r in range(RG):
                        j = k * RG + r
                        for half in range(2):
                            last = nc.tensor.matmul(mp[k][0:P, r * D:(r + 1) * D], lhsT=hidden[:, half, j * P:(j + 1) * P],
                                                    rhs=K.w2[:, half, :], start=(half == 0), stop=(half == 1))
                    last.then_inc(mp_done, 1)

            def turn(c, b, i):
                wait(pe, row_in[b], i * 64 + 64)
                for g in range(GROUPS):
                    if g < 2:
                        wait(pe, y_sum, c * RGROUPS + (g - 1))
                    else:
                        wait(pe, t_evac, c * GROUPS + (g - 1))
                    for k in range(TG):
                        last = nc.tensor.transpose(turned[g % 2][0:D, k * P:(k + 1) * P],
                                                   row[b][:, g * TG + k, :], K.eye[:, :])
                    last.then_inc(t_done, 1)

            def turn_back(c, b):
                wait(pe, added, c + 1)
                for k in range(RGROUPS):
                    if k >= 2:
                        wait(pe, y_sum, c * RGROUPS + (k - 1))
                    for r in range(RG):
                        j = k * RG + r
                        last = nc.tensor.matmul(turned[k % 2][0:P, r * D:(r + 1) * D], lhsT=resT[b][:, j * P:(j + 1) * P],
                                                rhs=K.eye[0:D, 0:D], start=True, stop=True)
                    last.then_inc(y_done, 1)

            def body(c, b, i):
                if not first(c, 1):
                    run_sums(c - 2, b)
                turn(c, b, i)
                if not first(c, 2):
                    mlp(c - 3)
                turn_back(c, b)
                if not first(c, 1):
                    hide(c - 2, b)

            over_chunks(pe, body)
            for c in (CHUNKS - 2, CHUNKS - 1):
                run_sums(c, c % 2)
                mlp(c - 1)
                hide(c, c % 2)
            mlp(CHUNKS - 1)

        @block.scalar
        def _(act):
            def hide(c, b):
                wait(act, mp_done, c * 2)
                at = 0
                for q, cnt in enumerate(HG):
                    for half in range(2):
                        wait(act, hp_done, c * 6 + (2 * q + half + 1))
                        nc.scalar.activation(hidden[:, half, at * P:(at + cnt) * P], hp[half][0:D, 0:cnt * P], ACT.Relu,
                                             bias=K.b1[:, half:half + 1]).then_inc(hid_ready, 1)
                    at += cnt

            def apply(c, b):
                wait(act, base_ready, c - 1)
                wait(act, msg_ready, c - 1)
                ln.apply_relu(act, ysum[b], norm[b], c)

            def body(c, b, i):
                wait(act, added, c)
                for g in range(GROUPS):
                    wait(act, t_done, c * GROUPS + (g + 1))
                    nc.scalar.activation(actT[:, g * TG * P:(g + 1) * TG * P], turned[g % 2][0:D, 0:TG * P],
                                         ACT.Relu, bias=K.shift[1][:, :], scale=K.scale[1][:, :]).then_inc(t_evac, 1)
                if not first(c):
                    apply(c - 1, 1 - b)
                if not first(c, 1):
                    hide(c - 2, b)
                ln.root(act, K, c)

            over_chunks(act, body)
            apply(CHUNKS - 1, 1)
            hide(CHUNKS - 2, 0)
            hide(CHUNKS - 1, 1)

        @block.vector
        def _(dve):
            def mask_same(c, b):
                wait(dve, dr_in, c * 16 + 16)
                wait(dve, aggr_ready, (c - 1) * ET)
                nc.vector.tensor_tensor(same[b][:, :, :], dst_row[:, :, :],
                                        bc(K.dst_f[:, bass.ds(c * ET, ET)].unsqueeze(2), [P, ET, P]),
                                        ALU.is_equal).then_inc(same_ready, 1)

            def mask_go_on(c, b):
                nc.vector.tensor_tensor(go_on[b][:, :, :], dst_row[0:D, :, :],
                                        bc(K.prev_b[:, bass.ds(c * ET, ET)].unsqueeze(2), [D, ET, P]),
                                        ALU.is_equal).then_inc(go_on_ready, 1)

            def sums(c, b):
                wait(dve, go_on_ready, c + 1)
                wait(dve, hp_done, c * 6 - 6)
                for j in range(ET):
                    if j % TG == 0:
                        wait(dve, ap_done, c * len(HG) + (j // TG + 1))
                    wait(dve, aggr_ready, c * ET + j)
                    before = aggr[b][:, j * P - 1:j * P] if j else aggr[1 - b][:, EDGES_C - 1:EDGES_C]
                    nc.vector.scalar_tensor_tensor(aggr[b][:, j * P:(j + 1) * P], go_on[b][:, j, :], before,
                                                   ap[j // TG][0:D, (j % TG) * P:(j % TG + 1) * P], ALU.mult,
                                                   ALU.add).then_inc(aggr_ready, 1)

            def base(c, b):
                wait(dve, ln.normed, c * GROUPS + GROUPS)
                wait(dve, base_half, c + 1)
                nc.vector.scalar_tensor_tensor(base_row[b][:, :, :], norm[b][:, ET:TILES, :], K.eps1[:, :],
                                               base_row[b][:, :, :], ALU.mult, ALU.add).then_inc(base_ready, 1)

            def finish(c, b, i):
                wait(dve, scattered[b], i * (16 * ET))
                wait(dve, base_ready, c + 1)
                for k in range(2):
                    wait(dve, mp_done, c * 2 + (k + 1))
                    nc.vector.tensor_tensor(flat(final[b][:, k * RG:(k + 1) * RG, :]), mp[k][0:P, 0:RG * D],
                                            flat(base_row[b][:, k * RG:(k + 1) * RG, :]), ALU.add).then_inc(final_ready, 1)

            def body(c, b, i):
                if not first(c, 1):
                    sums(c - 2, b)
                if not first(c):
                    mask_same(c - 1, 1 - b)
                wait(dve, res_in[b], i * 16 + 16)
                wait(dve, t_evac, c * GROUPS + GROUPS)
                nc.vector.tensor_tensor(resT[b][:, :], resT[b][:, :], actT[:, :], ALU.add).then_inc(added, 1)
                if not first(c, 2):
                    finish(c - 3, 1 - b, i - 1 if b else i - 2)
                if not first(c):
                    mask_go_on(c - 1, 1 - b)
                wait(dve, x_in[b], i * 32 + 32)
                wait(dve, base_ready, c - 1)
                for k in range(RGROUPS):
                    wait(dve, y_done, c * RGROUPS + (k + 1))
                    nc.vector.tensor_tensor(flat(ysum[b][:, k * RG:(k + 1) * RG, :]), turned[k % 2][0:P, 0:RG * D],
                                            flat(xrow[b][:, k * RG:(k + 1) * RG, :]), ALU.add).then_inc(y_sum, 1)
                wait(dve, y_sum, c * RGROUPS + RGROUPS)
                ln.statistics(dve, ysum[b], c)
                if not first(c):
                    base(c - 1, 1 - b)
                ln.factors(dve, c)

            nc.vector.memset(aggr[1][:, EDGES_C - 1:EDGES_C], 0.0).then_inc(blank, 1)
            dve.wait_ge(blank, 1)
            over_chunks(dve, body)
            sums(CHUNKS - 2, 0)
            mask_same(CHUNKS - 1, 1)
            mask_go_on(CHUNKS - 1, 1)
            finish(CHUNKS - 3, 1, LAST - 1)
            base(CHUNKS - 1, 1)
            sums(CHUNKS - 1, 1)
            finish(CHUNKS - 2, 0, LAST)
            finish(CHUNKS - 1, 1, LAST)


def build(nc, A, y):
    K = Core()
    K.y = y
    K.src, K.dst, K.attr = A["src"], A["dst"], A["edge_attr_96"]
    K.dst_rows = K.dst.rearrange("(c e) -> c e", c=CHUNKS)

    def dram(name, shape):
        return nc.dram_tensor(name, shape, fp32, kind="Internal").ap()

    K.out = [dram(f"out_rows{l}", [N, D]) for l in range(LAYERS)]
    K.h0T, K.x1T = dram("h0T", [CHUNKS, D, COLS]), dram("x1T", [CHUNKS, D, COLS])
    K.pairT = [dram(f"pairT{l}", [CHUNKS, D, COLS]) for l in range(LAYERS)]
    K.raw_pairs = dram("raw_pairs", [CHUNKS, P, TILES * D])
    K.out_pairs = [dram(f"out_pairs{l}", [CHUNKS, P, ET * D]) for l in range(LAYERS)]
    K.src_rows = dram("src_rows", [CHUNKS, P, ET * D])
    with Stage(nc, "all") as st:
        sb = st.sb
        K.eye, K.eps = sb("eye", (P, P)), sb("eps", (P, 1))
        K.w = [sb(f"w_heads{l}", (D, HD)) for l in range(LAYERS)]
        K.w_bar = [sb(f"w_bar{l}", (D, D)) for l in range(LAYERS)]
        K.w_att = [sb(f"w_att{l}", (D, 3 * H)) for l in range(LAYERS)]
        K.bias, K.gamma, K.beta, K.scale, K.shift = (
            [sb(f"{n}{l}", (D, 1)) for l in range(LAYERS)] for n in ("bias", "gamma", "beta", "scale", "shift"))
        K.w1, K.w2, K.b1 = sb("w1", (D, 2 * D)), sb("w2", (D, 2, D)), sb("b1", (D, 2))
        K.mlp_empty, K.b2b, K.eps1 = sb("mlp_empty", (P, D)), sb("b2b", (P, D)), sb("eps1", (P, 1))
        K.src_i, K.dst_i, K.tail_i = (sb(n, (P, EDGE_TILES), i32) for n in ("src_i", "dst_i", "tail_i"))
        K.dst_f, K.prev_last = (sb(n, (P, EDGE_TILES)) for n in ("dst_f", "prev_last"))
        K.prev_b = sb("prev_b", (D, EDGE_TILES))
        with Stage(nc, "gat") as gat:
            K.cont_f, K.cont_b, K.tail, K.pen_f = (gat.sb(n, (LANES, EDGES_C)) for n in ("cont_f", "cont_b", "tail", "pen_f"))
            K.all_f, K.all_b, K.all_pen = (gat.sb(n, (1, LANES)) for n in ("all_f", "all_b", "all_pen"))
            K.logits = gat.sb("logits", (P, 3 * H, EDGE_TILES))
            K.alpha = gat.sb("alpha", (P, 2, LANES, ET))
            K.alpha_flat = K.alpha[:, :, :, :].rearrange("p k (h b) j -> p (k h) (b j)", h=H)
            prepare(nc, K, A)
            first_layer(nc, K, A)
            edge_softmax(nc, K, 0)
            aggregate(nc, K, 0)
            batch_norm(nc, K, 0)
            second_layer(nc, K, A)
            edge_softmax(nc, K, 1)
            aggregate(nc, K, 1)
        batch_norm(nc, K, 1)
        third_nodes(nc, K, A)
        third_edges(nc, K, A)


_INS = ["x", "src", "dst", "edge_attr_96", "L0_gnn_W", "L0_gnn_att_src", "L0_gnn_att_dst", "L0_gnn_bias",
        "L0_gnn_gamma", "L0_gnn_beta", "L1_gnn_W1", "L1_gnn_b1", "L1_gnn_W2", "L1_gnn_b2", "L1_gnn_eps"]


def kernel(**inputs):
    import numpy as np
    import concourse.bacc as bacc
    from concourse.bass_utils import run_bass_kernel_spmd

    nc = bacc.Bacc("TRN2", target_bir_lowering=False, num_devices=1)
    arrays, A = {}, {}
    for name in _INS:
        a = np.ascontiguousarray(inputs[name])
        arrays[f"in_{name}"] = a
        A[name] = nc.dram_tensor(f"in_{name}", a.shape, mybir.dt.from_np(a.dtype), kind="ExternalInput").ap()
    y = nc.dram_tensor("out_0", (N, D), fp32, kind="ExternalOutput").ap()
    build(nc, A, y)
    r = run_bass_kernel_spmd(nc, [arrays], core_ids=[0])
    return r.results[0]["out_0"]
```
